# Optimizing a Trainium2 kernel written in Bass

```python
import numpy as np
import jax
import jax.numpy as jnp

def _softmax(x, axis=-1):
    return jax.nn.softmax(x, axis=axis)

def _gelu(x):
    return jax.nn.gelu(x, approximate=True)

def _silu(x):
    return jax.nn.silu(x)

def _sigmoid(x):
    return jax.nn.sigmoid(x)

def _layernorm(x, axis=-1, eps=1e-05):
    m = jnp.mean(x, axis=axis, keepdims=True)
    v = jnp.var(x, axis=axis, keepdims=True)
    return (x - m) / jnp.sqrt(v + eps)

def _scatter_add(tgt, idx, src, axis=0):
    return tgt.at[idx].add(src)

def _segment_sum(src, seg, n):
    return jax.ops.segment_sum(src, seg, n)
kernel_name = 'mk_seq_postln_d2_jaxref_r8_4bf7a7'

def setup_inputs(seed: int=0):
    np.random.seed(seed)
    _w = jnp.asarray

    def _L0_attn_setup():
        import jax, jax.numpy as jnp
        import numpy as np
        N_HEADS = 16
        HEAD_DIM = 64
        ROPE_THETA = 10000.0

        def _rope_cos_sin(seq_len, dim, theta):
            inv_freq = 1.0 / theta ** (jnp.arange(0, dim, 2, dtype=jnp.float32) / dim)
            pos = jnp.arange(seq_len, dtype=jnp.float32)
            freqs = pos[:, None] * inv_freq[None, :]
            emb = jnp.concatenate([freqs, freqs], axis=-1)
            return (jnp.cos(emb), jnp.sin(emb))

        def _rotate_half(x):
            d = x.shape[-1] // 2
            return jnp.concatenate([-x[..., d:], x[..., :d]], axis=-1)
        key = jax.random.key(seed)
        ks = jax.random.split(key, 6)
        B, S, D_MODEL, LATENT = (1, 512, 128, 64)
        q_dim = N_HEADS * HEAD_DIM
        sd = lambda fan_in: 1.0 / np.sqrt(fan_in)
        return {'x': jax.random.normal(ks[0], (B, S, D_MODEL), jnp.float32), 'wq': jax.random.normal(ks[1], (q_dim, D_MODEL), jnp.float32) * sd(D_MODEL), 'w_kv_down': jax.random.normal(ks[2], (LATENT, D_MODEL), jnp.float32) * sd(D_MODEL), 'w_k_up': jax.random.normal(ks[3], (q_dim, LATENT), jnp.float32) * sd(LATENT), 'w_v_up': jax.random.normal(ks[4], (q_dim, LATENT), jnp.float32) * sd(LATENT), 'wo': jax.random.normal(ks[5], (D_MODEL, q_dim), jnp.float32) * sd(q_dim)}
    _L0_attn_in = _L0_attn_setup()

    def _L0_ffn_setup():
        import jax, jax.numpy as jnp
        import numpy as np
        B, L, D = (4, 64, 128)
        E, TOP_K = (16, 4)
        F = 4 * D
        key = jax.random.key(seed)
        ks = jax.random.split(key, 6)
        scale = 0.02
        return {'x': jax.random.normal(ks[0], (B, L, D), jnp.float32), 'keys': jax.random.normal(ks[1], (E, D), jnp.float32), 'w1': jax.random.normal(ks[2], (E, F, D), jnp.float32) * scale, 'b1': jnp.zeros((E, F), jnp.float32), 'w2': jax.random.normal(ks[3], (E, D, F), jnp.float32) * scale, 'b2': jnp.zeros((E, D), jnp.float32), 'rw': jax.random.normal(ks[4], (E, D), jnp.float32) * scale, 'rb': jnp.zeros((E,), jnp.float32)}
    _L0_ffn_in = _L0_ffn_setup()

    def _L1_attn_setup():
        import jax, jax.numpy as jnp
        import numpy as np
        D_MODEL = 128
        N_HEADS = 16
        HEAD_DIM = D_MODEL // N_HEADS

        def _rope(x):
            B = x.shape[0]
            half = HEAD_DIM // 2
            theta = 1.0 / 10000.0 ** (jnp.arange(0, HEAD_DIM, 2, dtype=jnp.float32) / HEAD_DIM)
            pos = jnp.arange(B, dtype=jnp.float32)
            ang = pos[:, None] * theta[None, :]
            ang2 = jnp.concatenate([ang, ang], axis=-1)
            cos = jnp.cos(ang2)[:, None, None, :]
            sin = jnp.sin(ang2)[:, None, None, :]
            neg_half = jnp.concatenate([x[..., :half], -x[..., half:]], axis=-1)
            return x * cos + neg_half * sin
        key = jax.random.key(seed)
        k_x, k_q, k_k, k_v = jax.random.split(key, 4)
        B, S = (4, 256)
        scale = 1.0 / np.sqrt(D_MODEL)
        x = jax.random.normal(k_x, (B, S, D_MODEL), dtype=jnp.float32)
        Wq = jax.random.normal(k_q, (D_MODEL, D_MODEL), dtype=jnp.float32) * scale
        Wk = jax.random.normal(k_k, (D_MODEL, D_MODEL), dtype=jnp.float32) * scale
        Wv = jax.random.normal(k_v, (D_MODEL, D_MODEL), dtype=jnp.float32) * scale
        return {'x': x, 'Wq': Wq, 'Wk': Wk, 'Wv': Wv}
    _L1_attn_in = _L1_attn_setup()

    def _L1_ffn_setup():
        import jax, jax.numpy as jnp
        import numpy as np
        DIM = 128
        DEPTH = 2
        HEADS = 8
        DIM_HEAD = 64
        WINDOW = 64
        INNER = HEADS * DIM_HEAD
        HID = int(DIM * 4 * 2 / 3)
        B, N = (2, 1024)
        QK_SCALE = 8.0

        def shift_token(t):
            t1, t2 = jnp.split(t, 2, axis=-1)
            t2 = jnp.pad(t2, ((0, 0), (1, 0), (0, 0)))[:, :-1]
            return jnp.concatenate([t1, t2], axis=-1)

        def l2norm(t):
            return t / jnp.clip(jnp.linalg.norm(t, axis=-1, keepdims=True), 1e-12)

        def rotate_half(x):
            x1, x2 = jnp.split(x, 2, axis=-1)
            return jnp.concatenate([-x2, x1], axis=-1)

        def rotary_xpos(q, k):
            n = q.shape[-2]
            half_idx = jnp.arange(0, DIM_HEAD, 2, dtype=jnp.float32)
            inv_freq = 1.0 / 10000.0 ** (half_idx / DIM_HEAD)
            t = jnp.arange(n, dtype=jnp.float32)
            freqs = t[:, None] * inv_freq[None, :]
            freqs = jnp.concatenate([freqs, freqs], axis=-1)
            base = (half_idx + 0.4 * DIM_HEAD) / (1.4 * DIM_HEAD)
            power = (t - n // 2) / float(WINDOW // 2)
            scale = base[None, :] ** power[:, None]
            scale = jnp.concatenate([scale, scale], axis=-1)
            cos, sin = (jnp.cos(freqs), jnp.sin(freqs))
            q = q * cos * scale + rotate_half(q) * sin * scale
            k = k * cos / scale + rotate_half(k) * sin / scale
            return (q, k)

        def local_attention(q, k, v):
            b, h, n, d = q.shape
            w = n // WINDOW
            bq = q.reshape(b, h, w, WINDOW, d) * QK_SCALE
            bk = k.reshape(b, h, w, WINDOW, d)
            bv = v.reshape(b, h, w, WINDOW, d)

            def look_around(t):
                p = jnp.pad(t, ((0, 0), (0, 0), (1, 0), (0, 0), (0, 0)))
                return jnp.concatenate([p[:, :, :w], p[:, :, 1:]], axis=3)
            bk, bv = (look_around(bk), look_around(bv))
            bt = jnp.arange(n).reshape(w, WINDOW)
            btp = jnp.pad(bt, ((1, 0), (0, 0)), constant_values=-1)
            btk = jnp.concatenate([btp[:w], btp[1:]], axis=1)
            sim = jnp.einsum('bhwid,bhwjd->bhwij', bq, bk)
            i = bt[:, :, None]
            j = btk[:, None, :]
            mask = (i < j) | (i > j + WINDOW) | (j == -1)
            sim = jnp.where(mask, -jnp.finfo(sim.dtype).max, sim)
            attn = jax.nn.softmax(sim, axis=-1)
            out = jnp.einsum('bhwij,bhwjd->bhwid', attn, bv)
            return out.reshape(b, h, n, d)

        def _layer(x, wqkv, qs, ksc, wo, lg, lb, w1, b1, w2, b2):
            b, n, _ = x.shape
            h = shift_token(x)
            qkv = h @ wqkv
            q, k, v = jnp.split(qkv, 3, axis=-1)
            to_heads = lambda t: t.reshape(b, n, HEADS, DIM_HEAD).transpose(0, 2, 1, 3)
            q, k, v = (to_heads(q), to_heads(k), to_heads(v))
            q = l2norm(q) * qs
            k = l2norm(k) * ksc
            q, k = rotary_xpos(q, k)
            o = local_attention(q, k, v)
            o = o.transpose(0, 2, 1, 3).reshape(b, n, INNER)
            x = x + o @ wo
            h = shift_token(x)
            mu = h.mean(-1, keepdims=True)
            var = h.var(-1, keepdims=True)
            h = (h - mu) / jnp.sqrt(var + 1e-05) * lg + lb
            h = h @ w1 + b1
            a, g = jnp.split(h, 2, axis=-1)
            h = a * jax.nn.gelu(g, approximate=False)
            x = x + h @ w2 + b2
            return x
        key = jax.random.key(seed)
        ks = jax.random.split(key, 6)
        return {'x': jax.random.normal(ks[0], (B, N, DIM), jnp.float32), 'wqkv': jax.random.normal(ks[1], (DEPTH, DIM, 3 * INNER), jnp.float32) * 0.02, 'q_scale': jnp.ones((DEPTH, DIM_HEAD), jnp.float32), 'k_scale': jnp.ones((DEPTH, DIM_HEAD), jnp.float32), 'wo': jax.random.normal(ks[2], (DEPTH, INNER, DIM), jnp.float32) * 0.02, 'ln_g': jnp.ones((DEPTH, DIM), jnp.float32), 'ln_b': jnp.zeros((DEPTH, DIM), jnp.float32), 'w1': jax.random.normal(ks[3], (DEPTH, DIM, 2 * HID), jnp.float32) * 0.02, 'b1': jnp.zeros((DEPTH, 2 * HID), jnp.float32), 'w2': jax.random.normal(ks[4], (DEPTH, HID, DIM), jnp.float32) * 0.02, 'b2': jnp.zeros((DEPTH, DIM), jnp.float32)}
    _L1_ffn_in = _L1_ffn_setup()
    _d = {'L0_attn_x': _L0_attn_in['x'], 'L0_attn_wq': _L0_attn_in['wq'], 'L0_attn_w_kv_down': _L0_attn_in['w_kv_down'], 'L0_attn_w_k_up': _L0_attn_in['w_k_up'], 'L0_attn_w_v_up': _L0_attn_in['w_v_up'], 'L0_attn_wo': _L0_attn_in['wo'], 'L0_ffn_keys': _L0_ffn_in['keys'], 'L0_ffn_w1': _L0_ffn_in['w1'], 'L0_ffn_b1': _L0_ffn_in['b1'], 'L0_ffn_w2': _L0_ffn_in['w2'], 'L0_ffn_b2': _L0_ffn_in['b2'], 'L0_ffn_rw': _L0_ffn_in['rw'], 'L0_ffn_rb': _L0_ffn_in['rb'], 'L1_attn_Wq': _L1_attn_in['Wq'], 'L1_attn_Wk': _L1_attn_in['Wk'], 'L1_attn_Wv': _L1_attn_in['Wv'], 'L1_ffn_wqkv': _L1_ffn_in['wqkv'], 'L1_ffn_q_scale': _L1_ffn_in['q_scale'], 'L1_ffn_k_scale': _L1_ffn_in['k_scale'], 'L1_ffn_wo': _L1_ffn_in['wo'], 'L1_ffn_ln_g': _L1_ffn_in['ln_g'], 'L1_ffn_ln_b': _L1_ffn_in['ln_b'], 'L1_ffn_w1': _L1_ffn_in['w1'], 'L1_ffn_b1': _L1_ffn_in['b1'], 'L1_ffn_w2': _L1_ffn_in['w2'], 'L1_ffn_b2': _L1_ffn_in['b2']}
    _x0 = _d['L0_attn_x']
    _d['L0_attn_x'] = jax.random.normal(jax.random.fold_in(jax.random.key(seed), 1), (4, 512, 128), dtype=_x0.dtype)
    del _x0
    return _d

def reference(L0_attn_x, L0_attn_wq, L0_attn_w_kv_down, L0_attn_w_k_up, L0_attn_w_v_up, L0_attn_wo, L0_ffn_keys, L0_ffn_w1, L0_ffn_b1, L0_ffn_w2, L0_ffn_b2, L0_ffn_rw, L0_ffn_rb, L1_attn_Wq, L1_attn_Wk, L1_attn_Wv, L1_ffn_wqkv, L1_ffn_q_scale, L1_ffn_k_scale, L1_ffn_wo, L1_ffn_ln_g, L1_ffn_ln_b, L1_ffn_w1, L1_ffn_b1, L1_ffn_w2, L1_ffn_b2):

    def _L0_attn_ref(x, wq, w_kv_down, w_k_up, w_v_up, wo):
        import jax, jax.numpy as jnp
        import numpy as np
        N_HEADS = 16
        HEAD_DIM = 64
        ROPE_THETA = 10000.0

        def _rope_cos_sin(seq_len, dim, theta):
            inv_freq = 1.0 / theta ** (jnp.arange(0, dim, 2, dtype=jnp.float32) / dim)
            pos = jnp.arange(seq_len, dtype=jnp.float32)
            freqs = pos[:, None] * inv_freq[None, :]
            emb = jnp.concatenate([freqs, freqs], axis=-1)
            return (jnp.cos(emb), jnp.sin(emb))

        def _rotate_half(x):
            d = x.shape[-1] // 2
            return jnp.concatenate([-x[..., d:], x[..., :d]], axis=-1)
        B, S, _ = x.shape
        H, D = (N_HEADS, HEAD_DIM)
        q = jnp.einsum('bsd,qd->bsq', x, wq).reshape(B, S, H, D).transpose(0, 2, 1, 3)
        kv_latent = jnp.einsum('bsd,ld->bsl', x, w_kv_down)
        k = jnp.einsum('bsl,ql->bsq', kv_latent, w_k_up).reshape(B, S, H, D).transpose(0, 2, 1, 3)
        v = jnp.einsum('bsl,ql->bsq', kv_latent, w_v_up).reshape(B, S, H, D).transpose(0, 2, 1, 3)
        cos, sin = _rope_cos_sin(S, D, ROPE_THETA)
        cos = cos[None, None]
        sin = sin[None, None]
        q = q * cos + _rotate_half(q) * sin
        k = k * cos + _rotate_half(k) * sin
        scores = jnp.einsum('bhsd,bhtd->bhst', q, k) / jnp.sqrt(jnp.float32(D))
        causal = jnp.triu(jnp.full((S, S), -jnp.inf, dtype=jnp.float32), k=1)
        scores = scores + causal[None, None]
        probs = jax.nn.softmax(scores.astype(jnp.float32), axis=-1).astype(q.dtype)
        out = jnp.einsum('bhst,bhtd->bhsd', probs, v)
        out = out.transpose(0, 2, 1, 3).reshape(B, S, H * D)
        return jnp.einsum('bsq,dq->bsd', out, wo)

    def _L0_ffn_ref(x, keys, w1, b1, w2, b2, rw, rb):
        import jax, jax.numpy as jnp
        import numpy as np
        B, L, D = (4, 64, 128)
        E, TOP_K = (16, 4)
        F = 4 * D
        diff = x[:, :, None, :] - keys
        dist2 = jnp.sum(diff * diff, axis=-1)
        logits = -dist2 + jnp.einsum('bld,ed->ble', x, rw) + rb
        topv, topi = jax.lax.top_k(logits, TOP_K)
        w = jax.nn.softmax(topv, axis=-1)
        hidden = jax.nn.gelu(jnp.einsum('bld,efd->blef', x, w1) + b1, approximate=False)
        exp_out = jnp.einsum('blef,edf->bled', hidden, w2) + b2
        sel = jnp.take_along_axis(exp_out, topi[..., None], axis=2)
        fused = jnp.sum(w[..., None] * sel, axis=2)
        return fused

    def _L1_attn_ref(x, Wq, Wk, Wv):
        import jax, jax.numpy as jnp
        import numpy as np
        D_MODEL = 128
        N_HEADS = 16
        HEAD_DIM = D_MODEL // N_HEADS

        def _rope(x):
            B = x.shape[0]
            half = HEAD_DIM // 2
            theta = 1.0 / 10000.0 ** (jnp.arange(0, HEAD_DIM, 2, dtype=jnp.float32) / HEAD_DIM)
            pos = jnp.arange(B, dtype=jnp.float32)
            ang = pos[:, None] * theta[None, :]
            ang2 = jnp.concatenate([ang, ang], axis=-1)
            cos = jnp.cos(ang2)[:, None, None, :]
            sin = jnp.sin(ang2)[:, None, None, :]
            neg_half = jnp.concatenate([x[..., :half], -x[..., half:]], axis=-1)
            return x * cos + neg_half * sin
        B, S, D = x.shape
        q = (x @ Wq.T).reshape(B, S, N_HEADS, HEAD_DIM)
        k = (x @ Wk.T).reshape(B, S, N_HEADS, HEAD_DIM)
        v = (x @ Wv.T).reshape(B, S, N_HEADS, HEAD_DIM)
        q = _rope(q)
        k = _rope(k)
        q = q.transpose(0, 2, 1, 3)
        k = k.transpose(0, 2, 1, 3)
        v = v.transpose(0, 2, 1, 3)
        scores = jnp.einsum('bhqd,bhkd->bhqk', q, k) / np.sqrt(HEAD_DIM)
        weights = jax.nn.softmax(scores, axis=-1)
        out = jnp.einsum('bhqk,bhkd->bhqd', weights, v)
        return out.transpose(0, 2, 1, 3).reshape(B, S, D)

    def _L1_ffn_ref(x, wqkv, q_scale, k_scale, wo, ln_g, ln_b, w1, b1, w2, b2):
        import jax, jax.numpy as jnp
        import numpy as np
        DIM = 128
        DEPTH = 2
        HEADS = 8
        DIM_HEAD = 64
        WINDOW = 64
        INNER = HEADS * DIM_HEAD
        HID = int(DIM * 4 * 2 / 3)
        B, N = (2, 1024)
        QK_SCALE = 8.0

        def shift_token(t):
            t1, t2 = jnp.split(t, 2, axis=-1)
            t2 = jnp.pad(t2, ((0, 0), (1, 0), (0, 0)))[:, :-1]
            return jnp.concatenate([t1, t2], axis=-1)

        def l2norm(t):
            return t / jnp.clip(jnp.linalg.norm(t, axis=-1, keepdims=True), 1e-12)

        def rotate_half(x):
            x1, x2 = jnp.split(x, 2, axis=-1)
            return jnp.concatenate([-x2, x1], axis=-1)

        def rotary_xpos(q, k):
            n = q.shape[-2]
            half_idx = jnp.arange(0, DIM_HEAD, 2, dtype=jnp.float32)
            inv_freq = 1.0 / 10000.0 ** (half_idx / DIM_HEAD)
            t = jnp.arange(n, dtype=jnp.float32)
            freqs = t[:, None] * inv_freq[None, :]
            freqs = jnp.concatenate([freqs, freqs], axis=-1)
            base = (half_idx + 0.4 * DIM_HEAD) / (1.4 * DIM_HEAD)
            power = (t - n // 2) / float(WINDOW // 2)
            scale = base[None, :] ** power[:, None]
            scale = jnp.concatenate([scale, scale], axis=-1)
            cos, sin = (jnp.cos(freqs), jnp.sin(freqs))
            q = q * cos * scale + rotate_half(q) * sin * scale
            k = k * cos / scale + rotate_half(k) * sin / scale
            return (q, k)

        def local_attention(q, k, v):
            b, h, n, d = q.shape
            w = n // WINDOW
            bq = q.reshape(b, h, w, WINDOW, d) * QK_SCALE
            bk = k.reshape(b, h, w, WINDOW, d)
            bv = v.reshape(b, h, w, WINDOW, d)

            def look_around(t):
                p = jnp.pad(t, ((0, 0), (0, 0), (1, 0), (0, 0), (0, 0)))
                return jnp.concatenate([p[:, :, :w], p[:, :, 1:]], axis=3)
            bk, bv = (look_around(bk), look_around(bv))
            bt = jnp.arange(n).reshape(w, WINDOW)
            btp = jnp.pad(bt, ((1, 0), (0, 0)), constant_values=-1)
            btk = jnp.concatenate([btp[:w], btp[1:]], axis=1)
            sim = jnp.einsum('bhwid,bhwjd->bhwij', bq, bk)
            i = bt[:, :, None]
            j = btk[:, None, :]
            mask = (i < j) | (i > j + WINDOW) | (j == -1)
            sim = jnp.where(mask, -jnp.finfo(sim.dtype).max, sim)
            attn = jax.nn.softmax(sim, axis=-1)
            out = jnp.einsum('bhwij,bhwjd->bhwid', attn, bv)
            return out.reshape(b, h, n, d)

        def _layer(x, wqkv, qs, ksc, wo, lg, lb, w1, b1, w2, b2):
            b, n, _ = x.shape
            h = shift_token(x)
            qkv = h @ wqkv
            q, k, v = jnp.split(qkv, 3, axis=-1)
            to_heads = lambda t: t.reshape(b, n, HEADS, DIM_HEAD).transpose(0, 2, 1, 3)
            q, k, v = (to_heads(q), to_heads(k), to_heads(v))
            q = l2norm(q) * qs
            k = l2norm(k) * ksc
            q, k = rotary_xpos(q, k)
            o = local_attention(q, k, v)
            o = o.transpose(0, 2, 1, 3).reshape(b, n, INNER)
            x = x + o @ wo
            h = shift_token(x)
            mu = h.mean(-1, keepdims=True)
            var = h.var(-1, keepdims=True)
            h = (h - mu) / jnp.sqrt(var + 1e-05) * lg + lb
            h = h @ w1 + b1
            a, g = jnp.split(h, 2, axis=-1)
            h = a * jax.nn.gelu(g, approximate=False)
            x = x + h @ w2 + b2
            return x
        for l in range(DEPTH):
            x = _layer(x, wqkv[l], q_scale[l], k_scale[l], wo[l], ln_g[l], ln_b[l], w1[l], b1[l], w2[l], b2[l])
        return x
    x = L0_attn_x
    x = _layernorm(x + _L0_attn_ref(x, L0_attn_wq, L0_attn_w_kv_down, L0_attn_w_k_up, L0_attn_w_v_up, L0_attn_wo), axis=-1)
    x = _layernorm(x + _L0_ffn_ref(x, L0_ffn_keys, L0_ffn_w1, L0_ffn_b1, L0_ffn_w2, L0_ffn_b2, L0_ffn_rw, L0_ffn_rb), axis=-1)
    x = _layernorm(x + _L1_attn_ref(x, L1_attn_Wq, L1_attn_Wk, L1_attn_Wv), axis=-1)
    x = _layernorm(x + _L1_ffn_ref(x, L1_ffn_wqkv, L1_ffn_q_scale, L1_ffn_k_scale, L1_ffn_wo, L1_ffn_ln_g, L1_ffn_ln_b, L1_ffn_w1, L1_ffn_b1, L1_ffn_w2, L1_ffn_b2), axis=-1)
    return x

_drawn_inputs = setup_inputs


def setup_inputs(seed=0):
    import zlib

    import numpy as np

    out = dict(_drawn_inputs(seed))
    spreads = {'L0_ffn_b1': (0.0, 0.321),
     'L0_ffn_b2': (0.0, 0.1),
     'L0_ffn_rb': (0.0, 2.0),
     'L1_ffn_q_scale': (1.0, 0.6),
     'L1_ffn_k_scale': (1.0, 0.6),
     'L1_ffn_ln_g': (1.0, 0.6),
     'L1_ffn_ln_b': (0.0, 0.8),
     'L1_ffn_b1': (0.0, 0.8),
     'L1_ffn_b2': (0.0, 0.544)}
    factors = {'L0_ffn_rw': 8.0,
     'L1_ffn_wqkv': 3.105,
     'L1_ffn_wo': 3.184,
     'L1_ffn_w1': 6.612,
     'L1_ffn_w2': 6.483}
    for name, (base, spread) in spreads.items():
        noise = np.random.default_rng([zlib.crc32(name.encode()), seed]).standard_normal(out[name].shape)
        drawn = base * np.exp(spread * noise) if base else spread * noise
        out[name] = jnp.asarray(drawn.astype(out[name].dtype))
    for name, factor in factors.items():
        out[name] = (out[name] * factor).astype(out[name].dtype)
    return out
```

```python
from contextlib import ExitStack

import numpy as np

import concourse.bass as bass
from concourse import mybir

ALU = mybir.AluOpType
ACT = mybir.ActivationFunctionType
AX = mybir.AxisListType
F32 = mybir.dt.float32
BF16 = mybir.dt.bfloat16

P = 128
NB = 4
S = 512
D = 128
TPB = S // P
NT = NB * TPB
EPS = 1e-5

HD0 = 64
NP0 = 8
LAT = 64
UNITS = [(i, j) for i in reversed(range(TPB)) for j in range(2)]
NU = len(UNITS)

NE = 16
FF = 512
FB = FF // P
TOPK = 4


def attention0(nc, ctx, io, keep):

    def sb(name, shape, dt=F32):
        return ctx.enter_context(nc.sbuf_tensor("a_" + name, shape, dt))

    def sem(name):
        return nc.alloc_semaphore("a_" + name)

    ps = keep["ps"]
    qk_ps = ps[:, 0:2, :].rearrange("p a (t c) -> p (a t) c", c=256)
    o_ps = ps[:, 6, :]
    m_ps = ps[:, 7, :]

    wqk = sb("wqk", [P, NP0, 256])
    wvo = sb("wvo", [P, NP0, P])
    wkT = sb("wkT", [LAT, NP0 * P])
    wd = sb("wd", [LAT, P])
    wdT = sb("wdT", [P, LAT])
    wv = sb("wv", [P, NP0, LAT])
    woT = sb("woT", [P, NP0, P])
    cos = sb("cos", [P, TPB, HD0])
    sin = sb("sin", [P, TPB, HD0])
    cmask = sb("cmask", [P, P], BF16)
    identb = sb("identb", [P, P], BF16)
    xT = sb("xT", [P, S])
    xb = sb("xb", [P, TPB, D])
    lat = sb("lat", [P, TPB, LAT])
    qk_c = sb("qk_c", [P, TPB, 256])
    qk_s = sb("qk_s", [P, TPB, 256])
    qk_r = sb("qk_r", [P, TPB, 256])
    qkT = sb("qkT", [P, 2, S])
    negmax = sb("negmax", [P, NU])
    den = sb("den", [P, NU])
    rden = sb("rden", [P, NU])
    prob = sb("prob", [P, 4, S])
    probT = sb("probT", [P, 2, S])
    on = sb("on", [P, TPB, P])
    oT = sb("oT", [P, S])
    stats = sb("stats", [P, TPB, 6])
    mv = sb("mv", [P, TPB, 2])
    std = sb("std", [P, TPB])
    rstd = sb("rstd", [P, TPB])
    xf = sb("xf", [P, TPB, D])
    xfT = sb("xfT", [P, S])
    keysT = sb("keysT", [P, NE])
    rwT = sb("rwT", [P, NE])
    router = sb("router", [P, NE])
    keys2 = sb("keys2", [P, NE])
    rbrow = sb("rbrow", [1, NE])
    rbias = sb("rbias", [1, NE])
    ones = sb("ones", [P, P])
    neg_half = sb("neg_half", [P, TPB])
    eps = sb("eps", [P, TPB])
    ident = keep["ident"]

    w_ld = sem("w_ld")
    xT_ld = sem("xT_ld")
    xb_ld = sem("xb_ld")
    set_mm = sem("set_mm")
    set_ev = sem("set_ev")
    ones_set = sem("ones_set")
    wq_scaled = sem("wq_scaled")
    rt1 = sem("rt1")
    lat_mm = sem("lat_mm")
    lat_ev = sem("lat_ev")
    qk_mm = sem("qk_mm")
    rope_mul = sem("rope_mul")
    rope_add = sem("rope_add")
    qkT_mm = sem("qkT_mm")
    qkT_ev = sem("qkT_ev")
    s_mm = sem("s_mm")
    max_done = sem("max_done")
    exp_done = sem("exp_done")
    pT_mm = sem("pT_mm")
    pT_ev0 = sem("pT_ev0")
    pT_ev1 = sem("pT_ev1")
    o_mm = sem("o_mm")
    recip = sem("recip")
    o_norm = sem("o_norm")
    oT_mm = sem("oT_mm")
    oT_ev = sem("oT_ev")
    y_mm = sem("y_mm")
    y_add = sem("y_add")
    st_done = sem("st_done")
    ag_done = sem("ag_done")
    held = sem("held")
    std_done = sem("std_done")
    rstd_done = sem("rstd_done")
    ln_done = sem("ln_done")
    xfT_mm = sem("xfT_mm")
    xfT_ev = sem("xfT_ev")
    lg_mm = sem("lg_mm")
    lg_ev = sem("lg_ev")
    x_kept = sem("x_kept")

    NW = 14
    SCALE = HD0 ** -0.5

    block = ctx.enter_context(nc.Block())

    @block.sync
    def _(sp):
        def load(dst, src):
            sp.dma_start(dst, src).then_inc(w_ld, 16)

        load(wd[:, :], io["wd"])
        load(wkT[:, :], io["wkT"])
        load(wdT[:, :], io["wdT"])
        load(wqk[:, :, 0:P], io["wqT"].rearrange("c (h n) -> c h n", h=NP0))
        load(cos[:, :, :], io["cos0"].rearrange("(t p) d -> p t d", p=P))
        load(sin[:, :, :], io["sin0"].rearrange("(t p) d -> p t d", p=P))
        load(cmask[:, :], io["cmask"])
        load(identb[:, :], io["identb"])
        load(ident[:, :], io["ident"])
        load(wv[:, :, :], io["wv"].rearrange("(h q) l -> q h l", q=P))
        load(woT[:, :, :], io["woT"].rearrange("(h q) n -> q h n", q=P))
        load(keysT[:, :], io["keysT"])
        load(rwT[:, :], io["rwT"])
        load(rbrow[:, :], io["rb"])
        with sp.Fori(0, NB) as b:
            sp.wait_ge(qk_mm, NP0 * b)
            sp.wait_ge(lat_mm, b)
            sp.dma_start(xT[:, :], io["xT"][:, bass.ds(b * S, S)]).then_inc(xT_ld, 16)
            sp.wait_ge(ln_done, b)
            sp.dma_start(xb[:, :, :], io["x"][:, bass.ds(b * TPB, TPB), :]).then_inc(xb_ld, 16)
        sp.wait_ge(qk_mm, NP0 * NB)
        sp.wait_ge(lat_mm, NB)
        sp.dma_start(xT[:, :], io["xT"][:, 0:S]).then_inc(xT_ld, 16)

    @block.gpsimd
    def _(pool):
        nc.gpsimd.memset(ones[:, :], 1.0).then_inc(ones_set, 1)
        nc.gpsimd.memset(neg_half[:, :], -0.5).then_inc(ones_set, 1)
        nc.gpsimd.memset(eps[:, :], EPS).then_inc(ones_set, 1)

        def rope_sum(n):
            pool.wait_ge(rope_mul, n + 1)
            pool.wait_ge(qkT_mm, 2 * n)
            nc.gpsimd.tensor_tensor(qk_r[:, :, :], qk_c[:, :, :], qk_s[:, :, :], ALU.add).then_inc(rope_add, 1)

        rope_sum(0)
        with pool.Fori(0, NB) as b:
            with pool.Fori(0, NP0) as h:
                rope_sum(b * NP0 + h + 1)
            pool.wait_ge(ones_set, 3)
            pool.wait_ge(ag_done, b + 1)
            nc.gpsimd.tensor_tensor(std[:, :], mv[:, :, 1], eps[:, :], ALU.add).then_inc(std_done, 1)
            pool.wait_ge(std_done, b + 1)
            nc.gpsimd.tensor_tensor(rstd[:, :], std[:, :], neg_half[:, :], ALU.pow).then_inc(rstd_done, 1)
            pool.wait_ge(ln_done, b + 1)
            nc.gpsimd.tensor_copy(keep["x"][:, bass.ds(b * TPB, TPB), :], xf[:, :, :]).then_inc(x_kept, 1)
            pool.wait_ge(xfT_ev, b + 1)
            nc.gpsimd.tensor_copy(keep["xT"][:, bass.ds(b, 1), :].rearrange("p a n -> p (a n)"), xfT[:, :]).then_inc(x_kept, 1)

    @block.scalar
    def _(act):
        act.wait_ge(set_mm, 1)
        nc.scalar.activation(wqk[:, :, P:2 * P], ps[:, 0:2, :].rearrange("p a (h n) -> p (a h) n", n=P),
                             ACT.Copy).then_inc(set_ev, 1)
        act.wait_ge(set_mm, 2)
        nc.scalar.activation(wvo[:, :, :], ps[:, 2:4, :].rearrange("p a (h n) -> p (a h) n", n=P),
                             ACT.Copy).then_inc(set_ev, 1)

        def qkT_evac(n):
            for w in range(2):
                act.wait_ge(qkT_mm, 2 * n + w + 1)
                nc.scalar.activation(qkT[:, w, :], ps[:, w, :], ACT.Copy).then_inc(qkT_ev, 1)

        def pT_evac(it, u):
            i = UNITS[u][0]
            act.wait_ge(pT_mm, NU * it + u + 1)
            nc.scalar.activation(probT[:, 1, 0:(i + 1) * P], ps[:, 5, 0:(i + 1) * P], ACT.Copy).then_inc(pT_ev1, 1)

        def exp(it, u):
            i, j = UNITS[u]
            n = (i + 1) * P
            act.wait_ge(max_done, NU * it + u + 1)
            if u == 0:
                act.wait_ge(recip, it)
            nc.scalar.activation(prob[:, u % 4, 0:n], ps[:, 2 + j, 0:n], ACT.Exp, bias=negmax[:, u:u + 1],
                                 accum_out=den[:, 2 * i + j:2 * i + j + 1]).then_inc(exp_done, 1)

        qkT_evac(0)
        with act.Fori(0, NB) as b:
            with act.Fori(0, NP0) as h:
                it = b * NP0 + h
                for u in range(NU):
                    exp(it, u)
                    if u in (2, 4, 6):
                        pT_evac(it, u - 1)
                pT_evac(it, 7)
                qkT_evac(it + 1)
                act.wait_ge(oT_mm, it + 1)
                nc.scalar.activation(oT[:, :], m_ps, ACT.Copy).then_inc(oT_ev, 1)
            act.wait_ge(xfT_mm, b + 1)
            act.wait_ge(x_kept, 2 * b)
            nc.scalar.activation(xfT[:, :], m_ps, ACT.Copy).then_inc(xfT_ev, 1)

    @block.vector
    def _(dve):
        dve.wait_ge(w_ld, 16 * NW)
        nc.vector.tensor_scalar(wqk[:, :, 0:P], wqk[:, :, 0:P], SCALE, None, ALU.mult).then_inc(wq_scaled, 1)
        nc.vector.scalar_tensor_tensor(router[:, :], keysT[:, :], 2.0, rwT[:, :], ALU.mult, ALU.add).then_inc(rt1, 1)
        nc.vector.tensor_tensor(keys2[:, :], keysT[:, :], keysT[:, :], ALU.mult).then_inc(rt1, 1)
        dve.wait_ge(set_mm, 3)
        nc.vector.tensor_tensor(rbias[:, :], rbrow[:, :], ps[0:1, 4, 0:NE], ALU.subtract).then_inc(rt1, 1)

        def rope(n, part):
            g = qk_ps.rearrange("p t (g d) -> p t g d", d=HD0)
            h = HD0 // 2
            if part == 0:
                dve.wait_ge(qk_mm, n + 1)
                dve.wait_ge(rope_add, n)
                nc.vector.tensor_tensor(qk_c[:, :, :].rearrange("p t (g d) -> p t g d", d=HD0), g,
                                        cos[:, :, None, :].broadcast_to([P, TPB, 4, HD0]), ALU.mult)
            else:
                for a, last in ((0, False), (h, True)):
                    ins = nc.vector.tensor_tensor(
                        qk_s[:, :, :].rearrange("p t (g d) -> p t g d", d=HD0)[:, :, :, a:a + h],
                        g[:, :, :, h - a:2 * h - a],
                        sin[:, :, None, a:a + h].broadcast_to([P, TPB, 4, h]), ALU.mult)
                ins.then_inc(rope_mul, 1)

        def rowmax(it, u):
            i, j = UNITS[u]
            dve.wait_ge(s_mm, NU * it + u + 1)
            nc.vector.tensor_reduce(negmax[:, u:u + 1], ps[:, 2 + j, 0:(i + 1) * P], AX.X, ALU.max,
                                    negate=True).then_inc(max_done, 1)

        def pT_evac(it, u):
            i = UNITS[u][0]
            dve.wait_ge(pT_mm, NU * it + u + 1)
            nc.vector.tensor_copy(probT[:, 0, 0:(i + 1) * P], ps[:, 4, 0:(i + 1) * P]).then_inc(pT_ev0, 1)

        rope(0, 0)
        rope(0, 1)
        rowmax(0, 0)
        rowmax(0, 1)
        with dve.Fori(0, NB) as b:
            dve.wait_ge(lat_mm, b + 1)
            nc.vector.tensor_copy(lat[:, :, :], m_ps[:, 0:TPB * LAT].rearrange("p (t l) -> p t l", l=LAT)
                                  ).then_inc(lat_ev, 1)
            with dve.Fori(0, NP0) as h:
                it = b * NP0 + h
                for k in range(4):
                    pT_evac(it, 2 * k)
                    if k < 3:
                        rowmax(it, 2 * k + 2)
                        rowmax(it, 2 * k + 3)
                    if k < 2:
                        rope(it + 1, k)
                dve.wait_ge(exp_done, NU * (it + 1))
                nc.vector.reciprocal(rden[:, :], den[:, :]).then_inc(recip, 1)
                dve.wait_ge(recip, it + 1)
                dve.wait_ge(o_mm, it + 1)
                dve.wait_ge(oT_mm, it)
                nc.vector.tensor_tensor(on[:, :, :].rearrange("p t (j d) -> p (t j) d", j=2),
                                        o_ps.rearrange("p (u d) -> p u d", u=NU),
                                        rden[:, :, None].broadcast_to([P, NU, LAT]), ALU.mult).then_inc(o_norm, 1)
                rowmax(it + 1, 0)
                rowmax(it + 1, 1)
                dve.wait_ge(xb_ld, 16 * (b + 1))
                dve.wait_ge(y_mm, it + 1)
                dve.wait_ge(y_add, it)
                nc.vector.tensor_tensor(xb[:, :, :], m_ps.rearrange("p (t d) -> p t d", d=D), xb[:, :, :],
                                        ALU.add).then_inc(y_add, 1)
            dve.wait_ge(y_add, NP0 * (b + 1))
            for t in range(TPB):
                nc.vector.bn_stats(stats[:, t, :], xb[:, t, :]).then_inc(st_done, 1)
            dve.wait_ge(st_done, TPB * (b + 1))
            dve.sem_inc(held, 1)
            for t in range(TPB):
                ins = nc.vector.bn_aggr(mv[:, t, :], stats[:, t, :])
            ins.then_inc(ag_done, 1)
            dve.wait_ge(rstd_done, b + 1)
            dve.wait_ge(x_kept, 2 * b)
            dve.wait_ge(xfT_mm, b)
            for t in range(TPB):
                ins = nc.vector.tensor_scalar(xf[:, t, :], xb[:, t, :], mv[:, t, 0:1], rstd[:, t:t + 1],
                                              ALU.subtract, ALU.mult)
            ins.then_inc(ln_done, 1)
            dve.wait_ge(lg_mm, b + 1)
            nc.vector.tensor_copy(keep["logits"][:, bass.ds(b * TPB, TPB), :],
                                  m_ps[:, 0:TPB * NE].rearrange("p (t e) -> p t e", e=NE)).then_inc(lg_ev, 1)

    @block.tensor
    def _(pe):
        pe.wait_ge(w_ld, 16 * NW)
        for a in range(2):
            ins = nc.tensor.matmul(ps[:, a, :], wd[:, :], wkT[:, a * 512:(a + 1) * 512], start=True, stop=True)
        ins.then_inc(set_mm, 1)
        for h in range(NP0):
            for j in range(2):
                r = slice(64 * j, 64 * j + 64)
                ins = nc.tensor.matmul(ps[r, 2 + h // 4, (h % 4) * P:(h % 4 + 1) * P], wv[r, h, :], woT[r, h, :],
                                       start=True, stop=True)
        ins.then_inc(set_mm, 1)
        pe.wait_ge(rt1, 2)
        pe.wait_ge(ones_set, 1)
        nc.tensor.matmul(ps[0:1, 4, 0:NE], ones[:, 0:1], keys2[:, :], start=True, stop=True).then_inc(set_mm, 1)
        pe.wait_ge(set_ev, 2)
        pe.wait_ge(wq_scaled, 1)
        pe.wait_ge(rt1, 3)

        def project(n):
            pe.wait_ge(xT_ld, 16 * (n // NP0 + 1))
            pe.wait_ge(qkT_ev, 2 * n)
            for t in range(TPB):
                ins = nc.tensor.matmul(qk_ps[:, t, :], xT[:, t * P:(t + 1) * P],
                                       wqk[:, n % NP0, :] if isinstance(n, int) else
                                       wqk[:, bass.ds(n % NP0, 1), :].rearrange("p a n -> p (a n)"),
                                       start=True, stop=True)
            ins.then_inc(qk_mm, 1)

        def turn_qk(n):
            pe.wait_ge(rope_add, n + 1)
            for w in range(2):
                for t in range(TPB):
                    ins = nc.tensor.transpose(ps[:, w, t * P:(t + 1) * P], qk_r[:, t, w * P:(w + 1) * P],
                                              ident[:, :])
                ins.then_inc(qkT_mm, 1)

        def scores(it, u, waits=True):
            i, j = UNITS[u]
            if u == 0:
                pe.wait_ge(qkT_ev, 2 * it + 2)
            if waits:
                pe.wait_ge(exp_done, NU * it + u - 1)
            r = slice(64 * j, 64 * j + 64)
            nc.tensor.matmul(ps[:, 2 + j, 0:(i + 1) * P], qkT[r, 0, i * P:(i + 1) * P], qkT[r, 1, 0:(i + 1) * P],
                             start=True, stop=False, skip_group_check=True)
            nc.tensor.matmul(ps[:, 2 + j, i * P:(i + 1) * P], identb[:, :], cmask[:, :],
                             start=False, stop=True, skip_group_check=True).then_inc(s_mm, 1)

        def turn_p(it, u):
            i, j = UNITS[u]
            pe.wait_ge(exp_done, NU * it + u + 1)
            pe.wait_ge(pT_ev1 if j else pT_ev0, 4 * it + u // 2)
            for t in range(i + 1):
                ins = nc.tensor.transpose(ps[:, 4 + j, t * P:(t + 1) * P], prob[:, u % 4, t * P:(t + 1) * P],
                                          ident[:, :])
            ins.then_inc(pT_mm, 1)

        def values(it, u):
            i, j = UNITS[u]
            pe.wait_ge(pT_ev1 if j else pT_ev0, 4 * it + u // 2 + 1)
            if u == 0:
                pe.wait_ge(o_norm, it)
            c = 64 * (2 * i + j)
            for t in range(i + 1):
                ins = nc.tensor.matmul(o_ps[:, c:c + 64], probT[:, j, t * P:(t + 1) * P], lat[:, t, :],
                                       start=(t == 0), stop=(t == i))
            if u == NU - 1:
                ins.then_inc(o_mm, 1)

        project(0)
        turn_qk(0)
        scores(0, 0, waits=False)
        scores(0, 1, waits=False)
        with pe.Fori(0, NB) as b:
            pe.wait_ge(xT_ld, 16 * (b + 1))
            pe.wait_ge(lg_ev, b)
            for t in range(TPB):
                ins = nc.tensor.matmul(m_ps[:, t * LAT:(t + 1) * LAT], xT[:, t * P:(t + 1) * P], wdT[:, :],
                                       start=True, stop=True)
            ins.then_inc(lat_mm, 1)
            with pe.Fori(0, NP0) as h:
                it = b * NP0 + h
                pe.wait_ge(lat_ev, b + 1)
                for u in range(NU):
                    if u < 6:
                        scores(it, u + 2)
                    if u == 1:
                        project(it + 1)
                    if u == 6:
                        turn_qk(it + 1)
                    turn_p(it, u)
                    if u:
                        values(it, u - 1)
                scores(it + 1, 0)
                values(it, 7)
                scores(it + 1, 1)
                pe.wait_ge(o_norm, it + 1)
                pe.wait_ge(y_add, it)
                for t in range(TPB):
                    ins = nc.tensor.transpose(m_ps[:, t * P:(t + 1) * P], on[:, t, :], ident[:, :])
                ins.then_inc(oT_mm, 1)
                pe.wait_ge(oT_ev, it + 1)
                for t in range(TPB):
                    ins = nc.tensor.matmul(m_ps[:, t * P:(t + 1) * P], oT[:, t * P:(t + 1) * P],
                                           wvo[:, bass.ds(h, 1), :].rearrange("p a n -> p (a n)"),
                                           start=True, stop=True)
                ins.then_inc(y_mm, 1)
            pe.wait_ge(ln_done, b + 1)
            pe.wait_ge(y_add, NP0 * (b + 1))
            for t in range(TPB):
                ins = nc.tensor.transpose(m_ps[:, t * P:(t + 1) * P], xf[:, t, :], ident[:, :])
            ins.then_inc(xfT_mm, 1)
            pe.wait_ge(xfT_ev, b + 1)
            for t in range(TPB):
                nc.tensor.matmul(m_ps[:, t * NE:(t + 1) * NE], xfT[:, t * P:(t + 1) * P], router[:, :],
                                 start=True, stop=False)
                ins = nc.tensor.matmul(m_ps[:, t * NE:(t + 1) * NE], ones[0:1, :], rbias[:, :],
                                       start=False, stop=True)
            ins.then_inc(lg_mm, 1)



class Norm:

    def __init__(self, nc, ctx, keep, ps, banks, ready, counts, prefix):
        def sb(name, shape):
            return ctx.enter_context(nc.sbuf_tensor(prefix + name, shape, F32))

        def sem(name):
            return nc.alloc_semaphore(prefix + name)

        self.nc, self.keep, self.ps, self.banks, self.ready, self.counts = nc, keep, ps, banks, ready, counts
        self.stats = sb("stats", [P, NT, 6])
        self.mv = sb("mv", [P, NT, 2])
        self.var = sb("var", [P, NT])
        self.rstd = sb("rstd", [P, NT])
        self.eps = sb("eps", [P, TPB])
        self.neg_half = sb("neg_half", [P, TPB])
        self.consts = sem("consts")
        self.stats_done = sem("stats_done")
        self.mv_done = sem("mv_done")
        self.var_done = sem("var_done")
        self.rstd_done = sem("rstd_done")
        self.norm_done = sem("norm_done")
        self.turn_mm = sem("turn_mm")
        self.turn_ev = sem("turn_ev")

    def pool(self, pool):
        nc = self.nc
        nc.gpsimd.memset(self.eps[:, :], EPS).then_inc(self.consts, 1)
        nc.gpsimd.memset(self.neg_half[:, :], -0.5).then_inc(self.consts, 1)
        pool.wait_ge(self.consts, 2)
        for b in range(NB):
            t = slice(b * TPB, (b + 1) * TPB)
            pool.wait_ge(self.mv_done, b + 1)
            nc.gpsimd.tensor_tensor(self.var[:, t], self.mv[:, t, 1], self.eps[:, :], ALU.add
                                    ).then_inc(self.var_done, 1)
            pool.wait_ge(self.var_done, b + 1)
            nc.gpsimd.tensor_tensor(self.rstd[:, t], self.var[:, t], self.neg_half[:, :], ALU.pow
                                    ).then_inc(self.rstd_done, 1)

    def vector(self, dve):
        nc, x = self.nc, self.keep["x"]

        def moments(b):
            dve.wait_ge(self.ready, self.counts[b])
            for t in range(b * TPB, (b + 1) * TPB):
                nc.vector.bn_stats(self.stats[:, t, :], x[:, t, :]).then_inc(self.stats_done, 1)
            dve.wait_ge(self.stats_done, TPB * (b + 1))
            for t in range(b * TPB, (b + 1) * TPB):
                ins = nc.vector.bn_aggr(self.mv[:, t, :], self.stats[:, t, :])
            ins.then_inc(self.mv_done, 1)

        def normalise(b):
            dve.wait_ge(self.rstd_done, b + 1)
            for t in range(b * TPB, (b + 1) * TPB):
                ins = nc.vector.tensor_scalar(x[:, t, :], x[:, t, :], self.mv[:, t, 0:1], self.rstd[:, t:t + 1],
                                              ALU.subtract, ALU.mult)
            ins.then_inc(self.norm_done, 1)

        moments(0)
        for b in range(NB):
            if b + 1 < NB:
                moments(b + 1)
            normalise(b)

    def tensor(self, pe):
        for b in range(NB):
            pe.wait_ge(self.norm_done, b + 1)
            for t in range(TPB):
                ins = self.nc.tensor.transpose(self.ps[:, self.banks[b], t * P:(t + 1) * P],
                                               self.keep["x"][:, b * TPB + t, :], self.keep["ident"][:, :])
            ins.then_inc(self.turn_mm, 1)

    def scalar(self, act):
        for b in range(NB):
            act.wait_ge(self.turn_mm, b + 1)
            self.nc.scalar.activation(self.keep["xT"][:, b, :], self.ps[:, self.banks[b], :],
                                      ACT.Copy).then_inc(self.turn_ev, 1)


def experts0(nc, ctx, io, keep):

    def sb(name, shape, dt=F32):
        return ctx.enter_context(nc.sbuf_tensor("m_" + name, shape, dt))

    def sem(name):
        return nc.alloc_semaphore("m_" + name)

    ps = keep["ps"]

    w1 = sb("w1", [P, 2, FF + FB])
    w2 = sb("w2", [P, 2, FB, D])
    b2big = sb("b2big", [P, P // NE, D])
    iota = sb("iota", [P, NE])
    top = sb("top", [P, NT, 8])
    topi = sb("topi", [P, NT, 8], mybir.dt.uint32)
    topf = sb("topf", [P, NT, TOPK])
    tops = sb("tops", [P, NT, TOPK])
    tope = sb("tope", [P, NT, TOPK])
    topz = sb("topz", [P, NT])
    topr = sb("topr", [P, NT])
    topw = sb("topw", [P, NT, TOPK])
    hit = sb("hit", [P, NT, TOPK, NE])
    hitw = sb("hitw", [P, NT, TOPK, NE])
    gates = sb("gates", [P, NT, NE])
    gatesT = sb("gatesT", [P, 2, P])
    hid = sb("hid", [P, 2, FB, S])
    x, xT, logits, ident = keep["x"], keep["xT"], keep["logits"], keep["ident"]

    w1_ld = [sem(f"w1_ld{k}") for k in range(2)]
    w2_ld = [sem(f"w2_ld{k}") for k in range(2)]
    c_ld = sem("c_ld")
    b2_zero = sem("b2_zero")
    top_done = sem("top_done")
    topi_done = sem("topi_done")
    gate_step = sem("gate_step")
    top_exp = sem("top_exp")
    gT_mm = sem("gT_mm")
    gT_ev = sem("gT_ev")
    b2_mm = sem("b2_mm")
    b2_add = sem("b2_add")
    up_mm = sem("up_mm")
    gelu_done = sem("gelu_done")
    down_mm = sem("down_mm")
    acc_done = sem("acc_done")
    NC = 1 + P // NE
    STEPS = NE * NB
    norm = Norm(nc, ctx, keep, ps, [0, 1, 2, 3], b2_add, [1, 2, 3, 4], "mn_")

    block = ctx.enter_context(nc.Block())

    @block.sync
    def _(sp):
        sp.dma_start(iota[:, :], io["iota"]).then_inc(c_ld, 16)
        for k in range(2):
            sp.dma_start(w1[:, k, :], io["w1T"][:, k, :]).then_inc(w1_ld[k], 16)
            sp.dma_start(w2[:, k, :, :], io["w2T"][:, k * FB:(k + 1) * FB, :]).then_inc(w2_ld[k], 16)
        sp.wait_ge(b2_zero, 1)
        for t in range(P // NE):
            sp.dma_start(b2big[t * NE:(t + 1) * NE, t, :], io["b2"]).then_inc(c_ld, 16)
        with sp.Fori(1, NE // 2) as pair:
            for k in range(2):
                e = pair * 2 + k
                sp.wait_ge(gelu_done, FB * NB * (e - 1))
                sp.dma_start(w1[:, k, :], io["w1T"][:, bass.ds(e, 1), :].rearrange("d a f -> d (a f)")
                             ).then_inc(w1_ld[k], 16)
                sp.wait_ge(down_mm, NB * (e - 1))
                sp.dma_start(w2[:, k, :, :], io["w2T"][:, bass.ds(e * FB, FB), :]).then_inc(w2_ld[k], 16)
        sp.wait_ge(gelu_done, FB * NB * (NE - 1))
        sp.dma_start(w1[:, 0, :], io["w1T"][:, 0, :]).then_inc(w1_ld[0], 16)

    @block.gpsimd
    def _(pool):
        nc.gpsimd.memset(b2big[:, :, :], 0.0).then_inc(b2_zero, 1)
        norm.pool(pool)

    @block.scalar
    def _(act):
        act.wait_ge(gate_step, 2)
        nc.scalar.activation(tope[:, :, :], tops[:, :, :], ACT.Exp).then_inc(top_exp, 1)
        act.wait_ge(c_ld, 16 * NC)
        with act.Fori(0, NE // 2) as pair:
            for k in range(2):
                for c in range(NB):
                    n = pair * (2 * NB) + (k * NB + c)
                    for f in range(FB):
                        act.wait_ge(up_mm, n * FB + f + 1)
                        nc.scalar.activation(hid[:, c % 2, f, :], ps[:, f, :], ACT.Gelu,
                                             bias=w1[:, k, FF + f:FF + f + 1]
                                             ).then_inc(gelu_done, 1)
        act.wait_ge(gT_mm, 1)
        nc.scalar.activation(gatesT[:, :, :], ps[:, 6, 0:2 * P].rearrange("p (a t) -> p a t", a=2), ACT.Copy
                             ).then_inc(gT_ev, 1)
        norm.scalar(act)

    @block.vector
    def _(dve):
        for t in range(NT):
            nc.vector.max(top[:, t, :], logits[:, t, :]).then_inc(top_done, 1)
        for t in range(NT):
            dve.wait_ge(top_done, t + 1)
            nc.vector.max_index(topi[:, t, :], top[:, t, :], logits[:, t, :]).then_inc(topi_done, 1)
        dve.wait_ge(topi_done, NT)
        nc.vector.tensor_copy(topf[:, :, :], topi[:, :, 0:TOPK]).then_inc(gate_step, 1)
        nc.vector.tensor_tensor(tops[:, :, :], top[:, :, 0:TOPK], top[:, :, 0:1].broadcast_to([P, NT, TOPK]),
                                ALU.subtract).then_inc(gate_step, 1)
        dve.wait_ge(gate_step, 1)
        dve.wait_ge(c_ld, 16 * NC)
        nc.vector.tensor_tensor(hit[:, :, :, :], topf[:, :, :, None].broadcast_to([P, NT, TOPK, NE]),
                                iota[:, None, None, :].broadcast_to([P, NT, TOPK, NE]), ALU.is_equal
                                ).then_inc(gate_step, 1)
        dve.wait_ge(top_exp, 1)
        nc.vector.tensor_reduce(topz[:, :], tope[:, :, :], AX.X, ALU.add).then_inc(gate_step, 1)
        dve.wait_ge(gate_step, 4)
        nc.vector.reciprocal(topr[:, :], topz[:, :]).then_inc(gate_step, 1)
        dve.wait_ge(gate_step, 5)
        nc.vector.tensor_tensor(topw[:, :, :], tope[:, :, :], topr[:, :, None].broadcast_to([P, NT, TOPK]),
                                ALU.mult).then_inc(gate_step, 1)
        dve.wait_ge(gate_step, 6)
        nc.vector.tensor_tensor(hitw[:, :, :, :], hit[:, :, :, :], topw[:, :, :, None].broadcast_to([P, NT, TOPK, NE]),
                                ALU.mult).then_inc(gate_step, 1)
        dve.wait_ge(gate_step, 7)
        nc.vector.tensor_reduce(gates[:, :, :], hitw[:, :, :, :].rearrange("p t k e -> p t e k"), AX.X, ALU.add
                                ).then_inc(acc_done, NB)
        with dve.Fori(0, NE // 2) as pair:
            for k in range(2):
                for c in range(NB):
                    n = pair * (2 * NB) + (k * NB + c)
                    dve.wait_ge(down_mm, n + 1)
                    dve.wait_ge(acc_done, n + 1)
                    for t in range(TPB):
                        tt = c * TPB + t
                        ins = nc.vector.scalar_tensor_tensor(
                            x[:, tt, :], ps[:, 4 + c % 2, t * D:(t + 1) * D],
                            gates[:, tt, bass.ds(pair * 2 + k, 1)], x[:, tt, :], ALU.mult, ALU.add)
                    ins.then_inc(acc_done, 1)
        dve.wait_ge(acc_done, NB + STEPS)
        for b in range(NB):
            dve.wait_ge(b2_mm, b + 1)
            ts = slice(b * TPB, (b + 1) * TPB)
            nc.vector.tensor_tensor(x[:, ts, :], ps[:, 4 + b, :].rearrange("p (t d) -> p t d", d=D), x[:, ts, :],
                                    ALU.add).then_inc(b2_add, 1)
        norm.vector(dve)

    @block.tensor
    def _(pe):
        def up(n, c, k):
            for f in range(FB):
                pe.wait_ge(gelu_done, n * FB - FB + f + 1 if not isinstance(n, int) else 0)
                nc.tensor.matmul(ps[:, f, :], w1[:, k, f * P:(f + 1) * P], xT[:, c, :],
                                 start=True, stop=True).then_inc(up_mm, 1)

        pe.wait_ge(w1_ld[0], 16)
        up(0, 0, 0)
        with pe.Fori(0, NE // 2) as pair:
            for k in range(2):
                for c in range(NB):
                    n = pair * (2 * NB) + (k * NB + c)
                    if c == NB - 1:
                        pe.wait_ge(w1_ld[1 - k], 16 * (pair + 1 + k))
                        up(n + 1, 0, 1 - k)
                    else:
                        up(n + 1, c + 1, k)
                    if c == 0:
                        pe.wait_ge(w2_ld[k], 16 * (pair + 1))
                    pe.wait_ge(gelu_done, n * FB + FB)
                    pe.wait_ge(acc_done, n + NB - 1)
                    for t in range(TPB):
                        for f in range(FB):
                            ins = nc.tensor.matmul(ps[:, 4 + c % 2, t * D:(t + 1) * D],
                                                   hid[:, c % 2, f, t * P:(t + 1) * P], w2[:, k, f, :],
                                                   start=(f == 0), stop=(f == FB - 1))
                    ins.then_inc(down_mm, 1)
        for a in range(2):
            ins = nc.tensor.transpose(ps[:, 6, a * P:(a + 1) * P],
                                      gates[:, a * 8:(a + 1) * 8, :].rearrange("p t e -> p (t e)"), ident[:, :])
        ins.then_inc(gT_mm, 1)
        pe.wait_ge(gT_ev, 1)
        pe.wait_ge(c_ld, 16 * NC)
        pe.wait_ge(acc_done, NB + STEPS)
        for b in range(NB):
            nc.tensor.matmul(ps[:, 4 + b, :], gatesT[:, b // 2, :],
                             b2big[:, (b % 2) * TPB:(b % 2 + 1) * TPB, :].rearrange("p t d -> p (t d)"),
                             start=True, stop=True).then_inc(b2_mm, 1)
        norm.tensor(pe)


NH1 = 16
HD1 = 8
QUADS = NH1 // 4
KS = 9 * HD1
NSH = 3


def attention1(nc, ctx, io, keep):

    def sb(name, shape, dt=F32):
        return ctx.enter_context(nc.sbuf_tensor("c_sb_" + name, shape, dt))

    def sem(name):
        return nc.alloc_semaphore("c_" + name)

    ps = keep["ps"]
    parts_d = nc.dram_tensor("c_parts_d", (NB, 2, 3 * HD1, NH1 * S), BF16).ap()
    shift_d = nc.dram_tensor("c_shift_d", (NB, NSH, NH1 * S), BF16).ap()

    shT_ps = ps[:, 7, :].bitcast(BF16)[0:NSH * NH1, 0:S]

    wq = sb("wq", [P, P])
    wk = sb("wk", [P, P])
    wv = sb("wv", [P, P])
    rot = sb("rot", [P, NB])
    identb = sb("identb", [P, P], BF16)
    q32 = sb("q32", [P, 2, S])
    r32 = sb("r32", [P, 2, S])
    parts = sb("parts", [P, 2, 3, S], BF16)
    sq = sb("sq", [P, 2, NH1, S], BF16)
    sk = sb("sk", [P, 2, NH1, S], BF16)
    v_all = sb("v_all", [P, NT, P])
    v1 = sb("v1", [P, TPB, 4, 32])
    negmax = sb("negmax", [P, TPB, NH1])
    shr = sb("shr", [P, TPB, NH1])
    shp = sb("shp", [P, TPB, NSH, NH1], BF16)
    shT = sb("shT", [NSH * NH1, S], BF16)
    pT = sb("pT", [P, 4, TPB, S])
    oT = sb("oT", [P, S])
    rcp = sb("rcp", [P, TPB, 4])
    att = sb("att", [P, TPB, 4, HD1])
    x, xT, ident = keep["x"], keep["xT"], keep["ident"]

    w_ld = sem("w_ld")
    sq_zero = sem("sq_zero")
    sk_one = sem("sk_one")
    v1_init = sem("v1_init")
    v_mm = sem("v_mm")
    v_ev = sem("v_ev")
    qk_mm = sem("qk_mm")
    part_a = sem("part_a")
    part_b = sem("part_b")
    parts_st = [sem(f"parts_st{k}") for k in range(2)]
    stack_ld = sem("stack_ld")
    max_free = sem("max_free")
    max_mm = sem("max_mm")
    shift_step = sem("shift_step")
    shift_mm = sem("shift_mm")
    shift_ev = sem("shift_ev")
    shift_st = sem("shift_st")
    shift_ld = sem("shift_ld")
    exp_free = sem("exp_free")
    st_mm = sem("st_mm")
    v1_done = sem("v1_done")
    pv_mm = sem("pv_mm")
    oT_ev = sem("oT_ev")
    oT_mm = sem("oT_mm")
    rcp_done = sem("rcp_done")
    att_done = sem("att_done")
    x_add = sem("x_add")
    held = sem("held")
    NW = 5
    SCALE = HD1 ** -0.5
    norm = Norm(nc, ctx, keep, ps, [0, 1, 2, 3], x_add, [QUADS * (b + 1) for b in range(NB)], "cn_")

    block = ctx.enter_context(nc.Block())

    @block.sync
    def _(sp):
        for dst, src in ((wq[:, :], "c_wqT"), (wk[:, :], "c_wkT"), (wv[:, :], "c_wvT"), (rot[:, :], "c_rot"),
                         (identb[:, :], "identb")):
            sp.dma_start(dst, io[src]).then_inc(w_ld, 16)
        sp.wait_ge(sq_zero, 1)
        sp.wait_ge(sk_one, 1)
        for b in range(NB):
            for w in range(2):
                sp.wait_ge(part_b, 3 * (2 * b + w + 1))
                sp.dma_start(parts_d[b, w].rearrange("(a d) (h n) -> (d h) a n", a=3, h=NH1), parts[:, w, :, :]
                             ).then_inc(parts_st[w], 16)
        for w in range(2):
            sp.wait_ge(parts_st[w], 16 * NB)

        def stack(b):
            for a in range(3):
                for c in range(3):
                    r = (3 * a + c) * HD1
                    sp.dma_start(sq[r:r + HD1, bass.ds(b % 2, 1), :, :].rearrange("r a h n -> r (a h n)"),
                                 parts_d[bass.ds(b, 1), 0, a * HD1:(a + 1) * HD1, :].rearrange("b r n -> (b r) n")
                                 ).then_inc(stack_ld, 16)
                r = 3 * a * HD1
                sp.dma_start(sk[r:r + 3 * HD1, bass.ds(b % 2, 1), :, :].rearrange("r a h n -> r (a h n)"),
                             parts_d[bass.ds(b, 1), 1, :, :].rearrange("b r n -> (b r) n")).then_inc(stack_ld, 16)

        def shift(b):
            sp.wait_ge(shift_ev, b + 1)
            sp.sem_inc(held, 1)
            sp.dma_start(shift_d[bass.ds(b, 1)].rearrange("b a (h n) -> (b a h) n", h=NH1), shT[:, :]
                         ).then_inc(shift_st, 16)
            sp.wait_ge(shift_st, 16 * (b + 1))
            sp.sem_inc(held, 1)
            sp.dma_start(sq[KS:KS + NSH, bass.ds(b % 2, 1), :, :].rearrange("r a h n -> r (a h n)"),
                         shift_d[bass.ds(b, 1)].rearrange("b a n -> (b a) n")).then_inc(shift_ld, 16)

        stack(0)
        sp.wait_ge(stack_ld, 192)
        stack(1)
        shift(0)
        with sp.Fori(1, NB - 1) as b:
            shift(b)
            sp.wait_ge(pv_mm, QUADS * b)
            sp.sem_inc(held, 1)
            sp.wait_ge(stack_ld, 192 * (b + 1))
            sp.sem_inc(held, 1)
            stack(b + 1)
        shift(NB - 1)

    @block.gpsimd
    def _(pool):
        nc.gpsimd.memset(sk[:, :, :, :], 1.0).then_inc(sk_one, 1)
        nc.gpsimd.memset(v1[:, :, :, :], 0.0).then_inc(v1_init, 1)
        pool.wait_ge(v1_init, 1)
        nc.gpsimd.memset(v1[:, :, :, HD1:HD1 + 1], 1.0).then_inc(v1_init, 1)
        pool.wait_ge(v1_init, 2)
        pool.wait_ge(v_ev, NB)

        def values(m, t0, q):
            pool.wait_ge(pv_mm, m)
            nc.gpsimd.tensor_copy(v1[:, :, :, 0:HD1],
                                  v_all[:, bass.ds(t0, TPB), bass.ds(q * 4 * HD1, 4 * HD1)]
                                  .rearrange("p t (g d) -> p t g d", g=4)).then_inc(v1_done, 1)

        with pool.Fori(0, NB) as b:
            with pool.Fori(0, QUADS) as q:
                m = b * QUADS + q
                values(m, b * TPB, q)
                pool.wait_ge(att_done, m + 1)
                xs = x[:, bass.ds(b * TPB, TPB), bass.ds(q * 4 * HD1, 4 * HD1)]
                nc.gpsimd.tensor_tensor(xs, xs, att[:, :, :, :].rearrange("p t g d -> p t (g d)"), ALU.add
                                        ).then_inc(x_add, 1)
        norm.pool(pool)

    @block.scalar
    def _(act):
        act.wait_ge(w_ld, 16 * NW)
        nc.scalar.activation(oT[:, 0:1], rot[:, 0:1], ACT.Copy).then_inc(exp_free, 2)
        for b in range(NB):
            act.wait_ge(v_mm, b + 1)
            nc.scalar.activation(v_all[:, b * TPB:(b + 1) * TPB, :].rearrange("p t d -> p (t d)"), ps[:, 2 + b, :],
                                 ACT.Copy).then_inc(v_ev, 1)
        for n in range(2 * NB):
            b, w = n // 2, n % 2
            act.wait_ge(qk_mm, n + 1)
            if n >= 2:
                act.wait_ge(part_b, 3 * (n - 1))
                act.wait_ge(parts_st[w], 16 * b)
            nc.scalar.activation(q32[:, w, :], ps[:, w, :], ACT.Copy, scale=rot[:, b:b + 1]).then_inc(part_a, 1)
            act.wait_ge(part_a, 2 * n + 1)
            nc.scalar.activation(parts[:, w, 0, :], q32[:, w, :], ACT.Copy).then_inc(part_a, 1)

        def exps(b, q, g):
            u = b * NH1 + q * 4 + g
            for t in range(TPB):
                act.wait_ge(st_mm, u * TPB + t + 1)
                nc.scalar.activation(pT[:, g, t, :], ps[:, 4 + t % 2, :], ACT.Exp, scale=SCALE).then_inc(exp_free, 1)

        def turn_shift(b):
            act.wait_ge(shift_mm, b + 1)
            act.wait_ge(shift_st, 16 * b)
            nc.scalar.activation(shT[:, :], shT_ps, ACT.Copy).then_inc(shift_ev, 1)

        turn_shift(0)

        def batch(b, last):
            with act.Fori(0, QUADS) as q:
                m = b * QUADS + q
                for g in range(4):
                    exps(b, q, g)
                act.wait_ge(pv_mm, m + 1)
                nc.scalar.activation(oT[:, :], ps[:, 6, :], ACT.Copy).then_inc(oT_ev, 1)
            if not last:
                turn_shift(b + 1)

        with act.Fori(0, NB - 1) as b:
            batch(b, False)
        batch(NB - 1, True)
        norm.scalar(act)

    @block.vector
    def _(dve):
        nc.vector.memset(sq[:, :, :, :], 0.0).then_inc(sq_zero, 1)
        for n in range(2 * NB):
            b, w = n // 2, n % 2
            dve.wait_ge(part_a, 2 * n + 2)
            nc.vector.tensor_tensor(r32[:, w, :], q32[:, w, :], parts[:, w, 0, :], ALU.subtract).then_inc(part_b, 1)
            dve.wait_ge(part_b, 3 * n + 1)
            nc.vector.tensor_copy(parts[:, w, 1, :], r32[:, w, :]).then_inc(part_b, 1)
            dve.wait_ge(part_b, 3 * n + 2)
            nc.vector.tensor_tensor(parts[:, w, 2, :], r32[:, w, :], parts[:, w, 1, :], ALU.subtract
                                    ).then_inc(part_b, 1)
        nc.vector.memset(negmax[:, 0, 0:1], 0.0).then_inc(max_free, 2)

        def maxima(b, h):
            u = b * NH1 + h
            for i in range(2):
                dve.wait_ge(max_mm, 2 * u + i + 1)
                out = negmax[:, 2 * i:2 * i + 2, bass.ds(h, 1)].rearrange("p t a -> p (t a)")
                nc.vector.tensor_reduce(out, ps[:, 2 * i:2 * i + 2, :], AX.X, ALU.max, negate=True
                                        ).then_inc(max_free, 1)

        def shift(b):
            dve.wait_ge(max_free, 2 + 2 * NH1 * (b + 1))
            dve.wait_ge(shift_mm, b)
            nc.vector.tensor_copy(shp[:, :, 0, :], negmax[:, :, :]).then_inc(shift_step, 1)
            dve.wait_ge(shift_step, 4 * b + 1)
            nc.vector.tensor_tensor(shr[:, :, :], negmax[:, :, :], shp[:, :, 0, :], ALU.subtract
                                    ).then_inc(shift_step, 1)
            dve.wait_ge(shift_step, 4 * b + 2)
            nc.vector.tensor_copy(shp[:, :, 1, :], shr[:, :, :]).then_inc(shift_step, 1)
            dve.wait_ge(shift_step, 4 * b + 3)
            nc.vector.tensor_tensor(shp[:, :, 2, :], shr[:, :, :], shp[:, :, 1, :], ALU.subtract
                                    ).then_inc(shift_step, 1)

        with dve.Fori(0, NH1) as h:
            maxima(0, h)
        shift(0)

        def batch(b, last):
            with dve.Fori(0, QUADS) as q:
                m = b * QUADS + q
                if not last:
                    for g in range(4):
                        maxima(b + 1, q * 4 + g)
                dve.wait_ge(oT_mm, m + 1)
                dve.wait_ge(x_add, m)
                o4 = ps[:, 7, :].rearrange("p (t g c) -> p t g c", t=TPB, g=4)
                nc.vector.reciprocal(rcp[:, :, :], o4[:, :, :, HD1]).then_inc(rcp_done, 1)
                dve.wait_ge(rcp_done, m + 1)
                nc.vector.tensor_tensor(att[:, :, :, :], o4[:, :, :, 0:HD1],
                                        rcp[:, :, :, None].broadcast_to([P, TPB, 4, HD1]), ALU.mult
                                        ).then_inc(att_done, 1)
            if not last:
                shift(b + 1)

        with dve.Fori(0, NB - 1) as b:
            batch(b, False)
        batch(NB - 1, True)
        norm.vector(dve)

    @block.tensor
    def _(pe):
        pe.wait_ge(w_ld, 16 * NW)
        for b in range(NB):
            for t in range(TPB):
                ins = nc.tensor.matmul(ps[:, 2 + b, t * P:(t + 1) * P], xT[:, b, t * P:(t + 1) * P],
                                       wv[:, :], start=True, stop=True)
            ins.then_inc(v_mm, 1)
        for n in range(2 * NB):
            b, w = n // 2, n % 2
            if n >= 2:
                pe.wait_ge(part_a, 2 * (n - 1))
            nc.tensor.matmul(ps[:, w, :], (wq, wk)[w][:, :], xT[:, b, :], start=True, stop=True
                             ).then_inc(qk_mm, 1)

        def stacked(tile, b, h, rows, cols):
            return tile[0:rows, bass.ds(b % 2, 1), bass.ds(h, 1), cols].rearrange("r a h n -> r (a h n)")

        def max_scores(b, h):
            u = b * NH1 + h
            for i in range(TPB):
                if i % 2 == 0:
                    pe.wait_ge(max_free, 2 * u + i // 2 + 1)
                ins = nc.tensor.matmul(ps[:, i, :], stacked(sq, b, h, KS, slice(i * P, (i + 1) * P)),
                                       stacked(sk, b, h, KS, slice(0, S)), start=True, stop=True)
                if i % 2:
                    ins.then_inc(max_mm, 1)

        def exp_scores(b, h):
            u = b * NH1 + h
            for t in range(TPB):
                pe.wait_ge(exp_free, u * TPB + t + 1)
                nc.tensor.matmul(ps[:, 4 + t % 2, :], stacked(sk, b, h, P, slice(t * P, (t + 1) * P)),
                                 stacked(sq, b, h, P, slice(0, S)), start=True, stop=True).then_inc(st_mm, 1)

        def turn_shift(b):
            pe.wait_ge(shift_step, 4 * (b + 1))
            pe.wait_ge(att_done, QUADS * b)
            pe.sem_inc(held, 1)
            for i in range(TPB):
                ins = nc.tensor.transpose(shT_ps[:, i * P:(i + 1) * P],
                                          shp[:, i, :, :].rearrange("p a h -> p (a h)"), identb[:, :])
            ins.then_inc(shift_mm, 1)

        pe.wait_ge(stack_ld, 192)
        pe.wait_ge(part_a, 4 * NB)
        pe.wait_ge(v_ev, NB)
        with pe.Fori(0, NH1) as h:
            max_scores(0, h)
        turn_shift(0)

        def batch(b, last):
            with pe.Fori(0, QUADS) as q:
                m = b * QUADS + q
                if not last:
                    pe.wait_ge(stack_ld, 192 * (b + 2))
                pe.wait_ge(shift_ld, 16 * (b + 1))
                for g in range(4):
                    if not last:
                        max_scores(b + 1, q * 4 + g)
                    exp_scores(b, q * 4 + g)
                pe.wait_ge(v1_done, m + 1)
                pe.wait_ge(oT_ev, m)
                pe.wait_ge(exp_free, 2 + 4 * TPB * (m + 1))
                for t in range(TPB):
                    for g in range(4):
                        ins = nc.tensor.matmul(ps[32 * g:32 * g + 32, 6, :], v1[:, t, g, :], pT[:, g, t, :],
                                               start=(t == 0), stop=(t == TPB - 1), skip_group_check=True)
                ins.then_inc(pv_mm, 1)
                pe.wait_ge(oT_ev, m + 1)
                pe.wait_ge(att_done, m)
                pe.wait_ge(shift_ev, b + 1)
                for i in range(TPB):
                    ins = nc.tensor.transpose(ps[:, 7, i * P:(i + 1) * P], oT[:, i * P:(i + 1) * P], ident[:, :])
                ins.then_inc(oT_mm, 1)
            if not last:
                turn_shift(b + 1)

        with pe.Fori(0, NB - 1) as b:
            batch(b, False)
        batch(NB - 1, True)
        norm.tensor(pe)


LAYERS = 2
NH2 = 8
HD2 = 64
INNER = NH2 * HD2
WIN = 64
KEYS = P + WIN
HID = 341
HB = 3
HROWS = [P, P, HID - 2 * P]


def local_attention(nc, ctx, io, keep, layer):

    def keys(t):
        return slice(0 if t else WIN, KEYS)

    def sb(name, shape, dt=F32):
        return ctx.enter_context(nc.sbuf_tensor(f"l{layer}_sb_" + name, shape, dt))

    def sem(name):
        return nc.alloc_semaphore(f"l{layer}_" + name)

    ps = keep["ps"]
    o_ps = ps[:, 6, :]
    m_ps = ps[:, 7, :]

    wqkv = sb("wqkv", [P, 3, INNER])
    wo = sb("wo", [P, INNER // P, D])
    base_c = sb("base_c", [P, TPB, 2, HD2])
    base_s = sb("base_s", [P, TPB, 2, HD2])
    qks = sb("qks", [P, 2, HD2])
    tab_c = sb("tab_c", [P, TPB, 2, HD2])
    tab_s = sb("tab_s", [P, TPB, 2, HD2])
    wmask = sb("wmask", [P, 2, KEYS], BF16)
    identb = sb("identb", [P, P], BF16)
    hT = sb("hT", [P, P])
    qk_raw = sb("qk_raw", [P, 2, INNER])
    sqr = sb("sqr", [P, 2 * INNER])
    ssq = sb("ssq", [P, 2 * NH2])
    ssqc = sb("ssqc", [P, 2 * NH2])
    rn = sb("rn", [P, 2 * NH2])
    neg_half = sb("neg_half", [P, 2 * NH2])
    qk_c = sb("qk_c", [P, 2, INNER])
    qk_s = sb("qk_s", [P, 2, INNER])
    qk_r = sb("qk_r", [P, 2, INNER])
    qk_n = sb("qk_n", [P, 2, INNER])
    qT = sb("qT", [P, NH2 // 2, P])
    kT = sb("kT", [P, 2, NH2 // 2, KEYS])
    v = sb("v", [P, TPB, INNER])
    negmax = sb("negmax", [P, NH2])
    den = sb("den", [P, NH2])
    rden = sb("rden", [P, NH2])
    prob = sb("prob", [P, 4, 2 * P])
    probT = sb("probT", [P, 2, 2 * P])
    on = sb("on", [P, INNER])
    oT = sb("oT", [P, INNER])
    x, xT, ident = keep["x"], keep["xT"], keep["ident"]

    w_ld = sem("w_ld")
    inited = sem("inited")
    tab_done = sem("tab_done")
    held = sem("held")
    hT_done = sem("hT_done")
    qk_mm = sem("qk_mm")
    v_mm = sem("v_mm")
    v_ev = sem("v_ev")
    raw_done = sem("raw_done")
    sqr_done = sem("sqr_done")
    ssq_sum = sem("ssq_sum")
    ssq_done = sem("ssq_done")
    rn_step = sem("rn_step")
    rope_mul = sem("rope_mul")
    rope_add = sem("rope_add")
    qk_norm = sem("qk_norm")
    qkT_mm = sem("qkT_mm")
    qkT_ev = sem("qkT_ev")
    s_mm = sem("s_mm")
    max_done = sem("max_done")
    exp_done = sem("exp_done")
    pT_mm = sem("pT_mm")
    pT_ev0 = sem("pT_ev0")
    pT_ev1 = sem("pT_ev1")
    o_mm = sem("o_mm")
    recip = sem("recip")
    o_norm = sem("o_norm")
    oT_mm = sem("oT_mm")
    oT_ev = sem("oT_ev")
    y_mm = sem("y_mm")
    y_add = sem("y_add")
    NW = 8
    NU2 = NH2

    block = ctx.enter_context(nc.Block())

    @block.sync
    def _(sp):
        sp.dma_start(wqkv[:, :, :], io["wqkv"][layer]).then_inc(w_ld, 16)
        sp.dma_start(wo[:, :, :], io["l_wo"][layer]).then_inc(w_ld, 16)
        sp.dma_start(base_c[:, :, :, :], io["cos1"]).then_inc(w_ld, 16)
        sp.dma_start(base_s[:, :, :, :], io["sin1"]).then_inc(w_ld, 16)
        sp.dma_start(qks[:, 0, :], io["q_scale"][layer:layer + 1, :].broadcast_to([P, HD2])).then_inc(w_ld, 16)
        sp.dma_start(qks[:, 1, :], io["k_scale"][layer:layer + 1, :].broadcast_to([P, HD2])).then_inc(w_ld, 16)
        sp.dma_start(wmask[:, :, :], io["wmask"]).then_inc(w_ld, 16)
        sp.dma_start(identb[:, :], io["identb"]).then_inc(w_ld, 16)

    @block.gpsimd
    def _(pool):
        nc.gpsimd.memset(neg_half[:, :], -0.5).then_inc(inited, 1)
        nc.gpsimd.memset(prob[:, :, :], 0.0).then_inc(inited, 1)
        nc.gpsimd.memset(kT[:, :, :, :], 0.0).then_inc(inited, 1)
        nc.gpsimd.memset(v[:, :, :], 0.0).then_inc(inited, 1)
        nc.gpsimd.memset(keep["xT_pad"], 0.0).then_inc(inited, 1)
        pool.wait_ge(inited, 5)

        def shifted(n, t):
            b = n // TPB % NB
            pool.wait_ge(v_mm, n)
            pool.wait_ge(qk_norm, n)
            full = keep["xT_full"]
            nc.gpsimd.tensor_copy(hT[0:64, :], full[0:64, bass.ds(b, 1), bass.ds(t * P + 1, P)]
                                  .rearrange("p a n -> p (a n)")).then_inc(hT_done, 1)
            pool.wait_ge(hT_done, 2 * n + 1)
            nc.gpsimd.tensor_copy(hT[64:P, :], full[64:P, bass.ds(b, 1), bass.ds(t * P, P)]
                                  .rearrange("p a n -> p (a n)")).then_inc(hT_done, 1)

        def norms(n):
            pool.wait_ge(hT_done, 2 * n + 2)
            pool.wait_ge(ssq_done, n + 1)
            nc.gpsimd.tensor_tensor(rn[:, :], ssqc[:, :], neg_half[:, :], ALU.pow).then_inc(rn_step, 1)
            pool.wait_ge(rope_mul, n + 1)
            nc.gpsimd.tensor_tensor(qk_r[:, :, :], qk_c[:, :, :], qk_s[:, :, :], ALU.add).then_inc(rope_add, 1)
            pool.wait_ge(rope_add, n + 1)
            pool.wait_ge(rn_step, n + 1)
            pool.wait_ge(qkT_mm, 2 * n)
            nc.gpsimd.tensor_tensor(qk_n[:, :, :].rearrange("p w (h d) -> p (w h) d", d=HD2),
                                    qk_r[:, :, :].rearrange("p w (h d) -> p (w h) d", d=HD2),
                                    rn[:, :, None].broadcast_to([P, 2 * NH2, HD2]), ALU.mult).then_inc(qk_norm, 1)

        shifted(0, 0)
        norms(0)
        with pool.Fori(0, NB) as b:
            for t in range(TPB):
                shifted(TPB * b + t + 1, (t + 1) % TPB)
                norms(TPB * b + t + 1)

    @block.scalar
    def _(act):
        act.wait_ge(inited, 5)

        def start(n, t):
            act.wait_ge(qk_mm, n + 1)
            act.wait_ge(rope_mul, n)
            nc.scalar.activation(qk_raw[:, :, :], ps[:, 0:2, :], ACT.Copy).then_inc(raw_done, 1)
            act.wait_ge(raw_done, n + 1)
            act.wait_ge(ssq_sum, n)
            nc.scalar.activation(sqr[:, :], qk_raw[:, :, :].rearrange("p a n -> p (a n)"), ACT.Square
                                 ).then_inc(sqr_done, 1)
            act.wait_ge(v_mm, n + 1)
            nc.scalar.activation(v[:, t, :], m_ps, ACT.Copy
                                 ).then_inc(v_ev, 1)

        def qkT_evac(n, t):
            act.wait_ge(qkT_mm, 2 * n + 1)
            nc.scalar.activation(qT[:, :, :], ps[:, 0, :].rearrange("p (a n) -> p a n", n=P), ACT.Copy
                                 ).then_inc(qkT_ev, 1)
            act.wait_ge(qkT_mm, 2 * n + 2)
            k4 = ps[:, 1, :].rearrange("p (a n) -> p a n", n=P)
            nc.scalar.activation(kT[:, t % 2, :, WIN:KEYS], k4, ACT.Copy).then_inc(qkT_ev, 1)
            nc.scalar.activation(kT[:, (t + 1) % 2, :, 0:WIN], k4[:, :, P - WIN:P], ACT.Copy).then_inc(qkT_ev, 1)

        def pT_evac(n, t, u):
            act.wait_ge(pT_mm, NU2 * n + u + 1)
            c = slice(0 if t else P, 2 * P)
            nc.scalar.activation(probT[:, 1, c], ps[:, 5, c], ACT.Copy).then_inc(pT_ev1, 1)

        start(0, 0)
        qkT_evac(0, 0)
        with act.Fori(0, NB) as b:
            for t in range(TPB):
                n = TPB * b + t
                c = keys(t)
                for u in range(NU2):
                    act.wait_ge(max_done, NU2 * n + u + 1)
                    if u == 0:
                        act.wait_ge(recip, n)
                    nc.scalar.activation(prob[:, u % 4, WIN + c.start:2 * P], ps[:, 2 + u % 2, c], ACT.Exp,
                                         bias=negmax[:, u:u + 1], accum_out=den[:, u:u + 1]).then_inc(exp_done, 1)
                    if u == 0:
                        start(n + 1, (t + 1) % TPB)
                    if u in (2, 4, 6):
                        pT_evac(n, t, u - 1)
                pT_evac(n, t, 7)
                qkT_evac(n + 1, t + 1)
                act.wait_ge(oT_mm, n + 1)
                nc.scalar.activation(oT[:, :], m_ps, ACT.Copy).then_inc(oT_ev, 1)

    @block.vector
    def _(dve):
        dve.wait_ge(w_ld, 16 * NW)
        h = HD2 // 2
        nc.vector.tensor_tensor(tab_c[:, :, :, :], base_c[:, :, :, :],
                                qks[:, None, :, :].broadcast_to([P, TPB, 2, HD2]), ALU.mult).then_inc(tab_done, 1)
        for a in (0, h):
            nc.vector.tensor_tensor(tab_s[:, :, :, a:a + h], base_s[:, :, :, a:a + h],
                                    qks[:, None, :, h - a:2 * h - a].broadcast_to([P, TPB, 2, h]), ALU.mult
                                    ).then_inc(tab_done, 1)
        dve.wait_ge(tab_done, 3)

        def rope(n, t, part):
            g = qk_raw[:, :, :].rearrange("p w (g d) -> p w g d", d=HD2)

            def tab(tile, a, b):
                return tile[:, t, :, a:b][:, :, None, :]\
                    .broadcast_to([P, 2, NH2, b - a])

            if part == 0:
                dve.wait_ge(raw_done, n + 1)
                dve.wait_ge(rope_add, n)
                nc.vector.tensor_tensor(qk_c[:, :, :].rearrange("p w (g d) -> p w g d", d=HD2), g,
                                        tab(tab_c, 0, HD2), ALU.mult)
            elif part == 1:
                for a, last in ((0, False), (h, True)):
                    ins = nc.vector.tensor_tensor(
                        qk_s[:, :, :].rearrange("p w (g d) -> p w g d", d=HD2)[:, :, :, a:a + h],
                        g[:, :, :, h - a:2 * h - a], tab(tab_s, a, a + h), ALU.mult)
                ins.then_inc(rope_mul, 1)
            else:
                dve.wait_ge(sqr_done, n + 1)
                nc.vector.tensor_reduce(ssq[:, :], sqr[:, :].rearrange("p (g d) -> p g d", d=HD2), AX.X, ALU.add
                                        ).then_inc(ssq_sum, 1)
                dve.wait_ge(ssq_sum, n + 1)
                dve.wait_ge(rn_step, n)
                nc.vector.tensor_scalar(ssqc[:, :], ssq[:, :], 1e-24, None, ALU.max).then_inc(ssq_done, 1)

        def rowmax(n, t, u):
            dve.wait_ge(s_mm, NU2 * n + u + 1)
            nc.vector.tensor_reduce(negmax[:, u:u + 1], ps[:, 2 + u % 2, keys(t)], AX.X, ALU.max,
                                    negate=True).then_inc(max_done, 1)

        def pT_evac(n, t, u):
            dve.wait_ge(pT_mm, NU2 * n + u + 1)
            c = slice(0 if t else P, 2 * P)
            nc.vector.tensor_copy(probT[:, 0, c], ps[:, 4, c]).then_inc(pT_ev0, 1)

        for part in range(3):
            rope(0, 0, part)
        rowmax(0, 0, 0)
        rowmax(0, 0, 1)
        with dve.Fori(0, NB) as b:
            for t in range(TPB):
                n = TPB * b + t
                for k in range(4):
                    pT_evac(n, t, 2 * k)
                    if k < 3:
                        rowmax(n, t, 2 * k + 2)
                        rowmax(n, t, 2 * k + 3)
                        rope(n + 1, (t + 1) % TPB, k)
                dve.wait_ge(exp_done, NU2 * (n + 1))
                nc.vector.reciprocal(rden[:, :], den[:, :]).then_inc(recip, 1)
                dve.wait_ge(recip, n + 1)
                dve.wait_ge(o_mm, n + 1)
                dve.wait_ge(oT_mm, n)
                nc.vector.tensor_tensor(on[:, :].rearrange("p (u d) -> p u d", d=HD2),
                                        o_ps.rearrange("p (u d) -> p u d", d=HD2),
                                        rden[:, :, None].broadcast_to([P, NH2, HD2]), ALU.mult).then_inc(o_norm, 1)
                rowmax(n + 1, (t + 1) % TPB, 0)
                rowmax(n + 1, (t + 1) % TPB, 1)
                dve.wait_ge(y_mm, n + 1)
                xt = x[:, bass.ds(n, 1), :].rearrange("p a d -> p (a d)")
                nc.vector.tensor_tensor(xt, m_ps[:, 0:D], xt, ALU.add).then_inc(y_add, 1)

    @block.tensor
    def _(pe):
        pe.wait_ge(w_ld, 16 * NW)
        pe.wait_ge(inited, 5)

        def project(n):
            pe.wait_ge(hT_done, 2 * (n + 1))
            pe.wait_ge(qkT_ev, 3 * n)
            for w in range(2):
                ins = nc.tensor.matmul(ps[:, w, :], hT[:, :], wqkv[:, w, :], start=True, stop=True)
            ins.then_inc(qk_mm, 1)
            if not isinstance(n, int):
                pe.wait_ge(y_add, n - 1)
            nc.tensor.matmul(m_ps, hT[:, :], wqkv[:, 2, :], start=True, stop=True).then_inc(v_mm, 1)

        def turn_qk(n):
            pe.wait_ge(qk_norm, n + 1)
            for w in range(2):
                for a in range(4):
                    ins = nc.tensor.transpose(ps[:, w, a * P:(a + 1) * P], qk_n[:, w, a * P:(a + 1) * P],
                                              ident[:, :])
                ins.then_inc(qkT_mm, 1)

        def scores(n, t, u):
            if u == 0:
                pe.wait_ge(qkT_ev, 3 * n + 3)
            if not isinstance(n, int):
                pe.wait_ge(exp_done, NU2 * n + u - 1)
            r = slice(64 * (u % 2), 64 * (u % 2) + 64)
            c = keys(t)
            nc.tensor.matmul(ps[:, 2 + u % 2, c], qT[r, u // 2, :], kT[r, t % 2, u // 2, c], start=True,
                             stop=False, skip_group_check=True)
            nc.tensor.matmul(ps[:, 2 + u % 2, c], identb[:, :], wmask[:, 1 if t else 0, c],
                             start=False, stop=True, skip_group_check=True).then_inc(s_mm, 1)

        def turn_p(n, t, u):
            pe.wait_ge(exp_done, NU2 * n + u + 1)
            pe.wait_ge(pT_ev1 if u % 2 else pT_ev0, 4 * n + u // 2)
            for a in range(0 if t else 1, 2):
                ins = nc.tensor.transpose(ps[:, 4 + u % 2, a * P:(a + 1) * P], prob[:, u % 4, a * P:(a + 1) * P],
                                          ident[:, :])
            ins.then_inc(pT_mm, 1)

        def values(n, t, u):
            pe.wait_ge(pT_ev1 if u % 2 else pT_ev0, 4 * n + u // 2 + 1)
            if u == 0:
                pe.wait_ge(o_norm, n)
                pe.wait_ge(v_ev, n + 1)
            c = slice(HD2 * u, HD2 * u + HD2)
            ins = nc.tensor.matmul(o_ps[:, c], probT[:, u % 2, P:2 * P], v[:, t, c], start=True, stop=(t == 0))
            if t:
                ins = nc.tensor.matmul(o_ps[:, c], probT[64:P, u % 2, 0:P], v[64:P, t - 1, c],
                                       start=False, stop=True)
            if u == NU2 - 1:
                ins.then_inc(o_mm, 1)

        project(0)
        turn_qk(0)
        scores(0, 0, 0)
        scores(0, 0, 1)
        with pe.Fori(0, NB) as b:
            for t in range(TPB):
                n = TPB * b + t
                for u in range(NU2):
                    if u < 6:
                        scores(n, t, u + 2)
                    if u == 0:
                        project(n + 1)
                    if u == 6:
                        turn_qk(n + 1)
                    turn_p(n, t, u)
                    if u:
                        values(n, t, u - 1)
                scores(n + 1, (t + 1) % TPB, 0)
                values(n, t, 7)
                scores(n + 1, (t + 1) % TPB, 1)
                pe.wait_ge(o_norm, n + 1)
                pe.wait_ge(v_ev, n + 2)
                for a in range(4):
                    ins = nc.tensor.transpose(m_ps[:, a * P:(a + 1) * P], on[:, a * P:(a + 1) * P], ident[:, :])
                ins.then_inc(oT_mm, 1)
                pe.wait_ge(oT_ev, n + 1)
                for a in range(4):
                    ins = nc.tensor.matmul(m_ps[:, 0:D], oT[:, a * P:(a + 1) * P], wo[:, a, :],
                                           start=(a == 0), stop=(a == 3))
                ins.then_inc(y_mm, 1)


def gated_mlp(nc, ctx, io, keep, layer):

    def sb(name, shape, dt=F32):
        return ctx.enter_context(nc.sbuf_tensor(f"g{layer}_sb_" + name, shape, dt))

    def sem(name):
        return nc.alloc_semaphore(f"g{layer}_" + name)

    ps = keep["ps"]

    w1 = sb("w1", [P, 2, HID])
    w2 = sb("w2", [P, HB, D])
    b1 = sb("b1", [P, 2, HB])
    lgb = sb("lgb", [P, 2])
    hT = sb("hT", [P, S])
    stats = sb("stats", [P, NT, 6])
    mv = sb("mv", [P, NT, 2])
    var = sb("var", [P, NT])
    rstd = sb("rstd", [P, NT])
    eps = sb("eps", [P, TPB])
    neg_half = sb("neg_half", [P, TPB])
    hn = sb("hn", [P, TPB, D])
    hnT = sb("hnT", [P, 2, S])
    gl = sb("gl", [P, 2, S])
    hid = sb("hid", [P, 2, HB, S])
    x, xT, ident = keep["x"], keep["xT"], keep["ident"]

    w_ld = sem("w_ld")
    inited = sem("inited")
    x1_mm = sem("x1_mm")
    x1_ev = sem("x1_ev")
    h_mm = sem("h_mm")
    stats_done = sem("stats_done")
    mv_done = sem("mv_done")
    var_done = sem("var_done")
    rstd_done = sem("rstd_done")
    hn_done = sem("hn_done")
    hn_mm = sem("hn_mm")
    hn_ev = sem("hn_ev")
    g_mm = sem("g_mm")
    a_mm = sem("a_mm")
    gelu_done = sem("gelu_done")
    hid_done = sem("hid_done")
    y_mm = sem("y_mm")
    y_add = sem("y_add")
    x2_mm = sem("x2_mm")
    x2_ev = sem("x2_ev")
    NW = 6

    block = ctx.enter_context(nc.Block())

    @block.sync
    def _(sp):
        sp.dma_start(w1[:, :, :], io["l_w1"][layer]).then_inc(w_ld, 16)
        sp.dma_start(b1[:, :, :], io["l_b1"][layer]).then_inc(w_ld, 16)
        sp.dma_start(lgb[:, :], io["l_gb"][layer]).then_inc(w_ld, 16)
        for k in range(HB):
            r = HROWS[k] + (k == HB - 1)
            sp.dma_start(w2[0:r, k, :], io["l_w2"][layer, k * P:k * P + r, :]).then_inc(w_ld, 16)

    @block.gpsimd
    def _(pool):
        nc.gpsimd.memset(eps[:, :], EPS).then_inc(inited, 1)
        nc.gpsimd.memset(neg_half[:, :], -0.5).then_inc(inited, 1)
        nc.gpsimd.memset(hT[:, 0:1], 0.0).then_inc(inited, 1)
        nc.gpsimd.memset(hid[:, :, HB - 1, :], 1.0).then_inc(inited, 1)
        pool.wait_ge(inited, 4)
        for b in range(NB):
            t = slice(b * TPB, (b + 1) * TPB)
            pool.wait_ge(mv_done, b + 1)
            nc.gpsimd.tensor_tensor(var[:, t], mv[:, t, 1], eps[:, :], ALU.add).then_inc(var_done, 1)
            pool.wait_ge(var_done, b + 1)
            nc.gpsimd.tensor_tensor(rstd[:, t], var[:, t], neg_half[:, :], ALU.pow).then_inc(rstd_done, 1)

    @block.scalar
    def _(act):
        act.wait_ge(w_ld, 16 * NW)
        act.wait_ge(inited, 4)

        def front(b):
            act.wait_ge(x1_mm, b + 1)
            nc.scalar.activation(hT[0:64, :], ps[0:64, 0, :], ACT.Copy).then_inc(x1_ev, 1)
            nc.scalar.activation(hT[64:P, 1:S], ps[64:P, 0, 0:S - 1], ACT.Copy).then_inc(x1_ev, 1)
            act.wait_ge(hn_mm, b + 1)
            nc.scalar.activation(hnT[:, b % 2, :], ps[:, 2, :], ACT.Identity, scale=lgb[:, 0:1], bias=lgb[:, 1:2]
                                 ).then_inc(hn_ev, 1)

        front(0)
        for b in range(NB):
            for k in range(HB):
                r = HROWS[k]
                n = b * HB + k
                act.wait_ge(g_mm, n + 1)
                if n >= 2:
                    act.wait_ge(hid_done, n - 1)
                nc.scalar.activation(gl[0:r, n % 2, :], ps[0:r, 3 + n % 2, :], ACT.Gelu, bias=b1[0:r, 1, k:k + 1]
                                     ).then_inc(gelu_done, 1)
            if b + 1 < NB:
                front(b + 1)
            act.wait_ge(x2_mm, b + 1)
            nc.scalar.activation(xT[:, b, :], ps[:, 7, :], ACT.Copy).then_inc(x2_ev, 1)

    @block.vector
    def _(dve):
        dve.wait_ge(w_ld, 16 * NW)
        dve.wait_ge(inited, 4)

        def front(b):
            dve.wait_ge(h_mm, b + 1)
            for t in range(TPB):
                nc.vector.bn_stats(stats[:, b * TPB + t, :], ps[:, 1, t * P:(t + 1) * P]).then_inc(stats_done, 1)
            dve.wait_ge(stats_done, TPB * (b + 1))
            for t in range(TPB):
                ins = nc.vector.bn_aggr(mv[:, b * TPB + t, :], stats[:, b * TPB + t, :])
            ins.then_inc(mv_done, 1)
            dve.wait_ge(rstd_done, b + 1)
            if b:
                dve.wait_ge(hn_mm, b)
            for t in range(TPB):
                n = b * TPB + t
                ins = nc.vector.tensor_scalar(hn[:, t, :], ps[:, 1, t * P:(t + 1) * P], mv[:, n, 0:1],
                                              rstd[:, n:n + 1], ALU.subtract, ALU.mult)
            ins.then_inc(hn_done, 1)

        front(0)
        for b in range(NB):
            for k in range(HB):
                r = HROWS[k]
                n = b * HB + k
                dve.wait_ge(gelu_done, n + 1)
                dve.wait_ge(a_mm, n + 1)
                if k == 0 and b >= 2:
                    dve.wait_ge(y_mm, b - 1)
                nc.vector.scalar_tensor_tensor(hid[0:r, b % 2, k, :], ps[0:r, 5 + n % 2, :], b1[0:r, 0, k:k + 1],
                                               gl[0:r, n % 2, :], ALU.add, ALU.mult).then_inc(hid_done, 1)
            if b + 1 < NB:
                front(b + 1)
            dve.wait_ge(y_mm, b + 1)
            ts = slice(b * TPB, (b + 1) * TPB)
            nc.vector.tensor_tensor(x[:, ts, :], ps[:, 7, :].rearrange("p (t d) -> p t d", d=D), x[:, ts, :],
                                    ALU.add).then_inc(y_add, 1)

    @block.tensor
    def _(pe):
        pe.wait_ge(w_ld, 16 * NW)

        def turn(bank, src, done):
            for t in range(TPB):
                ins = nc.tensor.transpose(ps[:, bank, t * P:(t + 1) * P], src(t), ident[:, :])
            ins.then_inc(done, 1)

        def front_a(b):
            if b:
                pe.wait_ge(x1_ev, 2 * b)
            turn(0, lambda t: x[:, b * TPB + t, :], x1_mm)
            pe.wait_ge(x1_ev, 2 * (b + 1))
            pe.wait_ge(inited, 3)
            if b:
                pe.wait_ge(hn_done, b)
            turn(1, lambda t: hT[:, t * P:(t + 1) * P], h_mm)

        def front_b(b):
            pe.wait_ge(hn_done, b + 1)
            if b:
                pe.wait_ge(hn_ev, b)
            turn(2, lambda t: hn[:, t, :], hn_mm)

        def up(b):
            for k in range(HB):
                r = HROWS[k]
                n = b * HB + k
                if k == 0:
                    pe.wait_ge(hn_ev, b + 1)
                if n >= 2:
                    pe.wait_ge(gelu_done, n - 1)
                nc.tensor.matmul(ps[0:r, 3 + n % 2, :], w1[:, 1, k * P:k * P + r], hnT[:, b % 2, :],
                                 start=True, stop=True).then_inc(g_mm, 1)
                if n >= 2:
                    pe.wait_ge(hid_done, n - 1)
                nc.tensor.matmul(ps[0:r, 5 + n % 2, :], w1[:, 0, k * P:k * P + r], hnT[:, b % 2, :],
                                 start=True, stop=True).then_inc(a_mm, 1)

        def down(b):
            pe.wait_ge(hid_done, HB * (b + 1))
            if b:
                pe.wait_ge(x2_ev, b)
            for t in range(TPB):
                for k in range(HB):
                    r = HROWS[k] + (k == HB - 1)
                    ins = nc.tensor.matmul(ps[:, 7, t * P:(t + 1) * P], hid[0:r, b % 2, k, t * P:(t + 1) * P],
                                           w2[0:r, k, :], start=(k == 0), stop=(k == HB - 1))
            ins.then_inc(y_mm, 1)

        front_a(0)
        front_b(0)
        for b in range(NB):
            up(b)
            if b + 1 < NB:
                front_a(b + 1)
            down(b)
            if b + 1 < NB:
                front_b(b + 1)
            pe.wait_ge(y_add, b + 1)
            turn(7, lambda t: x[:, b * TPB + t, :], x2_mm)


def save_x(nc, ctx, keep):
    saved = nc.alloc_semaphore("x3_saved")
    block = ctx.enter_context(nc.Block())

    @block.vector
    def _(dve):
        nc.vector.tensor_copy(keep["x3"][:, :, :], keep["x"][:, :, :]).then_inc(saved, 1)


def finish(nc, ctx, keep, out):
    ps = keep["ps"]
    summed = nc.alloc_semaphore("f_summed")
    stored = nc.alloc_semaphore("f_stored")
    norm = Norm(nc, ctx, keep, ps, [0, 1, 2, 3], summed, [1, 2, 3, 4], "fn_")
    block = ctx.enter_context(nc.Block())
    x, x3 = keep["x"], keep["x3"]

    @block.gpsimd
    def _(pool):
        norm.pool(pool)

    @block.vector
    def _(dve):
        for b in range(NB):
            ts = slice(b * TPB, (b + 1) * TPB)
            nc.vector.tensor_tensor(x[:, ts, :], x[:, ts, :], x3[:, ts, :], ALU.add).then_inc(summed, 1)
        norm.vector(dve)

    @block.sync
    def _(sp):
        for b in range(NB):
            ts = slice(b * TPB, (b + 1) * TPB)
            sp.wait_ge(norm.norm_done, b + 1)
            sp.dma_start(out[b].rearrange("(t p) d -> p t d", p=P), x[:, ts, :]).then_inc(stored, 16)
        sp.wait_ge(stored, 16 * NB)


def program(nc, io, out):
    with ExitStack() as ctx:
        def tile(name, shape):
            return ctx.enter_context(nc.sbuf_tensor("keep_" + name, shape, F32))

        ps = ctx.enter_context(nc.psum_tensor("ps", [P, 8, 512], F32))
        xT_full = tile("xT", [P, NB, S + 1])
        keep = dict(ps=ps, x=tile("x", [P, NT, D]), logits=tile("logits", [P, NT, NE]), ident=tile("ident", [P, P]),
                    x3=tile("x3", [P, NT, D]), xT_full=xT_full, xT=xT_full[:, :, 1:S + 1],
                    xT_pad=xT_full[:, :, 0:1])
        for phase in (attention0, experts0, attention1):
            with nc.cleanup_on_exit(), ExitStack() as inner:
                phase(nc, inner, io, keep)
        with nc.cleanup_on_exit(), ExitStack() as inner:
            save_x(nc, inner, keep)
        for layer in range(LAYERS):
            for phase in (local_attention, gated_mlp):
                with nc.cleanup_on_exit(), ExitStack() as inner:
                    phase(nc, inner, io, keep, layer)
        with nc.cleanup_on_exit(), ExitStack() as inner:
            finish(nc, inner, keep, out)


def rotary(length, width):
    f32 = np.float32
    inv = f32(1.0) / f32(10000.0) ** (np.arange(0, width, 2, dtype=f32) / f32(width))
    angle = np.arange(length, dtype=f32)[:, None] * inv[None, :].astype(f32)
    angle = np.concatenate([angle, angle], 1)
    return np.cos(angle).astype(f32), np.sin(angle).astype(f32)


def shape_constants():
    f32 = np.float32
    bf16 = mybir.dt.np(BF16)
    c = {}
    c["ident"] = np.eye(P, dtype=f32)
    c["identb"] = np.eye(P).astype(bf16)
    c["iota"] = np.tile(np.arange(NE, dtype=f32), (P, 1))
    c["cmask"] = np.where(np.arange(P)[None, :] > np.arange(P)[:, None], -1e30, 0).astype(bf16)
    cos, sin = rotary(S, HD0)
    first = np.where(np.arange(HD0) < HD0 // 2, -1, 1).astype(f32)
    c["cos0"], c["sin0"] = cos, sin * first
    cos, sin = rotary(NB, 8)
    c["c_rot"] = np.repeat(np.concatenate([(cos + sin)[:, :4], (cos - sin)[:, 4:]], 1).T, 16, 0).astype(f32)
    cos, sin = rotary(S, HD2)
    half = np.arange(0, HD2, 2, dtype=f32)
    base = (half + f32(0.4 * HD2)) / f32(1.4 * HD2)
    power = (np.arange(S, dtype=f32) - S // 2) / f32(WIN // 2)
    scale = (base[None, :] ** power[:, None]).astype(f32)
    scale = np.concatenate([scale, scale], 1)
    c["cos1"] = np.stack([8 * cos * scale, cos / scale], 1).reshape(TPB, P, 2, HD2).transpose(1, 0, 2, 3)
    c["sin1"] = np.stack([8 * sin * scale * first, sin / scale * first], 1)\
        .reshape(TPB, P, 2, HD2).transpose(1, 0, 2, 3)
    key, query = np.arange(KEYS)[None, :], np.arange(P)[:, None]
    seen = (key >= query) & (key <= query + WIN)
    c["wmask"] = np.where(np.stack([seen & (key >= WIN), seen], 1), 0, -1e30).astype(bf16)
    return c


def layouts(i):
    a = {}
    x = i["L0_attn_x"]
    a["x"] = x.reshape(NT, P, D).transpose(1, 0, 2)
    a["xT"] = x.reshape(NB * S, D).T
    a["wd"] = i["L0_attn_w_kv_down"]
    a["wdT"] = i["L0_attn_w_kv_down"].T
    a["wkT"] = i["L0_attn_w_k_up"].T
    a["wqT"] = i["L0_attn_wq"].T
    a["wv"] = i["L0_attn_w_v_up"]
    a["woT"] = i["L0_attn_wo"].T
    a["keysT"] = i["L0_ffn_keys"].T
    a["rwT"] = i["L0_ffn_rw"].T
    a["rb"] = i["L0_ffn_rb"].reshape(1, NE)
    a["w1T"] = np.concatenate([i["L0_ffn_w1"].transpose(2, 0, 1),
                               i["L0_ffn_b1"].reshape(NE, FB, P).transpose(2, 0, 1)], 2)
    a["w2T"] = i["L0_ffn_w2"].reshape(NE, D, FB, P).transpose(3, 0, 2, 1).reshape(P, NE * FB, D)
    a["b2"] = i["L0_ffn_b2"]
    order = (np.arange(16)[None, :] * 8 + np.arange(8)[:, None]).reshape(-1)
    a["c_wqT"] = i["L1_attn_Wq"][order].T
    a["c_wkT"] = i["L1_attn_Wk"][order].T
    a["c_wvT"] = i["L1_attn_Wv"].T
    a["wqkv"] = i["L1_ffn_wqkv"].reshape(LAYERS, D, 3, INNER)
    a["l_wo"] = i["L1_ffn_wo"].reshape(LAYERS, INNER // P, P, D).transpose(0, 2, 1, 3)
    a["q_scale"], a["k_scale"] = i["L1_ffn_q_scale"], i["L1_ffn_k_scale"]
    a["l_w1"] = i["L1_ffn_w1"].reshape(LAYERS, D, 2, HID)
    b1 = np.zeros((LAYERS, 2, HB * P), np.float32)
    b1[:, :, :HID] = i["L1_ffn_b1"].reshape(LAYERS, 2, HID)
    a["l_b1"] = b1.reshape(LAYERS, 2, HB, P).transpose(0, 3, 1, 2)
    a["l_gb"] = np.stack([i["L1_ffn_ln_g"], i["L1_ffn_ln_b"]], -1)
    a["l_w2"] = np.concatenate([i["L1_ffn_w2"], i["L1_ffn_b2"][:, None, :]], 1)
    return a


def kernel(**inputs):
    import concourse.bacc as bacc
    from concourse.bass_utils import run_bass_kernel_spmd

    inputs = {name: np.asarray(a) for name, a in inputs.items()}
    arrays = {**shape_constants(), **layouts(inputs)}
    arrays = {name: np.ascontiguousarray(a) for name, a in arrays.items()}
    nc = bacc.Bacc("TRN2", target_bir_lowering=False, num_devices=1)
    io = {name: nc.dram_tensor(name, a.shape, mybir.dt.from_np(a.dtype), kind="ExternalInput").ap()
          for name, a in arrays.items()}
    out = nc.dram_tensor("out", (NB, S, D), F32, kind="ExternalOutput").ap()
    program(nc, io, out)
    result = run_bass_kernel_spmd(nc, [arrays], core_ids=[0])
    return result.results[0]["out"]
```

```python
from contextlib import ExitStack

import numpy as np

import concourse.bass as bass
from concourse import mybir

ALU = mybir.AluOpType
ACT = mybir.ActivationFunctionType
AX = mybir.AxisListType
F32 = mybir.dt.float32
BF16 = mybir.dt.bfloat16

P = 128
NB = 4
S = 512
D = 128
TPB = S // P
NT = NB * TPB
EPS = 1e-5

HD0 = 64
NP0 = 8
LAT = 64
UNITS = [(i, j) for i in reversed(range(TPB)) for j in range(2)]
NU = len(UNITS)

NE = 16
FF = 512
FB = FF // P
TOPK = 4


class Norm:

    def __init__(self, nc, ctx, keep, ps, banks, ready, counts, prefix):
        def sb(name, shape):
            return ctx.enter_context(nc.sbuf_tensor(prefix + name, shape, F32))

        def sem(name):
            return nc.alloc_semaphore(prefix + name)

        self.nc, self.keep, self.ps, self.banks, self.ready, self.counts = nc, keep, ps, banks, ready, counts
        self.stats = sb("stats", [P, NT, 6])
        self.mv = sb("mv", [P, NT, 2])
        self.var = sb("var", [P, NT])
        self.rstd = sb("rstd", [P, NT])
        self.eps = sb("eps", [P, TPB])
        self.neg_half = sb("neg_half", [P, TPB])
        self.consts = sem("consts")
        self.stats_done = sem("stats_done")
        self.mv_done = sem("mv_done")
        self.var_done = sem("var_done")
        self.rstd_done = sem("rstd_done")
        self.norm_done = sem("norm_done")
        self.turn_mm = sem("turn_mm")
        self.turn_ev = sem("turn_ev")

    def pool(self, pool):
        nc = self.nc
        nc.gpsimd.memset(self.eps[:, :], EPS).then_inc(self.consts, 1)
        nc.gpsimd.memset(self.neg_half[:, :], -0.5).then_inc(self.consts, 1)
        pool.wait_ge(self.consts, 2)
        for b in range(NB):
            t = slice(b * TPB, (b + 1) * TPB)
            pool.wait_ge(self.mv_done, b + 1)
            nc.gpsimd.tensor_tensor(self.var[:, t], self.mv[:, t, 1], self.eps[:, :], ALU.add
                                    ).then_inc(self.var_done, 1)
            pool.wait_ge(self.var_done, b + 1)
            nc.gpsimd.tensor_tensor(self.rstd[:, t], self.var[:, t], self.neg_half[:, :], ALU.pow
                                    ).then_inc(self.rstd_done, 1)

    def vector(self, dve):
        nc, x = self.nc, self.keep["x"]

        def moments(b):
            dve.wait_ge(self.ready, self.counts[b])
            for t in range(b * TPB, (b + 1) * TPB):
                nc.vector.bn_stats(self.stats[:, t, :], x[:, t, :]).then_inc(self.stats_done, 1)
            dve.wait_ge(self.stats_done, TPB * (b + 1))
            for t in range(b * TPB, (b + 1) * TPB):
                ins = nc.vector.bn_aggr(self.mv[:, t, :], self.stats[:, t, :])
            ins.then_inc(self.mv_done, 1)

        def normalise(b):
            dve.wait_ge(self.rstd_done, b + 1)
            for t in range(b * TPB, (b + 1) * TPB):
                ins = nc.vector.tensor_scalar(x[:, t, :], x[:, t, :], self.mv[:, t, 0:1], self.rstd[:, t:t + 1],
                                              ALU.subtract, ALU.mult)
            ins.then_inc(self.norm_done, 1)

        moments(0)
        for b in range(NB):
            if b + 1 < NB:
                moments(b + 1)
            normalise(b)

    def tensor(self, pe):
        for b in range(NB):
            pe.wait_ge(self.norm_done, b + 1)
            for t in range(TPB):
                ins = self.nc.tensor.transpose(self.ps[:, self.banks[b], t * P:(t + 1) * P],
                                               self.keep["x"][:, b * TPB + t, :], self.keep["ident"][:, :])
            ins.then_inc(self.turn_mm, 1)

    def scalar(self, act):
        for b in range(NB):
            act.wait_ge(self.turn_mm, b + 1)
            self.nc.scalar.activation(self.keep["xT"][:, b, :], self.ps[:, self.banks[b], :],
                                      ACT.Copy).then_inc(self.turn_ev, 1)


def wait_past(eng, sem, count):
    if not isinstance(count, int) or count > 0:
        eng.wait_ge(sem, count)


def attention0(nc, ctx, io, keep):

    def sb(name, shape, dt=F32):
        return ctx.enter_context(nc.sbuf_tensor("a_" + name, shape, dt))

    def sem(name):
        return nc.alloc_semaphore("a_" + name)

    ps = keep["ps"]
    qk_ps = ps[:, 0:2, :].rearrange("p a (t c) -> p (a t) c", c=256)
    o_ps = ps[:, 6, :]
    m_ps = ps[:, 7, :]

    wqk = sb("wqk", [P, NP0, 256])
    wvo = sb("wvo", [P, NP0, P])
    wkT = sb("wkT", [LAT, NP0 * P])
    wd = sb("wd", [LAT, P])
    wdT = sb("wdT", [P, LAT])
    wv = sb("wv", [P, NP0, LAT])
    woT = sb("woT", [P, NP0, P])
    cos = sb("cos", [P, TPB, HD0])
    sin = sb("sin", [P, TPB, HD0])
    cmask = sb("cmask", [P, P], BF16)
    identb = sb("identb", [P, P], BF16)
    lat = sb("lat", [P, NT, LAT])
    qk_c = sb("qk_c", [P, TPB, 256])
    qk_s = sb("qk_s", [P, TPB, 256])
    qk_r = sb("qk_r", [P, TPB, 256])
    qkT = sb("qkT", [P, 2, 2, S])
    negmax = sb("negmax", [P, NU])
    den = sb("den", [P, 2, NU])
    rden = sb("rden", [P, NU])
    prob = sb("prob", [P, 4, S])
    probT = sb("probT", [P, 2, S])
    on = sb("on", [P, TPB, P])
    oT = sb("oT", [P, S])
    keysT = sb("keysT", [P, NE])
    rwT = sb("rwT", [P, NE])
    router = sb("router", [P, NE])
    keys2 = sb("keys2", [P, NE])
    rbrow = sb("rbrow", [1, NE])
    rbias = sb("rbias", [1, NE])
    ones = sb("ones", [P, P])
    x, xT, ident = keep["x"], keep["xT"], keep["ident"]

    w_ld = sem("w_ld")
    o_ld = sem("o_ld")
    set_mm = sem("set_mm")
    set_ev = sem("set_ev")
    ones_set = sem("ones_set")
    wq_scaled = sem("wq_scaled")
    rt1 = sem("rt1")
    lat_mm = sem("lat_mm")
    lat_ev = sem("lat_ev")
    qk_mm = sem("qk_mm")
    rope_mul = sem("rope_mul")
    rope_add = sem("rope_add")
    qkT_mm = sem("qkT_mm")
    qkT_ev = sem("qkT_ev")
    s_mm = sem("s_mm")
    max_done = sem("max_done")
    exp_done = sem("exp_done")
    pT_mm = sem("pT_mm")
    pT_ev = [sem(f"pT_ev{j}") for j in range(2)]
    o_mm = sem("o_mm")
    recip = sem("recip")
    o_norm = sem("o_norm")
    oT_mm = sem("oT_mm")
    oT_ev = sem("oT_ev")
    y_mm = sem("y_mm")
    y_add = sem("y_add")
    lg_mm = sem("lg_mm")
    lg_ev = sem("lg_ev")

    NWEIGHTS = 10
    NLATER = 5
    NI = NP0 * NB
    SCALE = HD0 ** -0.5
    norm = Norm(nc, ctx, keep, ps, [0, 1, 2, 3], y_add, [NI - NB + b + 1 for b in range(NB)], "an_")

    block = ctx.enter_context(nc.Block())

    def each(eng, step):
        for b in range(NB):
            step(b, b)
        with eng.Fori(1, NP0) as h:
            for b in range(NB):
                step(h * NB + b, b)

    @block.sync
    def _(sp):
        def load(dst, src):
            sp.dma_start(dst, src).then_inc(w_ld, 16)

        def load_later(dst, src):
            sp.dma_start(dst, src).then_inc(o_ld, 16)

        load(wd[:, :], io["wd"])
        load(wkT[:, :], io["wkT"])
        load(wqk[:, :, 0:P], io["wqT"].rearrange("c (h n) -> c h n", h=NP0))
        load(xT, io["xT"].rearrange("c (b n) -> c b n", b=NB))
        load(wdT[:, :], io["wdT"])
        load(cos[:, :, :], io["cos0"].rearrange("(t p) d -> p t d", p=P))
        load(sin[:, :, :], io["sin0"].rearrange("(t p) d -> p t d", p=P))
        load(cmask[:, :], io["cmask"])
        load(identb[:, :], io["identb"])
        load(ident[:, :], io["ident"])
        load_later(wv[:, :, :], io["wv"].rearrange("(h q) l -> q h l", q=P))
        load_later(woT[:, :, :], io["woT"].rearrange("(h q) n -> q h n", q=P))
        load_later(x[:, :, :], io["x"])
        load_later(keysT[:, :], io["keysT"])
        load_later(rwT[:, :], io["rwT"])
        load_later(rbrow[:, :], io["rb"])

    @block.gpsimd
    def _(pool):
        nc.gpsimd.memset(ones[:, :], 1.0).then_inc(ones_set, 1)

        def rope_sum(n):
            pool.wait_ge(rope_mul, n + 1)
            wait_past(pool, qkT_mm, 2 * n)
            nc.gpsimd.tensor_tensor(qk_r[:, :, :], qk_c[:, :, :], qk_s[:, :, :], ALU.add).then_inc(rope_add, 1)

        rope_sum(0)
        each(pool, lambda n, b: rope_sum(n + 1))
        norm.pool(pool)

    @block.scalar
    def _(act):
        act.wait_ge(set_mm, 1)
        nc.scalar.activation(wqk[:, :, P:2 * P], ps[:, 0:2, :].rearrange("p a (h n) -> p (a h) n", n=P),
                             ACT.Copy).then_inc(set_ev, 1)
        act.wait_ge(lat_mm, 1)
        nc.scalar.activation(lat[:, :, :], ps[:, 4:6, :].rearrange("p a (t l) -> p (a t) l", l=LAT), ACT.Copy
                             ).then_inc(lat_ev, 1)

        def copy_qkT(n, b):
            for w in range(2):
                act.wait_ge(qkT_mm, 2 * n + w + 1)
                nc.scalar.activation(qkT[:, b % 2, w, :], ps[:, w, :], ACT.Copy).then_inc(qkT_ev, 1)

        def copy_pT(n, u):
            i = UNITS[u][0]
            act.wait_ge(pT_mm, NU * n + u + 1)
            nc.scalar.activation(probT[:, 1, 0:(i + 1) * P], ps[:, 5, 0:(i + 1) * P], ACT.Copy).then_inc(pT_ev[1], 1)

        def exp(n, b, u):
            i, j = UNITS[u]
            m = (i + 1) * P
            act.wait_ge(max_done, NU * n + u + 1)
            if u == 0:
                wait_past(act, recip, n - 1)
            nc.scalar.activation(prob[:, u % 4, 0:m], ps[:, 2 + j, 0:m], ACT.Exp, bias=negmax[:, u:u + 1],
                                 accum_out=den[:, b % 2, 2 * i + j:2 * i + j + 1]).then_inc(exp_done, 1)

        def copy_oT(n):
            act.wait_ge(oT_mm, n + 1)
            wait_past(act, y_mm, n)
            nc.scalar.activation(oT[:, :], m_ps, ACT.Copy).then_inc(oT_ev, 1)

        copy_qkT(0, 0)
        exp(0, 0, 0)
        exp(0, 0, 1)
        act.wait_ge(set_mm, 2)
        nc.scalar.activation(wvo[:, :, :], ps[:, 6:8, :].rearrange("p a (h n) -> p (a h) n", n=P),
                             ACT.Copy).then_inc(set_ev, 1)

        def step(n, b):
            copy_pT(n, 1)
            exp(n, b, 2)
            exp(n, b, 3)
            if not isinstance(n, int) or n > 0:
                copy_oT(n - 1)
            copy_pT(n, 3)
            exp(n, b, 4)
            exp(n, b, 5)
            copy_pT(n, 5)
            exp(n, b, 6)
            copy_qkT(n + 1, b + 1)
            exp(n, b, 7)
            copy_pT(n, 7)
            exp(n + 1, b + 1, 0)
            exp(n + 1, b + 1, 1)

        each(act, step)
        copy_oT(NI - 1)
        norm.scalar(act)

    @block.vector
    def _(dve):
        dve.wait_ge(w_ld, 16 * NWEIGHTS)
        nc.vector.tensor_scalar(wqk[:, :, 0:P], wqk[:, :, 0:P], SCALE, None, ALU.mult).then_inc(wq_scaled, 1)

        def rope_c(n):
            dve.wait_ge(qk_mm, n + 1)
            wait_past(dve, rope_add, n)
            nc.vector.tensor_tensor(qk_c[:, :, :].rearrange("p t (g d) -> p t g d", d=HD0),
                                    qk_ps.rearrange("p t (g d) -> p t g d", d=HD0),
                                    cos[:, :, None, :].broadcast_to([P, TPB, 4, HD0]), ALU.mult)

        def rope_s(n):
            h = HD0 // 2
            for a in (0, h):
                ins = nc.vector.tensor_tensor(
                    qk_s[:, :, :].rearrange("p t (g d) -> p t g d", d=HD0)[:, :, :, a:a + h],
                    qk_ps.rearrange("p t (g d) -> p t g d", d=HD0)[:, :, :, h - a:2 * h - a],
                    sin[:, :, None, a:a + h].broadcast_to([P, TPB, 4, h]), ALU.mult)
            ins.then_inc(rope_mul, 1)

        def rowmax(n, u):
            i, j = UNITS[u]
            dve.wait_ge(s_mm, NU * n + u + 1)
            nc.vector.tensor_reduce(negmax[:, u:u + 1], ps[:, 2 + j, 0:(i + 1) * P], AX.X, ALU.max,
                                    negate=True).then_inc(max_done, 1)

        def copy_pT(n, u):
            i = UNITS[u][0]
            dve.wait_ge(pT_mm, NU * n + u + 1)
            nc.vector.tensor_copy(probT[:, 0, 0:(i + 1) * P], ps[:, 4, 0:(i + 1) * P]).then_inc(pT_ev[0], 1)

        def normalise(n, b):
            dve.wait_ge(exp_done, NU * (n + 1))
            nc.vector.reciprocal(rden[:, :], den[:, b % 2, :]).then_inc(recip, 1)
            dve.wait_ge(recip, n + 1)
            dve.wait_ge(o_mm, n + 1)
            wait_past(dve, oT_mm, n)
            nc.vector.tensor_tensor(on[:, :, :].rearrange("p t (j d) -> p (t j) d", j=2),
                                    o_ps.rearrange("p (u d) -> p u d", u=NU),
                                    rden[:, :, None].broadcast_to([P, NU, LAT]), ALU.mult).then_inc(o_norm, 1)

        def add_y(n, b):
            dve.wait_ge(y_mm, n + 1)
            wait_past(dve, y_add, n - NB + 1)
            ts = slice(b * TPB, (b + 1) * TPB)
            nc.vector.tensor_tensor(x[:, ts, :], m_ps.rearrange("p (t d) -> p t d", d=D), x[:, ts, :],
                                    ALU.add).then_inc(y_add, 1)

        rope_c(0)
        rope_s(0)
        rowmax(0, 0)
        rowmax(0, 1)
        copy_pT(0, 0)
        dve.wait_ge(o_ld, 16 * (NLATER + 1))

        def step(n, b):
            rowmax(n, 2)
            rope_c(n + 1)
            rowmax(n, 3)
            copy_pT(n, 2)
            rope_s(n + 1)
            rowmax(n, 4)
            rowmax(n, 5)
            copy_pT(n, 4)
            if not isinstance(n, int) or n > 0:
                add_y(n - 1, (b - 1) % NB)
            rowmax(n, 6)
            rowmax(n, 7)
            copy_pT(n, 6)
            rowmax(n + 1, 0)
            rowmax(n + 1, 1)
            copy_pT(n + 1, 0)
            normalise(n, b)

        each(dve, step)
        add_y(NI - 1, NB - 1)
        nc.vector.scalar_tensor_tensor(router[:, :], keysT[:, :], 2.0, rwT[:, :], ALU.mult, ALU.add).then_inc(rt1, 1)
        nc.vector.tensor_tensor(keys2[:, :], keysT[:, :], keysT[:, :], ALU.mult).then_inc(rt1, 1)
        norm.vector(dve)
        dve.wait_ge(set_mm, 3)
        nc.vector.tensor_tensor(rbias[:, :], rbrow[:, :], ps[0:1, 4, 0:NE], ALU.subtract).then_inc(rt1, 1)
        dve.wait_ge(lg_mm, 1)
        nc.vector.tensor_copy(keep["logits"][:, :, :], ps[:, 5, 0:NT * NE].rearrange("p (t e) -> p t e", e=NE)
                              ).then_inc(lg_ev, 1)

    @block.tensor
    def _(pe):
        pe.wait_ge(w_ld, 16 * NWEIGHTS)
        for a in range(2):
            ins = nc.tensor.matmul(ps[:, a, :], wd[:, :], wkT[:, a * 512:(a + 1) * 512], start=True, stop=True)
        ins.then_inc(set_mm, 1)
        for n in range(NT):
            ins = nc.tensor.matmul(ps[:, 4 + n // 8, (n % 8) * LAT:(n % 8 + 1) * LAT],
                                   xT[:, n // TPB, (n % TPB) * P:(n % TPB + 1) * P], wdT[:, :], start=True, stop=True)
        ins.then_inc(lat_mm, 1)
        pe.wait_ge(set_ev, 1)
        pe.wait_ge(wq_scaled, 1)

        def project(n, b):
            wait_past(pe, qkT_ev, 2 * n)
            h = n // NB % NP0
            for t in range(TPB):
                ins = nc.tensor.matmul(qk_ps[:, t, :], xT[:, b, t * P:(t + 1) * P],
                                       wqk[:, bass.ds(h, 1), :].rearrange("p a n -> p (a n)"),
                                       start=True, stop=True)
            ins.then_inc(qk_mm, 1)

        def turn_qk(n):
            pe.wait_ge(rope_add, n + 1)
            for w in range(2):
                for t in range(TPB):
                    ins = nc.tensor.transpose(ps[:, w, t * P:(t + 1) * P], qk_r[:, t, w * P:(w + 1) * P],
                                              ident[:, :])
                ins.then_inc(qkT_mm, 1)

        def scores(n, b, u):
            i, j = UNITS[u]
            if u == 0:
                pe.wait_ge(qkT_ev, 2 * n + 2)
            wait_past(pe, exp_done, NU * n + u - 1)
            r = slice(64 * j, 64 * j + 64)
            nc.tensor.matmul(ps[:, 2 + j, 0:(i + 1) * P], qkT[r, b % 2, 0, i * P:(i + 1) * P],
                             qkT[r, b % 2, 1, 0:(i + 1) * P], start=True, stop=False, skip_group_check=True)
            nc.tensor.matmul(ps[:, 2 + j, i * P:(i + 1) * P], identb[:, :], cmask[:, :],
                             start=False, stop=True, skip_group_check=True).then_inc(s_mm, 1)

        def turn_p(n, u):
            i, j = UNITS[u]
            pe.wait_ge(exp_done, NU * n + u + 1)
            wait_past(pe, pT_ev[j], 4 * n + u // 2)
            for t in range(i + 1):
                ins = nc.tensor.transpose(ps[:, 4 + j, t * P:(t + 1) * P], prob[:, u % 4, t * P:(t + 1) * P],
                                          ident[:, :])
            ins.then_inc(pT_mm, 1)

        def values(n, b, u):
            i, j = UNITS[u]
            pe.wait_ge(pT_ev[j], 4 * n + u // 2 + 1)
            if u == 0:
                wait_past(pe, o_norm, n)
            c = 64 * (2 * i + j)
            for t in range(i + 1):
                ins = nc.tensor.matmul(o_ps[:, c:c + 64], probT[:, j, t * P:(t + 1) * P], lat[:, b * TPB + t, :],
                                       start=(t == 0), stop=(t == i))
            if u == NU - 1:
                ins.then_inc(o_mm, 1)

        def turn_o(n):
            pe.wait_ge(o_norm, n + 1)
            wait_past(pe, y_add, n)
            for t in range(TPB):
                ins = nc.tensor.transpose(m_ps[:, t * P:(t + 1) * P], on[:, t, :], ident[:, :])
            ins.then_inc(oT_mm, 1)

        def output(n):
            h = n // NB
            pe.wait_ge(oT_ev, n + 1)
            for t in range(TPB):
                ins = nc.tensor.matmul(m_ps[:, t * P:(t + 1) * P], oT[:, t * P:(t + 1) * P],
                                       wvo[:, bass.ds(h, 1), :].rearrange("p a n -> p (a n)"),
                                       start=True, stop=True)
            ins.then_inc(y_mm, 1)

        project(0, 0)
        turn_qk(0)
        scores(0, 0, 0)
        scores(0, 0, 1)
        pe.wait_ge(o_ld, 16 * (NLATER + 1))
        for h in range(NP0):
            for j in range(2):
                r = slice(64 * j, 64 * j + 64)
                ins = nc.tensor.matmul(ps[r, 6 + h // 4, (h % 4) * P:(h % 4 + 1) * P], wv[r, h, :], woT[r, h, :],
                                       start=True, stop=True)
        ins.then_inc(set_mm, 1)
        pe.wait_ge(lat_ev, 1)
        turn_p(0, 0)
        pe.wait_ge(set_ev, 2)

        def step(n, b):
            past = not isinstance(n, int) or n > 0
            scores(n, b, 2)
            turn_p(n, 1)
            project(n + 1, (b + 1) % NB)
            values(n, b, 0)
            if past:
                turn_o(n - 1)

            scores(n, b, 3)
            turn_p(n, 2)
            values(n, b, 1)
            if past:
                output(n - 1)

            scores(n, b, 4)
            turn_p(n, 3)
            values(n, b, 2)

            scores(n, b, 5)
            turn_p(n, 4)
            values(n, b, 3)

            scores(n, b, 6)
            turn_p(n, 5)
            values(n, b, 4)
            turn_qk(n + 1)

            scores(n, b, 7)
            turn_p(n, 6)
            values(n, b, 5)

            turn_p(n, 7)
            values(n, b, 6)
            scores(n + 1, b + 1, 0)

            values(n, b, 7)
            scores(n + 1, b + 1, 1)
            turn_p(n + 1, 0)

        each(pe, step)
        turn_o(NI - 1)
        output(NI - 1)
        norm.tensor(pe)
        pe.wait_ge(rt1, 2)
        pe.wait_ge(ones_set, 1)
        nc.tensor.matmul(ps[0:1, 4, 0:NE], ones[:, 0:1], keys2[:, :], start=True, stop=True).then_inc(set_mm, 1)
        pe.wait_ge(rt1, 3)
        for n in range(NT):
            if n % TPB == 0:
                pe.wait_ge(norm.turn_ev, n // TPB + 1)
            c = slice(n * NE, (n + 1) * NE)
            nc.tensor.matmul(ps[:, 5, c], xT[:, n // TPB, (n % TPB) * P:(n % TPB + 1) * P], router[:, :],
                             start=True, stop=False)
            ins = nc.tensor.matmul(ps[:, 5, c], ones[0:1, :], rbias[:, :], start=False, stop=True)
        ins.then_inc(lg_mm, 1)


def experts0(nc, ctx, io, keep):

    def sb(name, shape, dt=F32):
        return ctx.enter_context(nc.sbuf_tensor("m_" + name, shape, dt))

    def sem(name):
        return nc.alloc_semaphore("m_" + name)

    ps = keep["ps"]

    w1 = sb("w1", [P, 2, FF + FB])
    w2 = sb("w2", [P, 2, FB, D])
    b2big = sb("b2big", [P, P // NE, D])
    iota = sb("iota", [P, NE])
    top = sb("top", [P, NT, 8])
    topi = sb("topi", [P, NT, 8], mybir.dt.uint32)
    topf = sb("topf", [P, NT, TOPK])
    tops = sb("tops", [P, NT, TOPK])
    tope = sb("tope", [P, NT, TOPK])
    topz = sb("topz", [P, NT])
    topr = sb("topr", [P, NT])
    topw = sb("topw", [P, NT, TOPK])
    hit = sb("hit", [P, NT, TOPK, NE])
    hitw = sb("hitw", [P, NT, TOPK, NE])
    gates = sb("gates", [P, NT, NE])
    gatesT = sb("gatesT", [P, 2, P])
    hid = sb("hid", [P, 2, FB, S])
    x, xT, logits, ident = keep["x"], keep["xT"], keep["logits"], keep["ident"]

    w1_ld = [sem(f"w1_ld{k}") for k in range(2)]
    w2_ld = [sem(f"w2_ld{k}") for k in range(2)]
    c_ld = sem("c_ld")
    b2_zero = sem("b2_zero")
    top_done = sem("top_done")
    topi_done = sem("topi_done")
    gate_step = sem("gate_step")
    top_exp = sem("top_exp")
    gT_mm = sem("gT_mm")
    gT_ev = sem("gT_ev")
    b2_mm = sem("b2_mm")
    b2_add = sem("b2_add")
    up_mm = sem("up_mm")
    gelu_done = sem("gelu_done")
    down_mm = sem("down_mm")
    acc_done = sem("acc_done")
    NC = 1 + P // NE
    STEPS = NE * NB
    norm = Norm(nc, ctx, keep, ps, [0, 1, 2, 3], b2_add, [1, 2, 3, 4], "mn_")

    block = ctx.enter_context(nc.Block())

    @block.sync
    def _(sp):
        sp.dma_start(iota[:, :], io["iota"]).then_inc(c_ld, 16)
        for k in range(2):
            sp.dma_start(w1[:, k, :], io["w1T"][:, k, :]).then_inc(w1_ld[k], 16)
            sp.dma_start(w2[:, k, :, :], io["w2T"][:, k * FB:(k + 1) * FB, :]).then_inc(w2_ld[k], 16)
        sp.wait_ge(b2_zero, 1)
        for t in range(P // NE):
            sp.dma_start(b2big[t * NE:(t + 1) * NE, t, :], io["b2"]).then_inc(c_ld, 16)
        with sp.Fori(1, NE // 2) as pair:
            for k in range(2):
                e = pair * 2 + k
                sp.wait_ge(gelu_done, FB * NB * (e - 1))
                sp.dma_start(w1[:, k, :], io["w1T"][:, bass.ds(e, 1), :].rearrange("d a f -> d (a f)")
                             ).then_inc(w1_ld[k], 16)
                sp.wait_ge(down_mm, NB * (e - 1))
                sp.dma_start(w2[:, k, :, :], io["w2T"][:, bass.ds(e * FB, FB), :]).then_inc(w2_ld[k], 16)
        sp.wait_ge(gelu_done, FB * NB * (NE - 1))
        sp.dma_start(w1[:, 0, :], io["w1T"][:, 0, :]).then_inc(w1_ld[0], 16)

    @block.gpsimd
    def _(pool):
        nc.gpsimd.memset(b2big[:, :, :], 0.0).then_inc(b2_zero, 1)
        norm.pool(pool)

    @block.scalar
    def _(act):
        act.wait_ge(gate_step, 2)
        nc.scalar.activation(tope[:, :, :], tops[:, :, :], ACT.Exp).then_inc(top_exp, 1)
        act.wait_ge(c_ld, 16 * NC)
        with act.Fori(0, NE // 2) as pair:
            for k in range(2):
                for c in range(NB):
                    n = pair * (2 * NB) + (k * NB + c)
                    for f in range(FB):
                        act.wait_ge(up_mm, n * FB + f + 1)
                        nc.scalar.activation(hid[:, c % 2, f, :], ps[:, f, :], ACT.Gelu,
                                             bias=w1[:, k, FF + f:FF + f + 1]
                                             ).then_inc(gelu_done, 1)
        act.wait_ge(gT_mm, 1)
        nc.scalar.activation(gatesT[:, :, :], ps[:, 6, 0:2 * P].rearrange("p (a t) -> p a t", a=2), ACT.Copy
                             ).then_inc(gT_ev, 1)
        norm.scalar(act)

    @block.vector
    def _(dve):
        for t in range(NT):
            nc.vector.max(top[:, t, :], logits[:, t, :]).then_inc(top_done, 1)
        for t in range(NT):
            dve.wait_ge(top_done, t + 1)
            nc.vector.max_index(topi[:, t, :], top[:, t, :], logits[:, t, :]).then_inc(topi_done, 1)
        dve.wait_ge(topi_done, NT)
        nc.vector.tensor_copy(topf[:, :, :], topi[:, :, 0:TOPK]).then_inc(gate_step, 1)
        nc.vector.tensor_tensor(tops[:, :, :], top[:, :, 0:TOPK], top[:, :, 0:1].broadcast_to([P, NT, TOPK]),
                                ALU.subtract).then_inc(gate_step, 1)
        dve.wait_ge(gate_step, 1)
        dve.wait_ge(c_ld, 16 * NC)
        nc.vector.tensor_tensor(hit[:, :, :, :], topf[:, :, :, None].broadcast_to([P, NT, TOPK, NE]),
                                iota[:, None, None, :].broadcast_to([P, NT, TOPK, NE]), ALU.is_equal
                                ).then_inc(gate_step, 1)
        dve.wait_ge(top_exp, 1)
        nc.vector.tensor_reduce(topz[:, :], tope[:, :, :], AX.X, ALU.add).then_inc(gate_step, 1)
        dve.wait_ge(gate_step, 4)
        nc.vector.reciprocal(topr[:, :], topz[:, :]).then_inc(gate_step, 1)
        dve.wait_ge(gate_step, 5)
        nc.vector.tensor_tensor(topw[:, :, :], tope[:, :, :], topr[:, :, None].broadcast_to([P, NT, TOPK]),
                                ALU.mult).then_inc(gate_step, 1)
        dve.wait_ge(gate_step, 6)
        nc.vector.tensor_tensor(hitw[:, :, :, :], hit[:, :, :, :], topw[:, :, :, None].broadcast_to([P, NT, TOPK, NE]),
                                ALU.mult).then_inc(gate_step, 1)
        dve.wait_ge(gate_step, 7)
        nc.vector.tensor_reduce(gates[:, :, :], hitw[:, :, :, :].rearrange("p t k e -> p t e k"), AX.X, ALU.add
                                ).then_inc(acc_done, NB)
        with dve.Fori(0, NE // 2) as pair:
            for k in range(2):
                for c in range(NB):
                    n = pair * (2 * NB) + (k * NB + c)
                    dve.wait_ge(down_mm, n + 1)
                    dve.wait_ge(acc_done, n + 1)
                    for t in range(TPB):
                        tt = c * TPB + t
                        ins = nc.vector.scalar_tensor_tensor(
                            x[:, tt, :], ps[:, 4 + c % 2, t * D:(t + 1) * D],
                            gates[:, tt, bass.ds(pair * 2 + k, 1)], x[:, tt, :], ALU.mult, ALU.add)
                    ins.then_inc(acc_done, 1)
        dve.wait_ge(acc_done, NB + STEPS)
        for b in range(NB):
            dve.wait_ge(b2_mm, b + 1)
            ts = slice(b * TPB, (b + 1) * TPB)
            nc.vector.tensor_tensor(x[:, ts, :], ps[:, 4 + b, :].rearrange("p (t d) -> p t d", d=D), x[:, ts, :],
                                    ALU.add).then_inc(b2_add, 1)
        norm.vector(dve)

    @block.tensor
    def _(pe):
        def up(n, c, k):
            for f in range(FB):
                pe.wait_ge(gelu_done, n * FB - FB + f + 1 if not isinstance(n, int) else 0)
                nc.tensor.matmul(ps[:, f, :], w1[:, k, f * P:(f + 1) * P], xT[:, c, :],
                                 start=True, stop=True).then_inc(up_mm, 1)

        pe.wait_ge(w1_ld[0], 16)
        up(0, 0, 0)
        with pe.Fori(0, NE // 2) as pair:
            for k in range(2):
                for c in range(NB):
                    n = pair * (2 * NB) + (k * NB + c)
                    if c == NB - 1:
                        pe.wait_ge(w1_ld[1 - k], 16 * (pair + 1 + k))
                        up(n + 1, 0, 1 - k)
                    else:
                        up(n + 1, c + 1, k)
                    if c == 0:
                        pe.wait_ge(w2_ld[k], 16 * (pair + 1))
                    pe.wait_ge(gelu_done, n * FB + FB)
                    pe.wait_ge(acc_done, n + NB - 1)
                    for t in range(TPB):
                        for f in range(FB):
                            ins = nc.tensor.matmul(ps[:, 4 + c % 2, t * D:(t + 1) * D],
                                                   hid[:, c % 2, f, t * P:(t + 1) * P], w2[:, k, f, :],
                                                   start=(f == 0), stop=(f == FB - 1))
                    ins.then_inc(down_mm, 1)
        for a in range(2):
            ins = nc.tensor.transpose(ps[:, 6, a * P:(a + 1) * P],
                                      gates[:, a * 8:(a + 1) * 8, :].rearrange("p t e -> p (t e)"), ident[:, :])
        ins.then_inc(gT_mm, 1)
        pe.wait_ge(gT_ev, 1)
        pe.wait_ge(c_ld, 16 * NC)
        pe.wait_ge(acc_done, NB + STEPS)
        for b in range(NB):
            nc.tensor.matmul(ps[:, 4 + b, :], gatesT[:, b // 2, :],
                             b2big[:, (b % 2) * TPB:(b % 2 + 1) * TPB, :].rearrange("p t d -> p (t d)"),
                             start=True, stop=True).then_inc(b2_mm, 1)
        norm.tensor(pe)


NH1 = 16
HD1 = 8
QUADS = NH1 // 4
KS = 9 * HD1
NSH = 3


def attention1(nc, ctx, io, keep):

    def sb(name, shape, dt=F32):
        return ctx.enter_context(nc.sbuf_tensor("c_sb_" + name, shape, dt))

    def sem(name):
        return nc.alloc_semaphore("c_" + name)

    ps = keep["ps"]
    parts_d = nc.dram_tensor("c_parts_d", (NB, 2, 3 * HD1, NH1 * S), BF16).ap()
    shift_d = nc.dram_tensor("c_shift_d", (NB * QUADS, NSH, 4 * S), BF16).ap()

    shT_ps = ps[:, 7, :].bitcast(BF16)[0:NSH * 4, 0:S]

    wq = sb("wq", [P, P])
    wk = sb("wk", [P, P])
    wv = sb("wv", [P, P])
    rot = sb("rot", [P, NB])
    identb = sb("identb", [P, P], BF16)
    q32 = sb("q32", [P, 2, S])
    r32 = sb("r32", [P, 2, S])
    parts = sb("parts", [P, 2, 3, S], BF16)
    sq = sb("sq", [P, 2, NH1, S], BF16)
    sk = sb("sk", [P, 2, NH1, S], BF16)
    v_all = sb("v_all", [P, NT, P])
    v1 = sb("v1", [P, TPB, 4, 32])
    negmax = sb("negmax", [P, TPB, 4])
    shr = sb("shr", [P, TPB, 4])
    shp = sb("shp", [P, TPB, NSH, 4], BF16)
    shT = sb("shT", [NSH * 4, S], BF16)
    pT = sb("pT", [P, 2, 4, TPB, S])
    oT = sb("oT", [P, S])
    rcp = sb("rcp", [P, TPB, 4])
    att = sb("att", [P, TPB, 4, HD1])
    x, xT, ident = keep["x"], keep["xT"], keep["ident"]

    w_ld = sem("w_ld")
    sq_zero = sem("sq_zero")
    sk_one = sem("sk_one")
    v1_init = sem("v1_init")
    v_mm = sem("v_mm")
    v_ev = sem("v_ev")
    qk_mm = sem("qk_mm")
    part_a = sem("part_a")
    part_b = sem("part_b")
    parts_st = [sem(f"parts_st{k}") for k in range(2)]
    stack_ld = sem("stack_ld")
    max_free = sem("max_free")
    max_mm = sem("max_mm")
    shift_step = sem("shift_step")
    shift_mm = sem("shift_mm")
    shift_ev = sem("shift_ev")
    shift_st = sem("shift_st")
    shift_ld = sem("shift_ld")
    exp_free = sem("exp_free")
    st_mm = sem("st_mm")
    v1_done = sem("v1_done")
    pv_mm = sem("pv_mm")
    oT_ev = sem("oT_ev")
    oT_mm = sem("oT_mm")
    rcp_done = sem("rcp_done")
    att_done = sem("att_done")
    x_add = sem("x_add")
    held = sem("held")
    NW = 5
    NQ = NB * QUADS
    SCALE = HD1 ** -0.5
    norm = Norm(nc, ctx, keep, ps, [0, 1, 2, 3], x_add, [QUADS * (b + 1) for b in range(NB)], "cn_")

    block = ctx.enter_context(nc.Block())

    def each_quad(eng, step):
        for m in range(2):
            step(m, m)
        with eng.Fori(1, NQ // 2 - 1) as pair:
            for k in range(2):
                step(pair * 2 + k, k)
        for k in range(2):
            step(NQ - 2 + k, k)

    def known(m, below):
        return isinstance(m, int) and m < below

    @block.sync
    def _(sp):
        for dst, src in ((wq[:, :], "c_wqT"), (wk[:, :], "c_wkT"), (wv[:, :], "c_wvT"), (rot[:, :], "c_rot"),
                         (identb[:, :], "identb")):
            sp.dma_start(dst, io[src]).then_inc(w_ld, 16)
        sp.wait_ge(sq_zero, 1)
        sp.wait_ge(sk_one, 1)
        def store_parts(b):
            for w in range(2):
                sp.wait_ge(part_b, 3 * (2 * b + w + 1))
                sp.dma_start(parts_d[b, w].rearrange("(a d) (h n) -> (d h) a n", a=3, h=NH1), parts[:, w, :, :]
                             ).then_inc(parts_st[w], 16)

        def stack(b):
            for a in range(3):
                for c in range(3):
                    r = (3 * a + c) * HD1
                    sp.dma_start(sq[r:r + HD1, bass.ds(b % 2, 1), :, :].rearrange("r a h n -> r (a h n)"),
                                 parts_d[bass.ds(b, 1), 0, a * HD1:(a + 1) * HD1, :].rearrange("b r n -> (b r) n")
                                 ).then_inc(stack_ld, 16)
                r = 3 * a * HD1
                sp.dma_start(sk[r:r + 3 * HD1, bass.ds(b % 2, 1), :, :].rearrange("r a h n -> r (a h n)"),
                             parts_d[bass.ds(b, 1), 1, :, :].rearrange("b r n -> (b r) n")).then_inc(stack_ld, 16)

        def shift(m):
            sp.wait_ge(shift_ev, m + 1)
            sp.sem_inc(held, 1)
            sp.dma_start(shift_d[bass.ds(m, 1)].rearrange("b a (h n) -> (b a h) n", h=4), shT[:, :]
                         ).then_inc(shift_st, 16)
            sp.wait_ge(shift_st, 16 * (m + 1))
            sp.sem_inc(held, 1)
            sp.dma_start(sq[KS:KS + NSH, bass.ds(m // QUADS % 2, 1), bass.ds(m % QUADS * 4, 4), :]
                         .rearrange("r a h n -> r (a h n)"),
                         shift_d[bass.ds(m, 1)].rearrange("b a n -> (b a) n")).then_inc(shift_ld, 16)

        store_parts(0)
        for w in range(2):
            sp.wait_ge(parts_st[w], 16)
        stack(0)
        for b in range(1, NB):
            store_parts(b)
        for w in range(2):
            sp.wait_ge(parts_st[w], 16 * NB)
        sp.wait_ge(stack_ld, 192)
        stack(1)
        for m in range(QUADS + 1):
            shift(m)
        with sp.Fori(1, NB - 1) as b:
            sp.wait_ge(st_mm, NH1 * TPB * b)
            sp.sem_inc(held, 1)
            sp.wait_ge(stack_ld, 192 * (b + 1))
            sp.sem_inc(held, 1)
            stack(b + 1)
            for q in range(QUADS):
                shift(b * QUADS + q + 1)
        for q in range(QUADS - 1):
            shift(NQ - QUADS + q + 1)

    @block.gpsimd
    def _(pool):
        nc.gpsimd.memset(sk[:, :, :, :], 1.0).then_inc(sk_one, 1)
        nc.gpsimd.memset(v1[:, :, :, :], 0.0).then_inc(v1_init, 1)
        pool.wait_ge(v1_init, 1)
        nc.gpsimd.memset(v1[:, :, :, HD1:HD1 + 1], 1.0).then_inc(v1_init, 1)
        pool.wait_ge(v1_init, 2)
        pool.wait_ge(v_ev, NB)

        def step(m, k):
            wait_past(pool, pv_mm, m)
            nc.gpsimd.tensor_copy(v1[:, :, :, 0:HD1],
                                  v_all[:, bass.ds(m // QUADS * TPB, TPB), bass.ds(m % QUADS * 4 * HD1, 4 * HD1)]
                                  .rearrange("p t (g d) -> p t g d", g=4)).then_inc(v1_done, 1)
            if not known(m, 2):
                add(m - 2)

        def add(m):
            pool.wait_ge(att_done, m + 1)
            xs = x[:, bass.ds(m // QUADS * TPB, TPB), bass.ds(m % QUADS * 4 * HD1, 4 * HD1)]
            nc.gpsimd.tensor_tensor(xs, xs, att[:, :, :, :].rearrange("p t g d -> p t (g d)"), ALU.add
                                    ).then_inc(x_add, 1)

        each_quad(pool, step)
        add(NQ - 2)
        add(NQ - 1)
        norm.pool(pool)

    @block.scalar
    def _(act):
        act.wait_ge(w_ld, 16 * NW)
        nc.scalar.activation(oT[:, 0:1], rot[:, 0:1], ACT.Copy).then_inc(exp_free, 2)
        for b in range(NB):
            act.wait_ge(v_mm, b + 1)
            nc.scalar.activation(v_all[:, b * TPB:(b + 1) * TPB, :].rearrange("p t d -> p (t d)"), ps[:, 2 + b, :],
                                 ACT.Copy).then_inc(v_ev, 1)
        for n in range(2 * NB):
            b, w = n // 2, n % 2
            act.wait_ge(qk_mm, n + 1)
            if n >= 2:
                act.wait_ge(part_b, 3 * (n - 1))
                act.wait_ge(parts_st[w], 16 * b)
            nc.scalar.activation(q32[:, w, :], ps[:, w, :], ACT.Copy, scale=rot[:, b:b + 1]).then_inc(part_a, 1)
            act.wait_ge(part_a, 2 * n + 1)
            nc.scalar.activation(parts[:, w, 0, :], q32[:, w, :], ACT.Copy).then_inc(part_a, 1)

        def exps(m, k, g):
            for t in range(TPB):
                act.wait_ge(st_mm, (m * 4 + g) * TPB + t + 1)
                nc.scalar.activation(pT[:, k, g, t, :], ps[:, 4 + t % 2, :], ACT.Exp, scale=SCALE).then_inc(exp_free, 1)

        def copy_shift(m):
            act.wait_ge(shift_mm, m + 1)
            wait_past(act, shift_st, 16 * m)
            nc.scalar.activation(shT[:, :], shT_ps, ACT.Copy).then_inc(shift_ev, 1)

        def copy_o(m):
            act.wait_ge(pv_mm, m + 1)
            wait_past(act, oT_mm, m)
            nc.scalar.activation(oT[:, :], ps[:, 6, :], ACT.Copy).then_inc(oT_ev, 1)

        copy_shift(0)

        def step(m, k):
            wait_past(act, pv_mm, m - 1)
            exps(m, k, 0)
            if not isinstance(m, int) or m < NQ - 1:
                copy_shift(m + 1)
            exps(m, k, 1)
            exps(m, k, 2)
            exps(m, k, 3)
            if not known(m, 1):
                copy_o(m - 1)

        each_quad(act, step)
        copy_o(NQ - 1)
        norm.scalar(act)

    @block.vector
    def _(dve):
        nc.vector.memset(sq[:, :, :, :], 0.0).then_inc(sq_zero, 1)
        for n in range(2 * NB):
            b, w = n // 2, n % 2
            dve.wait_ge(part_a, 2 * n + 2)
            nc.vector.tensor_tensor(r32[:, w, :], q32[:, w, :], parts[:, w, 0, :], ALU.subtract).then_inc(part_b, 1)
            dve.wait_ge(part_b, 3 * n + 1)
            nc.vector.tensor_copy(parts[:, w, 1, :], r32[:, w, :]).then_inc(part_b, 1)
            dve.wait_ge(part_b, 3 * n + 2)
            nc.vector.tensor_tensor(parts[:, w, 2, :], r32[:, w, :], parts[:, w, 1, :], ALU.subtract
                                    ).then_inc(part_b, 1)
        nc.vector.memset(negmax[:, 0, 0:1], 0.0).then_inc(max_free, 2)

        def maxima(m, g):
            for i in range(2):
                dve.wait_ge(max_mm, 2 * (4 * m + g) + i + 1)
                nc.vector.tensor_reduce(negmax[:, 2 * i:2 * i + 2, g], ps[:, 2 * i:2 * i + 2, :], AX.X, ALU.max,
                                        negate=True).then_inc(max_free, 1)

        def shift(m):
            dve.wait_ge(max_free, 2 + 8 * (m + 1))
            wait_past(dve, shift_mm, m)
            nc.vector.tensor_copy(shp[:, :, 0, :], negmax[:, :, :]).then_inc(shift_step, 1)
            dve.wait_ge(shift_step, 4 * m + 1)
            nc.vector.tensor_tensor(shr[:, :, :], negmax[:, :, :], shp[:, :, 0, :], ALU.subtract
                                    ).then_inc(shift_step, 1)
            dve.wait_ge(shift_step, 4 * m + 2)
            nc.vector.tensor_copy(shp[:, :, 1, :], shr[:, :, :]).then_inc(shift_step, 1)
            dve.wait_ge(shift_step, 4 * m + 3)
            nc.vector.tensor_tensor(shp[:, :, 2, :], shr[:, :, :], shp[:, :, 1, :], ALU.subtract
                                    ).then_inc(shift_step, 1)

        def normalise(m):
            dve.wait_ge(oT_mm, m + 1)
            wait_past(dve, x_add, m)
            o4 = ps[:, 7, :].rearrange("p (t g c) -> p t g c", t=TPB, g=4)
            nc.vector.reciprocal(rcp[:, :, :], o4[:, :, :, HD1]).then_inc(rcp_done, 1)
            dve.wait_ge(rcp_done, m + 1)
            nc.vector.tensor_tensor(att[:, :, :, :], o4[:, :, :, 0:HD1],
                                    rcp[:, :, :, None].broadcast_to([P, TPB, 4, HD1]), ALU.mult
                                    ).then_inc(att_done, 1)

        for m in range(2):
            for g in range(4):
                maxima(m, g)
            shift(m)

        def step(m, k):
            for g in range(4):
                if not isinstance(m, int) or m < NQ - 2:
                    maxima(m + 2, g)
                if g == 2 and not known(m, 2):
                    normalise(m - 2)
            if not isinstance(m, int) or m < NQ - 2:
                shift(m + 2)

        each_quad(dve, step)
        normalise(NQ - 2)
        normalise(NQ - 1)
        norm.vector(dve)

    @block.tensor
    def _(pe):
        pe.wait_ge(w_ld, 16 * NW)
        for b in range(NB):
            for t in range(TPB):
                ins = nc.tensor.matmul(ps[:, 2 + b, t * P:(t + 1) * P], xT[:, b, t * P:(t + 1) * P],
                                       wv[:, :], start=True, stop=True)
            ins.then_inc(v_mm, 1)
        for n in range(2 * NB):
            b, w = n // 2, n % 2
            if n >= 2:
                pe.wait_ge(part_a, 2 * (n - 1))
            nc.tensor.matmul(ps[:, w, :], (wq, wk)[w][:, :], xT[:, b, :], start=True, stop=True
                             ).then_inc(qk_mm, 1)

        def stacked(tile, m, g, rows, cols):
            return tile[0:rows, bass.ds(m // QUADS % 2, 1), bass.ds(m % QUADS * 4 + g, 1), cols]\
                .rearrange("r a h n -> r (a h n)")

        def max_scores(m, g, half):
            pe.wait_ge(max_free, 2 * (4 * m + g) + half + 1)
            for i in range(2 * half, 2 * half + 2):
                ins = nc.tensor.matmul(ps[:, i, :], stacked(sq, m, g, KS, slice(i * P, (i + 1) * P)),
                                       stacked(sk, m, g, KS, slice(0, S)), start=True, stop=True)
            ins.then_inc(max_mm, 1)

        def exp_scores(m, g, half):
            for t in range(2 * half, 2 * half + 2):
                pe.wait_ge(exp_free, (4 * m + g) * TPB + t + 1)
                nc.tensor.matmul(ps[:, 4 + t % 2, :], stacked(sk, m, g, P, slice(t * P, (t + 1) * P)),
                                 stacked(sq, m, g, P, slice(0, S)), start=True, stop=True).then_inc(st_mm, 1)

        def turn_shift(m):
            pe.wait_ge(shift_step, 4 * (m + 1))
            wait_past(pe, att_done, m - 3)
            wait_past(pe, shift_ev, m)
            pe.sem_inc(held, 1)
            for i in range(TPB):
                ins = nc.tensor.transpose(shT_ps[:, i * P:(i + 1) * P],
                                          shp[:, i, :, :].rearrange("p a h -> p (a h)"), identb[:, :])
            ins.then_inc(shift_mm, 1)

        def sums(m, k, t):
            if t == 0:
                pe.wait_ge(v1_done, m + 1)
                wait_past(pe, oT_ev, m)
                pe.wait_ge(exp_free, 2 + 4 * TPB * (m + 1))
            for g in range(4):
                ins = nc.tensor.matmul(ps[32 * g:32 * g + 32, 6, :], v1[:, t, g, :], pT[:, k, g, t, :],
                                       start=(t == 0), stop=(t == TPB - 1), skip_group_check=True)
            if t == TPB - 1:
                ins.then_inc(pv_mm, 1)

        def turn_o(m):
            pe.wait_ge(oT_ev, m + 1)
            wait_past(pe, att_done, m)
            pe.wait_ge(shift_ev, m + 4 if not isinstance(m, int) or m < NQ - 4 else NQ)
            for i in range(TPB):
                ins = nc.tensor.transpose(ps[:, 7, i * P:(i + 1) * P], oT[:, i * P:(i + 1) * P], ident[:, :])
            ins.then_inc(oT_mm, 1)

        pe.wait_ge(part_a, 4 * NB)
        pe.wait_ge(v_ev, NB)
        pe.wait_ge(stack_ld, 192)
        for m in range(2):
            for g in range(4):
                for half in range(2):
                    max_scores(m, g, half)
            if m == 0:
                turn_shift(0)

        def step(m, k):
            early = not isinstance(m, int) or m < NQ - 2
            if early:
                pe.wait_ge(stack_ld, 192 * ((m + 2) // QUADS + 1))
            pe.wait_ge(shift_ld, 16 * (m + 1))
            for g in range(4):
                for half in range(2):
                    if early:
                        max_scores(m + 2, g, half)
                    exp_scores(m, g, half)
                if g == 0 and (not isinstance(m, int) or m < NQ - 1):
                    turn_shift(m + 1)
                if g == 1 and not known(m, 2):
                    turn_o(m - 2)
                if not known(m, 1):
                    sums(m - 1, 1 - k, g)

        each_quad(pe, step)
        turn_o(NQ - 2)
        for t in range(TPB):
            sums(NQ - 1, 1, t)
        turn_o(NQ - 1)
        norm.tensor(pe)


LAYERS = 2
NH2 = 8
HD2 = 64
INNER = NH2 * HD2
WIN = 64
KEYS = P + WIN
HID = 341
HB = 3
HROWS = [P, P, HID - 2 * P]


def local_attention(nc, ctx, io, keep, layer):

    def head(k, i):
        return 4 * (k // 2) + 2 * i + k % 2

    def keys(t):
        return slice(0 if t else WIN, KEYS)

    def sb(name, shape, dt=F32):
        return ctx.enter_context(nc.sbuf_tensor(f"l{layer}_sb_" + name, shape, dt))

    def sem(name):
        return nc.alloc_semaphore(f"l{layer}_" + name)

    ps = keep["ps"]
    o_ps = ps[:, 6, :]
    m_ps = ps[:, 7, :]
    PAIRS = NH2 // 2

    wqkv = sb("wqkv", [P, 3, INNER])
    wo = sb("wo", [P, INNER // P, D])
    base_c = sb("base_c", [P, TPB, 2, HD2])
    base_s = sb("base_s", [P, TPB, 2, HD2])
    qks = sb("qks", [P, 2, HD2])
    tab_c = sb("tab_c", [P, TPB, 2, HD2])
    tab_s = sb("tab_s", [P, TPB, 2, HD2])
    wmask = sb("wmask", [P, 2, KEYS], BF16)
    identb = sb("identb", [P, P], BF16)
    hT = sb("hT", [P, P])
    qk_raw = sb("qk_raw", [P, 2, INNER])
    sqr = sb("sqr", [P, 2 * INNER])
    ssq = sb("ssq", [P, 2 * NH2])
    ssqc = sb("ssqc", [P, 2 * NH2])
    rn = sb("rn", [P, 2 * NH2])
    neg_half = sb("neg_half", [P, 2 * NH2])
    qk_c = sb("qk_c", [P, 2, INNER])
    qk_s = sb("qk_s", [P, 2, INNER])
    qk_r = sb("qk_r", [P, 2, INNER])
    qk_n = sb("qk_n", [P, 2, INNER])
    qT = sb("qT", [P, PAIRS, P])
    kT = sb("kT", [P, 2, PAIRS, KEYS])
    v = sb("v", [P, TPB, INNER])
    negmax = sb("negmax", [P, NH2])
    den = sb("den", [P, 2, NH2])
    rden = sb("rden", [P, NH2])
    prob = sb("prob", [P, 2, 2, 2 * P])
    probT = sb("probT", [P, 2, 2, 2 * P])
    on = sb("on", [P, INNER])
    oT = sb("oT", [P, INNER])
    x, ident = keep["x"], keep["ident"]

    w_ld = sem("w_ld")
    inited = sem("inited")
    tab_done = sem("tab_done")
    hT_done = sem("hT_done")
    qk_mm = sem("qk_mm")
    v_mm = sem("v_mm")
    v_ev = sem("v_ev")
    raw_done = sem("raw_done")
    sqr_done = sem("sqr_done")
    ssq_sum = sem("ssq_sum")
    ssq_done = sem("ssq_done")
    rn_step = sem("rn_step")
    rope_mul = sem("rope_mul")
    rope_add = sem("rope_add")
    qk_norm = sem("qk_norm")
    qkT_mm = sem("qkT_mm")
    qkT_ev = sem("qkT_ev")
    s_mm = sem("s_mm")
    max_done = sem("max_done")
    exp_done = sem("exp_done")
    pT_mm = sem("pT_mm")
    pT_ev = [sem(f"pT_ev{k}") for k in range(2)]
    o_mm = sem("o_mm")
    recip = sem("recip")
    o_norm = sem("o_norm")
    oT_mm = sem("oT_mm")
    oT_ev = sem("oT_ev")
    y_mm = sem("y_mm")
    y_add = sem("y_add")
    NW = 8

    block = ctx.enter_context(nc.Block())

    def each_tile(eng, step):
        for t in range(TPB):
            step(t, t)
        with eng.Fori(1, NB) as b:
            for t in range(TPB):
                step(TPB * b + t, t)

    @block.sync
    def _(sp):
        sp.dma_start(wqkv[:, :, :], io["wqkv"][layer]).then_inc(w_ld, 16)
        sp.dma_start(wo[:, :, :], io["l_wo"][layer]).then_inc(w_ld, 16)
        sp.dma_start(base_c[:, :, :, :], io["cos1"]).then_inc(w_ld, 16)
        sp.dma_start(base_s[:, :, :, :], io["sin1"]).then_inc(w_ld, 16)
        sp.dma_start(qks[:, 0, :], io["q_scale"][layer:layer + 1, :].broadcast_to([P, HD2])).then_inc(w_ld, 16)
        sp.dma_start(qks[:, 1, :], io["k_scale"][layer:layer + 1, :].broadcast_to([P, HD2])).then_inc(w_ld, 16)
        sp.dma_start(wmask[:, :, :], io["wmask"]).then_inc(w_ld, 16)
        sp.dma_start(identb[:, :], io["identb"]).then_inc(w_ld, 16)

    @block.gpsimd
    def _(pool):
        nc.gpsimd.memset(neg_half[:, :], -0.5).then_inc(inited, 1)
        nc.gpsimd.memset(prob[:, :, :, :], 0.0).then_inc(inited, 1)
        nc.gpsimd.memset(keep["xT_pad"], 0.0).then_inc(inited, 1)
        pool.wait_ge(inited, 3)

        def shifted(n, t):
            b = n // TPB % NB
            wait_past(pool, v_mm, n)
            full = keep["xT_full"]
            nc.gpsimd.tensor_copy(hT[0:64, :], full[0:64, bass.ds(b, 1), bass.ds(t * P + 1, P)]
                                  .rearrange("p a n -> p (a n)")).then_inc(hT_done, 1)
            pool.wait_ge(hT_done, 2 * n + 1)
            nc.gpsimd.tensor_copy(hT[64:P, :], full[64:P, bass.ds(b, 1), bass.ds(t * P, P)]
                                  .rearrange("p a n -> p (a n)")).then_inc(hT_done, 1)
            pool.wait_ge(hT_done, 2 * n + 2)

        def norms(n):
            pool.wait_ge(ssq_done, n + 1)
            nc.gpsimd.tensor_tensor(rn[:, :], ssqc[:, :], neg_half[:, :], ALU.pow).then_inc(rn_step, 1)
            pool.wait_ge(rope_add, n + 1)
            pool.wait_ge(rn_step, n + 1)
            wait_past(pool, qkT_mm, 2 * n)
            for w in range(2):
                nc.gpsimd.tensor_tensor(qk_n[:, w, :].rearrange("p (h d) -> p h d", d=HD2),
                                        qk_r[:, w, :].rearrange("p (h d) -> p h d", d=HD2),
                                        rn[:, w * NH2:(w + 1) * NH2, None].broadcast_to([P, NH2, HD2]), ALU.mult
                                        ).then_inc(qk_norm, 1)
            pool.wait_ge(qk_norm, 2 * n + 2)

        shifted(0, 0)
        shifted(1, 1)
        norms(0)
        shifted(2, 2)

        def step(n, t):
            norms(n + 1)
            shifted(n + 3, (t + 3) % TPB)

        each_tile(pool, step)

    @block.scalar
    def _(act):
        act.wait_ge(inited, 3)

        def copy_qk(n):
            wait_past(act, rope_mul, n)
            nc.scalar.activation(qk_raw[:, :, :], ps[:, 0:2, :], ACT.Copy).then_inc(raw_done, 1)

        def squares(n):
            act.wait_ge(qk_mm, n + 1)
            wait_past(act, ssq_sum, n)
            nc.scalar.activation(sqr[:, :], ps[:, 0:2, :].rearrange("p a n -> p (a n)"), ACT.Square
                                 ).then_inc(sqr_done, 1)

        def copy_v(n, t):
            act.wait_ge(v_mm, n + 1)
            nc.scalar.activation(v[:, t, :], m_ps, ACT.Copy).then_inc(v_ev, 1)

        def copy_qkT(n, t):
            act.wait_ge(qkT_mm, 2 * n + 1)
            nc.scalar.activation(qT[:, :, :], ps[:, 0, :].rearrange("p (a n) -> p a n", n=P), ACT.Copy
                                 ).then_inc(qkT_ev, 1)
            act.wait_ge(qkT_mm, 2 * n + 2)
            k4 = ps[:, 1, :].rearrange("p (a n) -> p a n", n=P)
            nc.scalar.activation(kT[:, t % 2, :, WIN:KEYS], k4, ACT.Copy).then_inc(qkT_ev, 1)
            nc.scalar.activation(kT[:, (t + 1) % 2, :, 0:WIN], k4[:, :, P - WIN:P], ACT.Copy).then_inc(qkT_ev, 1)

        def exps(n, t, k):
            c = keys(t)
            j = PAIRS * n + k
            act.wait_ge(max_done, j + 1)
            if k == 0:
                wait_past(act, recip, n - 1)
            for i in range(2):
                u = head(k, i)
                ins = nc.scalar.activation(prob[:, k % 2, i, WIN + c.start:2 * P],
                                           ps[:, 2 + k % 2, i * KEYS + c.start:(i + 1) * KEYS], ACT.Exp,
                                           bias=negmax[:, u:u + 1], accum_out=den[:, t % 2, u:u + 1])
            ins.then_inc(exp_done, 1)

        def copy_pT(n, t, k):
            act.wait_ge(pT_mm, PAIRS * n + k + 1)
            c = slice(0 if t else P, 2 * P)
            nc.scalar.activation(probT[:, 1, :, c], ps[:, 5, :].rearrange("p (i c) -> p i c", i=2)[:, :, c],
                                 ACT.Copy).then_inc(pT_ev[1], 1)

        def copy_oT(n):
            act.wait_ge(oT_mm, n + 1)
            wait_past(act, y_mm, n)
            nc.scalar.activation(oT[:, :], m_ps, ACT.Copy).then_inc(oT_ev, 1)

        squares(0)
        copy_qk(0)
        copy_v(0, 0)
        copy_qkT(0, 0)
        squares(1)
        copy_qk(1)
        copy_v(1, 1)
        exps(0, 0, 0)
        exps(0, 0, 1)

        def step(n, t):
            copy_pT(n, t, 1)
            exps(n, t, 2)
            exps(n, t, 3)
            if not isinstance(n, int) or n > 0:
                copy_oT(n - 1)
            copy_qkT(n + 1, (t + 1) % TPB)
            copy_pT(n, t, 3)
            exps(n + 1, (t + 1) % TPB, 0)
            squares(n + 2)
            copy_qk(n + 2)
            exps(n + 1, (t + 1) % TPB, 1)
            copy_v(n + 2, (t + 2) % TPB)

        each_tile(act, step)
        copy_oT(NT - 1)

    @block.vector
    def _(dve):
        dve.wait_ge(w_ld, 16 * NW)
        h = HD2 // 2
        nc.vector.tensor_tensor(tab_c[:, :, :, :], base_c[:, :, :, :],
                                qks[:, None, :, :].broadcast_to([P, TPB, 2, HD2]), ALU.mult).then_inc(tab_done, 1)
        for a in (0, h):
            nc.vector.tensor_tensor(tab_s[:, :, :, a:a + h], base_s[:, :, :, a:a + h],
                                    qks[:, None, :, h - a:2 * h - a].broadcast_to([P, TPB, 2, h]), ALU.mult
                                    ).then_inc(tab_done, 1)
        dve.wait_ge(tab_done, 3)

        raw = qk_raw[:, :, :].rearrange("p w (g d) -> p w g d", d=HD2)

        def tab(tile, t, a, b):
            return tile[:, t, :, a:b][:, :, None, :].broadcast_to([P, 2, NH2, b - a])

        def rope_c(n, t):
            dve.wait_ge(raw_done, n + 1)
            nc.vector.tensor_tensor(qk_c[:, :, :].rearrange("p w (g d) -> p w g d", d=HD2), raw,
                                    tab(tab_c, t, 0, HD2), ALU.mult)

        def rope_s(n, t):
            for a in (0, h):
                ins = nc.vector.tensor_tensor(
                    qk_s[:, :, :].rearrange("p w (g d) -> p w g d", d=HD2)[:, :, :, a:a + h],
                    raw[:, :, :, h - a:2 * h - a], tab(tab_s, t, a, a + h), ALU.mult)
            ins.then_inc(rope_mul, 1)

        def rope_sum(n):
            dve.wait_ge(rope_mul, n + 1)
            wait_past(dve, qk_norm, 2 * n)
            nc.vector.tensor_tensor(qk_r[:, :, :], qk_c[:, :, :], qk_s[:, :, :], ALU.add).then_inc(rope_add, 1)

        def squares(n):
            dve.wait_ge(sqr_done, n + 1)
            nc.vector.tensor_reduce(ssq[:, :], sqr[:, :].rearrange("p (g d) -> p g d", d=HD2), AX.X, ALU.add
                                    ).then_inc(ssq_sum, 1)
            dve.wait_ge(ssq_sum, n + 1)
            wait_past(dve, rn_step, n)
            nc.vector.tensor_scalar(ssqc[:, :], ssq[:, :], 1e-24, None, ALU.max).then_inc(ssq_done, 1)

        def rowmax(n, t, k):
            dve.wait_ge(s_mm, PAIRS * n + k + 1)
            nc.vector.tensor_reduce(negmax[:, head(k, 0):head(k, 1) + 1:2],
                                    ps[:, 2 + k % 2, 0:2 * KEYS].rearrange("p (i c) -> p i c", i=2)[:, :, keys(t)],
                                    AX.X, ALU.max, negate=True).then_inc(max_done, 1)

        def copy_pT(n, t, k):
            dve.wait_ge(pT_mm, PAIRS * n + k + 1)
            c = slice(0 if t else P, 2 * P)
            nc.vector.tensor_copy(probT[:, 0, :, c], ps[:, 4, :].rearrange("p (i c) -> p i c", i=2)[:, :, c]
                                  ).then_inc(pT_ev[0], 1)

        def normalise(n, t):
            dve.wait_ge(exp_done, PAIRS * (n + 1))
            nc.vector.reciprocal(rden[:, :], den[:, t % 2, :]).then_inc(recip, 1)
            dve.wait_ge(recip, n + 1)
            dve.wait_ge(o_mm, n + 1)
            wait_past(dve, oT_mm, n)
            nc.vector.tensor_tensor(on[:, :].rearrange("p (u d) -> p u d", d=HD2),
                                    o_ps.rearrange("p (u d) -> p u d", d=HD2),
                                    rden[:, :, None].broadcast_to([P, NH2, HD2]), ALU.mult).then_inc(o_norm, 1)

        def add_y(n):
            dve.wait_ge(y_mm, n + 1)
            xt = x[:, bass.ds(n, 1), :].rearrange("p a d -> p (a d)")
            nc.vector.tensor_tensor(xt, m_ps[:, 0:D], xt, ALU.add).then_inc(y_add, 1)

        squares(0)
        rope_c(0, 0)
        rope_s(0, 0)
        rope_sum(0)
        squares(1)
        rope_c(1, 1)
        rope_s(1, 1)
        rowmax(0, 0, 0)
        rowmax(0, 0, 1)
        copy_pT(0, 0, 0)

        def step(n, t):
            rowmax(n, t, 2)
            rope_sum(n + 1)
            rowmax(n, t, 3)
            copy_pT(n, t, 2)
            if not isinstance(n, int) or n > 0:
                add_y(n - 1)
            rowmax(n + 1, (t + 1) % TPB, 0)
            squares(n + 2)
            rowmax(n + 1, (t + 1) % TPB, 1)
            copy_pT(n + 1, (t + 1) % TPB, 0)
            rope_c(n + 2, (t + 2) % TPB)
            normalise(n, t)
            rope_s(n + 2, (t + 2) % TPB)

        each_tile(dve, step)
        add_y(NT - 1)

    @block.tensor
    def _(pe):
        pe.wait_ge(w_ld, 16 * NW)
        pe.wait_ge(inited, 3)

        def project_qk(n):
            pe.wait_ge(hT_done, 2 * (n + 1))
            wait_past(pe, qkT_ev, 3 * n)
            for w in range(2):
                ins = nc.tensor.matmul(ps[:, w, :], hT[:, :], wqkv[:, w, :], start=True, stop=True)
            ins.then_inc(qk_mm, 1)

        def project_v(n):
            wait_past(pe, y_add, n - 2)
            wait_past(pe, v_ev, n)
            nc.tensor.matmul(m_ps, hT[:, :], wqkv[:, 2, :], start=True, stop=True).then_inc(v_mm, 1)

        def turn_qk(n):
            for w in range(2):
                pe.wait_ge(qk_norm, 2 * n + w + 1)
                for a in range(4):
                    ins = nc.tensor.transpose(ps[:, w, a * P:(a + 1) * P], qk_n[:, w, a * P:(a + 1) * P],
                                              ident[:, :])
                ins.then_inc(qkT_mm, 1)

        def scores(n, t, k):
            if k == 0:
                pe.wait_ge(qkT_ev, 3 * n + 3)
            wait_past(pe, exp_done, PAIRS * n + k - 1)
            c = keys(t)
            nc.tensor.matmul(ps[:, 2 + k % 2, 0:2 * KEYS].rearrange("p (i c) -> p i c", i=2)[:, :, c], identb[:, :],
                             wmask[:, 1 if t else 0, c][:, None, :].broadcast_to([P, 2, KEYS - c.start]),
                             start=True, stop=False, skip_group_check=True)
            for i in range(2):
                r = slice(64 * (k % 2), 64 * (k % 2) + 64)
                ins = nc.tensor.matmul(ps[:, 2 + k % 2, i * KEYS + c.start:(i + 1) * KEYS],
                                       qT[r, head(k, i) // 2, :], kT[r, t % 2, head(k, i) // 2, c],
                                       start=False, stop=(i == 1), skip_group_check=True)
            ins.then_inc(s_mm, 1)

        def turn_p(n, t, k):
            pe.wait_ge(exp_done, PAIRS * n + k + 1)
            wait_past(pe, pT_ev[k % 2], 2 * n + k // 2)
            for i in range(2):
                for a in range(0 if t else 1, 2):
                    ins = nc.tensor.transpose(ps[:, 4 + k % 2, (2 * i + a) * P:(2 * i + a + 1) * P],
                                              prob[:, k % 2, i, a * P:(a + 1) * P], ident[:, :])
            ins.then_inc(pT_mm, 1)

        def values(n, t, k):
            pe.wait_ge(pT_ev[k % 2], 2 * n + k // 2 + 1)
            if k == 0:
                wait_past(pe, o_norm, n)
                pe.wait_ge(v_ev, n + 1)
            for i in range(2):
                c = slice(HD2 * head(k, i), HD2 * (head(k, i) + 1))
                ins = nc.tensor.matmul(o_ps[:, c], probT[:, k % 2, i, P:2 * P], v[:, t, c], start=True,
                                       stop=(t == 0))
                if t:
                    ins = nc.tensor.matmul(o_ps[:, c], probT[64:P, k % 2, i, 0:P], v[64:P, t - 1, c],
                                           start=False, stop=True)
            if k == PAIRS - 1:
                ins.then_inc(o_mm, 1)

        def turn_o(n):
            pe.wait_ge(o_norm, n + 1)
            pe.wait_ge(v_ev, n + 3 if not isinstance(n, int) or n < NT - 1 else NT + 2)
            for a in range(4):
                ins = nc.tensor.transpose(m_ps[:, a * P:(a + 1) * P], on[:, a * P:(a + 1) * P], ident[:, :])
            ins.then_inc(oT_mm, 1)

        def output(n):
            pe.wait_ge(oT_ev, n + 1)
            for a in range(4):
                ins = nc.tensor.matmul(m_ps[:, 0:D], oT[:, a * P:(a + 1) * P], wo[:, a, :],
                                       start=(a == 0), stop=(a == 3))
            ins.then_inc(y_mm, 1)

        project_qk(0)
        project_v(0)
        turn_qk(0)
        project_qk(1)
        project_v(1)
        scores(0, 0, 0)
        scores(0, 0, 1)
        turn_p(0, 0, 0)

        def step(n, t):
            past = not isinstance(n, int) or n > 0
            scores(n, t, 2)
            turn_p(n, t, 1)
            scores(n, t, 3)
            values(n, t, 0)
            if past:
                turn_o(n - 1)

            turn_p(n, t, 2)
            values(n, t, 1)
            if past:
                output(n - 1)
            turn_qk(n + 1)

            turn_p(n, t, 3)
            values(n, t, 2)
            scores(n + 1, (t + 1) % TPB, 0)

            project_qk(n + 2)
            scores(n + 1, (t + 1) % TPB, 1)
            turn_p(n + 1, (t + 1) % TPB, 0)
            values(n, t, 3)
            project_v(n + 2)

        each_tile(pe, step)
        turn_o(NT - 1)
        output(NT - 1)


def gated_mlp(nc, ctx, io, keep, layer):

    def sb(name, shape, dt=F32):
        return ctx.enter_context(nc.sbuf_tensor(f"g{layer}_sb_" + name, shape, dt))

    def sem(name):
        return nc.alloc_semaphore(f"g{layer}_" + name)

    ps = keep["ps"]

    w1 = sb("w1", [P, 2, HID])
    w2 = sb("w2", [P, HB, D])
    b1 = sb("b1", [P, 2, HB])
    lgb = sb("lgb", [P, 2])
    hT = sb("hT", [P, S])
    stats = sb("stats", [P, NT, 6])
    mv = sb("mv", [P, NT, 2])
    var = sb("var", [P, NT])
    rstd = sb("rstd", [P, NT])
    eps = sb("eps", [P, TPB])
    neg_half = sb("neg_half", [P, TPB])
    hn = sb("hn", [P, TPB, D])
    hnT = sb("hnT", [P, 2, S])
    gl = sb("gl", [P, 2, S])
    hid = sb("hid", [P, 2, HB, S])
    x, xT, ident = keep["x"], keep["xT"], keep["ident"]

    w_ld = sem("w_ld")
    inited = sem("inited")
    x1_mm = sem("x1_mm")
    x1_ev = sem("x1_ev")
    h_mm = sem("h_mm")
    stats_done = sem("stats_done")
    mv_done = sem("mv_done")
    var_done = sem("var_done")
    rstd_done = sem("rstd_done")
    hn_done = sem("hn_done")
    hn_mm = sem("hn_mm")
    hn_ev = sem("hn_ev")
    g_mm = sem("g_mm")
    a_mm = sem("a_mm")
    gelu_done = sem("gelu_done")
    hid_done = sem("hid_done")
    y_mm = sem("y_mm")
    y_add = sem("y_add")
    x2_mm = sem("x2_mm")
    x2_ev = sem("x2_ev")
    NW = 6

    block = ctx.enter_context(nc.Block())

    @block.sync
    def _(sp):
        sp.dma_start(w1[:, :, :], io["l_w1"][layer]).then_inc(w_ld, 16)
        sp.dma_start(b1[:, :, :], io["l_b1"][layer]).then_inc(w_ld, 16)
        sp.dma_start(lgb[:, :], io["l_gb"][layer]).then_inc(w_ld, 16)
        for k in range(HB):
            r = HROWS[k] + (k == HB - 1)
            sp.dma_start(w2[0:r, k, :], io["l_w2"][layer, k * P:k * P + r, :]).then_inc(w_ld, 16)

    @block.gpsimd
    def _(pool):
        nc.gpsimd.memset(eps[:, :], EPS).then_inc(inited, 1)
        nc.gpsimd.memset(neg_half[:, :], -0.5).then_inc(inited, 1)
        nc.gpsimd.memset(hT[:, 0:1], 0.0).then_inc(inited, 1)
        nc.gpsimd.memset(hid[:, :, HB - 1, :], 1.0).then_inc(inited, 1)
        pool.wait_ge(inited, 4)
        for b in range(NB):
            t = slice(b * TPB, (b + 1) * TPB)
            pool.wait_ge(mv_done, b + 1)
            nc.gpsimd.tensor_tensor(var[:, t], mv[:, t, 1], eps[:, :], ALU.add).then_inc(var_done, 1)
            pool.wait_ge(var_done, b + 1)
            nc.gpsimd.tensor_tensor(rstd[:, t], var[:, t], neg_half[:, :], ALU.pow).then_inc(rstd_done, 1)

    @block.scalar
    def _(act):
        act.wait_ge(w_ld, 16 * NW)
        act.wait_ge(inited, 4)

        def front(b):
            act.wait_ge(x1_mm, b + 1)
            nc.scalar.activation(hT[0:64, :], ps[0:64, 0, :], ACT.Copy).then_inc(x1_ev, 1)
            nc.scalar.activation(hT[64:P, 1:S], ps[64:P, 0, 0:S - 1], ACT.Copy).then_inc(x1_ev, 1)
            act.wait_ge(hn_mm, b + 1)
            nc.scalar.activation(hnT[:, b % 2, :], ps[:, 2, :], ACT.Identity, scale=lgb[:, 0:1], bias=lgb[:, 1:2]
                                 ).then_inc(hn_ev, 1)

        front(0)
        for b in range(NB):
            for k in range(HB):
                r = HROWS[k]
                n = b * HB + k
                act.wait_ge(g_mm, n + 1)
                if n >= 2:
                    act.wait_ge(hid_done, n - 1)
                nc.scalar.activation(gl[0:r, n % 2, :], ps[0:r, 3 + n % 2, :], ACT.Gelu, bias=b1[0:r, 1, k:k + 1]
                                     ).then_inc(gelu_done, 1)
            if b + 1 < NB:
                front(b + 1)
            act.wait_ge(x2_mm, b + 1)
            nc.scalar.activation(xT[:, b, :], ps[:, 7, :], ACT.Copy).then_inc(x2_ev, 1)

    @block.vector
    def _(dve):
        dve.wait_ge(w_ld, 16 * NW)
        dve.wait_ge(inited, 4)

        def front(b):
            dve.wait_ge(h_mm, b + 1)
            for t in range(TPB):
                nc.vector.bn_stats(stats[:, b * TPB + t, :], ps[:, 1, t * P:(t + 1) * P]).then_inc(stats_done, 1)
            dve.wait_ge(stats_done, TPB * (b + 1))
            for t in range(TPB):
                ins = nc.vector.bn_aggr(mv[:, b * TPB + t, :], stats[:, b * TPB + t, :])
            ins.then_inc(mv_done, 1)
            dve.wait_ge(rstd_done, b + 1)
            if b:
                dve.wait_ge(hn_mm, b)
            for t in range(TPB):
                n = b * TPB + t
                ins = nc.vector.tensor_scalar(hn[:, t, :], ps[:, 1, t * P:(t + 1) * P], mv[:, n, 0:1],
                                              rstd[:, n:n + 1], ALU.subtract, ALU.mult)
            ins.then_inc(hn_done, 1)

        front(0)
        for b in range(NB):
            for k in range(HB):
                r = HROWS[k]
                n = b * HB + k
                dve.wait_ge(gelu_done, n + 1)
                dve.wait_ge(a_mm, n + 1)
                if k == 0 and b >= 2:
                    dve.wait_ge(y_mm, b - 1)
                nc.vector.scalar_tensor_tensor(hid[0:r, b % 2, k, :], ps[0:r, 5 + n % 2, :], b1[0:r, 0, k:k + 1],
                                               gl[0:r, n % 2, :], ALU.add, ALU.mult).then_inc(hid_done, 1)
            if b + 1 < NB:
                front(b + 1)
            dve.wait_ge(y_mm, b + 1)
            ts = slice(b * TPB, (b + 1) * TPB)
            nc.vector.tensor_tensor(x[:, ts, :], ps[:, 7, :].rearrange("p (t d) -> p t d", d=D), x[:, ts, :],
                                    ALU.add).then_inc(y_add, 1)

    @block.tensor
    def _(pe):
        pe.wait_ge(w_ld, 16 * NW)

        def turn(bank, src, done):
            for t in range(TPB):
                ins = nc.tensor.transpose(ps[:, bank, t * P:(t + 1) * P], src(t), ident[:, :])
            ins.then_inc(done, 1)

        def front_a(b):
            if b:
                pe.wait_ge(x1_ev, 2 * b)
            turn(0, lambda t: x[:, b * TPB + t, :], x1_mm)
            pe.wait_ge(x1_ev, 2 * (b + 1))
            pe.wait_ge(inited, 3)
            if b:
                pe.wait_ge(hn_done, b)
            turn(1, lambda t: hT[:, t * P:(t + 1) * P], h_mm)

        def front_b(b):
            pe.wait_ge(hn_done, b + 1)
            if b:
                pe.wait_ge(hn_ev, b)
            turn(2, lambda t: hn[:, t, :], hn_mm)

        def up(b):
            for k in range(HB):
                r = HROWS[k]
                n = b * HB + k
                if k == 0:
                    pe.wait_ge(hn_ev, b + 1)
                if n >= 2:
                    pe.wait_ge(gelu_done, n - 1)
                nc.tensor.matmul(ps[0:r, 3 + n % 2, :], w1[:, 1, k * P:k * P + r], hnT[:, b % 2, :],
                                 start=True, stop=True).then_inc(g_mm, 1)
                if n >= 2:
                    pe.wait_ge(hid_done, n - 1)
                nc.tensor.matmul(ps[0:r, 5 + n % 2, :], w1[:, 0, k * P:k * P + r], hnT[:, b % 2, :],
                                 start=True, stop=True).then_inc(a_mm, 1)

        def down(b):
            pe.wait_ge(hid_done, HB * (b + 1))
            if b:
                pe.wait_ge(x2_ev, b)
            for t in range(TPB):
                for k in range(HB):
                    r = HROWS[k] + (k == HB - 1)
                    ins = nc.tensor.matmul(ps[:, 7, t * P:(t + 1) * P], hid[0:r, b % 2, k, t * P:(t + 1) * P],
                                           w2[0:r, k, :], start=(k == 0), stop=(k == HB - 1))
            ins.then_inc(y_mm, 1)

        front_a(0)
        front_b(0)
        for b in range(NB):
            up(b)
            if b + 1 < NB:
                front_a(b + 1)
            down(b)
            if b + 1 < NB:
                front_b(b + 1)
            pe.wait_ge(y_add, b + 1)
            turn(7, lambda t: x[:, b * TPB + t, :], x2_mm)


def save_x(nc, ctx, keep):
    saved = nc.alloc_semaphore("x3_saved")
    block = ctx.enter_context(nc.Block())

    @block.vector
    def _(dve):
        nc.vector.tensor_copy(keep["x3"][:, :, :], keep["x"][:, :, :]).then_inc(saved, 1)


def finish(nc, ctx, keep, out):
    ps = keep["ps"]
    summed = nc.alloc_semaphore("f_summed")
    stored = nc.alloc_semaphore("f_stored")
    norm = Norm(nc, ctx, keep, ps, [0, 1, 2, 3], summed, [1, 2, 3, 4], "fn_")
    block = ctx.enter_context(nc.Block())
    x, x3 = keep["x"], keep["x3"]

    @block.gpsimd
    def _(pool):
        norm.pool(pool)

    @block.vector
    def _(dve):
        for b in range(NB):
            ts = slice(b * TPB, (b + 1) * TPB)
            nc.vector.tensor_tensor(x[:, ts, :], x[:, ts, :], x3[:, ts, :], ALU.add).then_inc(summed, 1)
        norm.vector(dve)

    @block.sync
    def _(sp):
        for b in range(NB):
            ts = slice(b * TPB, (b + 1) * TPB)
            sp.wait_ge(norm.norm_done, b + 1)
            sp.dma_start(out[b].rearrange("(t p) d -> p t d", p=P), x[:, ts, :]).then_inc(stored, 16)
        sp.wait_ge(stored, 16 * NB)


def program(nc, io, out):
    with ExitStack() as ctx:
        def tile(name, shape):
            return ctx.enter_context(nc.sbuf_tensor("keep_" + name, shape, F32))

        ps = ctx.enter_context(nc.psum_tensor("ps", [P, 8, 512], F32))
        xT_full = tile("xT", [P, NB, S + 1])
        keep = dict(ps=ps, x=tile("x", [P, NT, D]), logits=tile("logits", [P, NT, NE]), ident=tile("ident", [P, P]),
                    x3=tile("x3", [P, NT, D]), xT_full=xT_full, xT=xT_full[:, :, 1:S + 1],
                    xT_pad=xT_full[:, :, 0:1])
        for phase in (attention0, experts0, attention1):
            with nc.cleanup_on_exit(), ExitStack() as inner:
                phase(nc, inner, io, keep)
        with nc.cleanup_on_exit(), ExitStack() as inner:
            save_x(nc, inner, keep)
        for layer in range(LAYERS):
            for phase in (local_attention, gated_mlp):
                with nc.cleanup_on_exit(), ExitStack() as inner:
                    phase(nc, inner, io, keep, layer)
        with nc.cleanup_on_exit(), ExitStack() as inner:
            finish(nc, inner, keep, out)


def rotary(length, width):
    f32 = np.float32
    inv = f32(1.0) / f32(10000.0) ** (np.arange(0, width, 2, dtype=f32) / f32(width))
    angle = np.arange(length, dtype=f32)[:, None] * inv[None, :].astype(f32)
    angle = np.concatenate([angle, angle], 1)
    return np.cos(angle).astype(f32), np.sin(angle).astype(f32)


def shape_constants():
    f32 = np.float32
    bf16 = mybir.dt.np(BF16)
    c = {}
    c["ident"] = np.eye(P, dtype=f32)
    c["identb"] = np.eye(P).astype(bf16)
    c["iota"] = np.tile(np.arange(NE, dtype=f32), (P, 1))
    c["cmask"] = np.where(np.arange(P)[None, :] > np.arange(P)[:, None], -1e30, 0).astype(bf16)
    cos, sin = rotary(S, HD0)
    first = np.where(np.arange(HD0) < HD0 // 2, -1, 1).astype(f32)
    c["cos0"], c["sin0"] = cos, sin * first
    cos, sin = rotary(NB, 8)
    c["c_rot"] = np.repeat(np.concatenate([(cos + sin)[:, :4], (cos - sin)[:, 4:]], 1).T, 16, 0).astype(f32)
    cos, sin = rotary(S, HD2)
    half = np.arange(0, HD2, 2, dtype=f32)
    base = (half + f32(0.4 * HD2)) / f32(1.4 * HD2)
    power = (np.arange(S, dtype=f32) - S // 2) / f32(WIN // 2)
    scale = (base[None, :] ** power[:, None]).astype(f32)
    scale = np.concatenate([scale, scale], 1)
    c["cos1"] = np.stack([8 * cos * scale, cos / scale], 1).reshape(TPB, P, 2, HD2).transpose(1, 0, 2, 3)
    c["sin1"] = np.stack([8 * sin * scale * first, sin / scale * first], 1)\
        .reshape(TPB, P, 2, HD2).transpose(1, 0, 2, 3)
    key, query = np.arange(KEYS)[None, :], np.arange(P)[:, None]
    seen = (key >= query) & (key <= query + WIN)
    c["wmask"] = np.where(np.stack([seen & (key >= WIN), seen], 1), 0, -1e30).astype(bf16)
    return c


def layouts(i):
    a = {}
    x = i["L0_attn_x"]
    a["x"] = x.reshape(NT, P, D).transpose(1, 0, 2)
    a["xT"] = x.reshape(NB * S, D).T
    a["wd"] = i["L0_attn_w_kv_down"]
    a["wdT"] = i["L0_attn_w_kv_down"].T
    a["wkT"] = i["L0_attn_w_k_up"].T
    a["wqT"] = i["L0_attn_wq"].T
    a["wv"] = i["L0_attn_w_v_up"]
    a["woT"] = i["L0_attn_wo"].T
    a["keysT"] = i["L0_ffn_keys"].T
    a["rwT"] = i["L0_ffn_rw"].T
    a["rb"] = i["L0_ffn_rb"].reshape(1, NE)
    a["w1T"] = np.concatenate([i["L0_ffn_w1"].transpose(2, 0, 1),
                               i["L0_ffn_b1"].reshape(NE, FB, P).transpose(2, 0, 1)], 2)
    a["w2T"] = i["L0_ffn_w2"].reshape(NE, D, FB, P).transpose(3, 0, 2, 1).reshape(P, NE * FB, D)
    a["b2"] = i["L0_ffn_b2"]
    order = (np.arange(16)[None, :] * 8 + np.arange(8)[:, None]).reshape(-1)
    a["c_wqT"] = i["L1_attn_Wq"][order].T
    a["c_wkT"] = i["L1_attn_Wk"][order].T
    a["c_wvT"] = i["L1_attn_Wv"].T
    a["wqkv"] = i["L1_ffn_wqkv"].reshape(LAYERS, D, 3, INNER)
    a["l_wo"] = i["L1_ffn_wo"].reshape(LAYERS, INNER // P, P, D).transpose(0, 2, 1, 3)
    a["q_scale"], a["k_scale"] = i["L1_ffn_q_scale"], i["L1_ffn_k_scale"]
    a["l_w1"] = i["L1_ffn_w1"].reshape(LAYERS, D, 2, HID)
    b1 = np.zeros((LAYERS, 2, HB * P), np.float32)
    b1[:, :, :HID] = i["L1_ffn_b1"].reshape(LAYERS, 2, HID)
    a["l_b1"] = b1.reshape(LAYERS, 2, HB, P).transpose(0, 3, 1, 2)
    a["l_gb"] = np.stack([i["L1_ffn_ln_g"], i["L1_ffn_ln_b"]], -1)
    a["l_w2"] = np.concatenate([i["L1_ffn_w2"], i["L1_ffn_b2"][:, None, :]], 1)
    return a


def kernel(**inputs):
    import concourse.bacc as bacc
    from concourse.bass_utils import run_bass_kernel_spmd

    inputs = {name: np.asarray(a) for name, a in inputs.items()}
    arrays = {**shape_constants(), **layouts(inputs)}
    arrays = {name: np.ascontiguousarray(a) for name, a in arrays.items()}
    nc = bacc.Bacc("TRN2", target_bir_lowering=False, num_devices=1)
    io = {name: nc.dram_tensor(name, a.shape, mybir.dt.from_np(a.dtype), kind="ExternalInput").ap()
          for name, a in arrays.items()}
    out = nc.dram_tensor("out", (NB, S, D), F32, kind="ExternalOutput").ap()
    program(nc, io, out)
    result = run_bass_kernel_spmd(nc, [arrays], core_ids=[0])
    return result.results[0]["out"]
```

```python
from contextlib import ExitStack

import numpy as np

import concourse.bass as bass
from concourse import mybir

ALU = mybir.AluOpType
ACT = mybir.ActivationFunctionType
AX = mybir.AxisListType
F32 = mybir.dt.float32
BF16 = mybir.dt.bfloat16
F32R = mybir.dt.float32r

P = 128
NB = 4
S = 512
D = 128
TPB = S // P
NT = NB * TPB
EPS = 1e-5

HD0 = 64
NP0 = 8
LAT = 64
UNITS = [(i, j) for i in reversed(range(TPB)) for j in range(2)]
NU = len(UNITS)

NE = 16
FF = 512
FB = FF // P
TOPK = 4


NH1 = 16
HD1 = 8
QUADS = NH1 // 4
KS = 9 * HD1
NSH = 3

LAYERS = 2
NH2 = 8
HD2 = 64
INNER = NH2 * HD2
WIN = 64
KEYS = P + WIN
HID = 341
HB = 3
HROWS = [P, P, HID - 2 * P]


class Preloaded:

    def __init__(self, nc, ctx, io):
        self.loads = []

        def tile(name, shape, dt=F32):
            return ctx.enter_context(nc.sbuf_tensor("pre_" + name, shape, dt))

        def load(dst, src):
            self.loads.append((dst, src))

        self.w1 = tile("w1", [P, 2, FF + FB])
        self.w2 = tile("w2", [P, 2, FB, D])
        self.b2 = tile("b2", [NE, D])
        self.iota = tile("iota", [P, NE])
        load(self.iota[:, :], io["iota"])
        load(self.b2[:, :], io["b2"])
        load(self.w1[:, :, :], io["w1T"][:, 0:2, :])
        load(self.w2[:, :, :, :], io["w2T"][:, 0:2 * FB, :].rearrange("p (e f) d -> p e f d", e=2))
        self.wq, self.wk, self.wv = (tile(n, [P, P]) for n in ("wq", "wk", "wv"))
        self.rot = tile("rot", [P, NB])
        self.identb = tile("identb", [P, P], BF16)
        for dst, src in ((self.wq, "c_wqT"), (self.wk, "c_wkT"), (self.wv, "c_wvT"), (self.rot, "c_rot"),
                         (self.identb, "identb")):
            load(dst[:, :], io[src])
        self.wqkv = [tile(f"wqkv{i}", [P, 3, INNER]) for i in range(LAYERS)]
        self.wo = [tile(f"wo{i}", [P, INNER // P, D]) for i in range(LAYERS)]
        self.base_c = tile("base_c", [P, TPB, 2, HD2])
        self.base_s = tile("base_s", [P, TPB, 2, HD2])
        self.qks = [tile(f"qks{i}", [P, 2, HD2]) for i in range(LAYERS)]
        self.wmask = tile("wmask", [P, 2, KEYS], BF16)
        load(self.base_c[:, :, :, :], io["cos1"])
        load(self.base_s[:, :, :, :], io["sin1"])
        load(self.wmask[:, :, :], io["wmask"])
        self.m_w1 = [tile(f"m_w1{i}", [P, 2, HID]) for i in range(LAYERS)]
        self.m_w2 = [tile(f"m_w2{i}", [P, HB, D]) for i in range(LAYERS)]
        self.m_b1 = [tile(f"m_b1{i}", [P, 2, HB]) for i in range(LAYERS)]
        self.m_lgb = [tile(f"m_lgb{i}", [P, 2]) for i in range(LAYERS)]
        for i in range(LAYERS):
            load(self.wqkv[i][:, :, :], io["wqkv"][i])
            load(self.wo[i][:, :, :], io["l_wo"][i])
            load(self.qks[i][:, 0, :], io["q_scale"][i:i + 1, :].broadcast_to([P, HD2]))
            load(self.qks[i][:, 1, :], io["k_scale"][i:i + 1, :].broadcast_to([P, HD2]))
            load(self.m_w1[i][:, :, :], io["l_w1"][i])
            load(self.m_b1[i][:, :, :], io["l_b1"][i])
            load(self.m_lgb[i][:, :], io["l_gb"][i])
            for k in range(HB):
                r = HROWS[k] + (k == HB - 1)
                load(self.m_w2[i][0:r, k, :], io["l_w2"][i, k * P:k * P + r, :])


class Norm:

    def __init__(self, nc, ctx, keep, ps, banks, ready, counts, prefix):
        def sb(name, shape):
            return ctx.enter_context(nc.sbuf_tensor(prefix + name, shape, F32))

        def sem(name):
            return nc.alloc_semaphore(prefix + name)

        self.nc, self.keep, self.ps, self.banks, self.ready, self.counts = nc, keep, ps, banks, ready, counts
        self.stats = sb("stats", [P, NT, 6])
        self.mv = sb("mv", [P, NT, 2])
        self.var = sb("var", [P, NT])
        self.rstd = sb("rstd", [P, NT])
        self.eps = sb("eps", [P, TPB])
        self.neg_half = sb("neg_half", [P, TPB])
        self.consts = sem("consts")
        self.stats_done = sem("stats_done")
        self.mv_done = sem("mv_done")
        self.var_done = sem("var_done")
        self.rstd_done = sem("rstd_done")
        self.norm_done = sem("norm_done")
        self.turn_mm = sem("turn_mm")
        self.turn_ev = sem("turn_ev")

    def pool(self, pool):
        nc = self.nc
        nc.gpsimd.memset(self.eps[:, :], EPS).then_inc(self.consts, 1)
        nc.gpsimd.memset(self.neg_half[:, :], -0.5).then_inc(self.consts, 1)
        pool.wait_ge(self.consts, 2)
        for b in range(NB):
            t = slice(b * TPB, (b + 1) * TPB)
            pool.wait_ge(self.mv_done, b + 1)
            nc.gpsimd.tensor_tensor(self.var[:, t], self.mv[:, t, 1], self.eps[:, :], ALU.add
                                    ).then_inc(self.var_done, 1)
            pool.wait_ge(self.var_done, b + 1)
            nc.gpsimd.tensor_tensor(self.rstd[:, t], self.var[:, t], self.neg_half[:, :], ALU.pow
                                    ).then_inc(self.rstd_done, 1)

    def vector(self, dve):
        nc, x = self.nc, self.keep["x"]

        def moments(b):
            dve.wait_ge(self.ready, self.counts[b])
            for t in range(b * TPB, (b + 1) * TPB):
                nc.vector.bn_stats(self.stats[:, t, :], x[:, t, :]).then_inc(self.stats_done, 1)
            dve.wait_ge(self.stats_done, TPB * (b + 1))
            for t in range(b * TPB, (b + 1) * TPB):
                ins = nc.vector.bn_aggr(self.mv[:, t, :], self.stats[:, t, :])
            ins.then_inc(self.mv_done, 1)

        def normalise(b):
            dve.wait_ge(self.rstd_done, b + 1)
            for t in range(b * TPB, (b + 1) * TPB):
                ins = nc.vector.tensor_scalar(x[:, t, :], x[:, t, :], self.mv[:, t, 0:1], self.rstd[:, t:t + 1],
                                              ALU.subtract, ALU.mult)
            ins.then_inc(self.norm_done, 1)

        moments(0)
        for b in range(NB):
            if b + 1 < NB:
                moments(b + 1)
            normalise(b)

    def tensor(self, pe):
        for b in range(NB):
            pe.wait_ge(self.norm_done, b + 1)
            for t in range(TPB):
                ins = self.nc.tensor.transpose(self.ps[:, self.banks[b], t * P:(t + 1) * P],
                                               self.keep["x"][:, b * TPB + t, :], self.keep["ident"][:, :])
            ins.then_inc(self.turn_mm, 1)

    def scalar(self, act):
        for b in range(NB):
            act.wait_ge(self.turn_mm, b + 1)
            self.nc.scalar.activation(self.keep["xT"][:, b, :], self.ps[:, self.banks[b], :],
                                      ACT.Copy).then_inc(self.turn_ev, 1)


def wait_past(eng, sem, count):
    if not isinstance(count, int) or count > 0:
        eng.wait_ge(sem, count)


def attention0(nc, ctx, io, keep):

    def sb(name, shape, dt=F32):
        return ctx.enter_context(nc.sbuf_tensor("a_" + name, shape, dt))

    def sem(name):
        return nc.alloc_semaphore("a_" + name)

    ps = keep["ps"]
    qk_ps = ps[:, 0:2, :].rearrange("p a (t c) -> p (a t) c", c=256)
    o_ps = ps[:, 6, :]
    m_ps = ps[:, 7, :]

    wqk = sb("wqk", [P, NP0, 256])
    wvo = sb("wvo", [P, NP0, P])
    wkT = sb("wkT", [LAT, NP0 * P])
    wd = sb("wd", [LAT, P])
    wdT = sb("wdT", [P, LAT])
    wv = sb("wv", [P, NP0, LAT])
    woT = sb("woT", [P, NP0, P])
    cos = sb("cos", [P, TPB, HD0])
    sin = sb("sin", [P, TPB, HD0])
    cmask = sb("cmask", [P, P], BF16)
    identb = sb("identb", [P, P], BF16)
    lat = sb("lat", [P, NT, LAT])
    qk_c = sb("qk_c", [P, TPB, 256])
    qk_s = sb("qk_s", [P, TPB, 256])
    qk_r = sb("qk_r", [P, TPB, 256])
    qkT = sb("qkT", [P, 2, 2, S])
    negmax = sb("negmax", [P, NU])
    den = sb("den", [P, 2, NU])
    rden = sb("rden", [P, NU])
    prob = sb("prob", [P, 4, S])
    probT = sb("probT", [P, 2, S])
    on = sb("on", [P, TPB, P])
    oT = sb("oT", [P, S])
    keysT = sb("keysT", [P, NE])
    rwT = sb("rwT", [P, NE])
    router = sb("router", [P, NE])
    keys2 = sb("keys2", [P, NE])
    rbrow = sb("rbrow", [1, NE])
    rbias = sb("rbias", [1, NE])
    ones = sb("ones", [P, P])
    x, xT, ident = keep["x"], keep["xT"], keep["ident"]

    w_ld = sem("w_ld")
    o_ld = sem("o_ld")
    pre_ld = sem("pre_ld")
    set_mm = sem("set_mm")
    set_ev = sem("set_ev")
    ones_set = sem("ones_set")
    wq_scaled = sem("wq_scaled")
    rt1 = sem("rt1")
    lat_mm = sem("lat_mm")
    lat_ev = sem("lat_ev")
    qk_mm = sem("qk_mm")
    rope_mul = sem("rope_mul")
    rope_add = sem("rope_add")
    qkT_mm = sem("qkT_mm")
    qkT_ev = sem("qkT_ev")
    s_mm = sem("s_mm")
    max_done = sem("max_done")
    exp_done = sem("exp_done")
    pT_mm = sem("pT_mm")
    pT_ev = [sem(f"pT_ev{j}") for j in range(2)]
    o_mm = sem("o_mm")
    recip = sem("recip")
    o_norm = sem("o_norm")
    oT_mm = sem("oT_mm")
    oT_ev = sem("oT_ev")
    y_mm = sem("y_mm")
    y_add = sem("y_add")
    lg_mm = sem("lg_mm")
    lg_ev = sem("lg_ev")

    NWEIGHTS = 10
    NLATER = 5
    NI = NP0 * NB
    SCALE = HD0 ** -0.5
    norm = Norm(nc, ctx, keep, ps, [0, 1, 2, 3], y_add, [NI - NB + b + 1 for b in range(NB)], "an_")

    block = ctx.enter_context(nc.Block())

    def each(eng, step):
        for b in range(NB):
            step(b, b)
        with eng.Fori(1, NP0) as h:
            for b in range(NB):
                step(h * NB + b, b)

    @block.sync
    def _(sp):
        def load(dst, src):
            sp.dma_start(dst, src).then_inc(w_ld, 16)

        def load_later(dst, src):
            sp.dma_start(dst, src).then_inc(o_ld, 16)

        load(wd[:, :], io["wd"])
        load(wkT[:, :], io["wkT"])
        load(wqk[:, :, 0:P], io["wqT"].rearrange("c (h n) -> c h n", h=NP0))
        load(xT, io["xT"].rearrange("c (b n) -> c b n", b=NB))
        load(wdT[:, :], io["wdT"])
        load(cos[:, :, :], io["cos0"].rearrange("(t p) d -> p t d", p=P))
        load(sin[:, :, :], io["sin0"].rearrange("(t p) d -> p t d", p=P))
        load(cmask[:, :], io["cmask"])
        load(identb[:, :], io["identb"])
        load(ident[:, :], io["ident"])
        load_later(wv[:, :, :], io["wv"].rearrange("(h q) l -> q h l", q=P))
        load_later(woT[:, :, :], io["woT"].rearrange("(h q) n -> q h n", q=P))
        load_later(x[:, :, :], io["x"])
        load_later(keysT[:, :], io["keysT"])
        load_later(rwT[:, :], io["rwT"])
        load_later(rbrow[:, :], io["rb"])
        for dst, src in keep["pre"].loads:
            sp.dma_start(dst, src).then_inc(pre_ld, 16)
        sp.wait_ge(pre_ld, 16 * len(keep["pre"].loads))

    @block.gpsimd
    def _(pool):
        nc.gpsimd.memset(ones[:, :], 1.0).then_inc(ones_set, 1)

        def rope_sum(n):
            pool.wait_ge(rope_mul, n + 1)
            wait_past(pool, qkT_mm, 2 * n)
            nc.gpsimd.tensor_tensor(qk_r[:, :, :], qk_c[:, :, :], qk_s[:, :, :], ALU.add).then_inc(rope_add, 1)

        rope_sum(0)
        each(pool, lambda n, b: rope_sum(n + 1))
        norm.pool(pool)

    @block.scalar
    def _(act):
        act.wait_ge(set_mm, 1)
        nc.scalar.activation(wqk[:, :, P:2 * P], ps[:, 0:2, :].rearrange("p a (h n) -> p (a h) n", n=P),
                             ACT.Copy).then_inc(set_ev, 1)
        act.wait_ge(lat_mm, 1)
        nc.scalar.activation(lat[:, :, :], ps[:, 4:6, :].rearrange("p a (t l) -> p (a t) l", l=LAT), ACT.Copy
                             ).then_inc(lat_ev, 1)

        def copy_qkT(n, b):
            for w in range(2):
                act.wait_ge(qkT_mm, 2 * n + w + 1)
                nc.scalar.activation(qkT[:, b % 2, w, :], ps[:, w, :], ACT.Copy).then_inc(qkT_ev, 1)

        def copy_pT(n, u):
            i = UNITS[u][0]
            act.wait_ge(pT_mm, NU * n + u + 1)
            nc.scalar.activation(probT[:, 1, 0:(i + 1) * P], ps[:, 5, 0:(i + 1) * P], ACT.Copy).then_inc(pT_ev[1], 1)

        def exp(n, b, u):
            i, j = UNITS[u]
            m = (i + 1) * P
            act.wait_ge(max_done, NU * n + u + 1)
            if u == 0:
                wait_past(act, recip, n - 1)
            nc.scalar.activation(prob[:, u % 4, 0:m], ps[:, 2 + j, 0:m], ACT.Exp, bias=negmax[:, u:u + 1],
                                 accum_out=den[:, b % 2, 2 * i + j:2 * i + j + 1]).then_inc(exp_done, 1)

        def copy_oT(n):
            act.wait_ge(oT_mm, n + 1)
            wait_past(act, y_mm, n)
            nc.scalar.activation(oT[:, :], m_ps, ACT.Copy).then_inc(oT_ev, 1)

        copy_qkT(0, 0)
        exp(0, 0, 0)
        exp(0, 0, 1)
        act.wait_ge(set_mm, 2)
        nc.scalar.activation(wvo[:, :, :], ps[:, 6:8, :].rearrange("p a (h n) -> p (a h) n", n=P),
                             ACT.Copy).then_inc(set_ev, 1)

        def step(n, b):
            copy_pT(n, 1)
            exp(n, b, 2)
            if not isinstance(n, int) or n > 0:
                copy_oT(n - 1)
            exp(n, b, 3)
            copy_pT(n, 3)
            exp(n, b, 4)
            exp(n, b, 5)
            copy_pT(n, 5)
            exp(n, b, 6)
            copy_qkT(n + 1, b + 1)
            exp(n, b, 7)
            copy_pT(n, 7)
            exp(n + 1, b + 1, 0)
            exp(n + 1, b + 1, 1)

        each(act, step)
        copy_oT(NI - 1)
        norm.scalar(act)

    @block.vector
    def _(dve):
        dve.wait_ge(w_ld, 16 * NWEIGHTS)
        nc.vector.tensor_scalar(wqk[:, :, 0:P], wqk[:, :, 0:P], SCALE, None, ALU.mult).then_inc(wq_scaled, 1)

        def rope_c(n):
            dve.wait_ge(qk_mm, n + 1)
            wait_past(dve, rope_add, n)
            nc.vector.tensor_tensor(qk_c[:, :, :].rearrange("p t (g d) -> p t g d", d=HD0),
                                    qk_ps.rearrange("p t (g d) -> p t g d", d=HD0),
                                    cos[:, :, None, :].broadcast_to([P, TPB, 4, HD0]), ALU.mult)

        def rope_s(n):
            h = HD0 // 2
            for a in (0, h):
                ins = nc.vector.tensor_tensor(
                    qk_s[:, :, :].rearrange("p t (g d) -> p t g d", d=HD0)[:, :, :, a:a + h],
                    qk_ps.rearrange("p t (g d) -> p t g d", d=HD0)[:, :, :, h - a:2 * h - a],
                    sin[:, :, None, a:a + h].broadcast_to([P, TPB, 4, h]), ALU.mult)
            ins.then_inc(rope_mul, 1)

        def rowmax(n, u):
            i, j = UNITS[u]
            dve.wait_ge(s_mm, NU * n + u + 1)
            nc.vector.tensor_reduce(negmax[:, u:u + 1], ps[:, 2 + j, 0:(i + 1) * P], AX.X, ALU.max,
                                    negate=True).then_inc(max_done, 1)

        def copy_pT(n, u):
            i = UNITS[u][0]
            dve.wait_ge(pT_mm, NU * n + u + 1)
            nc.vector.tensor_copy(probT[:, 0, 0:(i + 1) * P], ps[:, 4, 0:(i + 1) * P]).then_inc(pT_ev[0], 1)

        def normalise(n, b):
            dve.wait_ge(exp_done, NU * (n + 1))
            nc.vector.reciprocal(rden[:, :], den[:, b % 2, :]).then_inc(recip, 1)
            dve.wait_ge(recip, n + 1)
            dve.wait_ge(o_mm, n + 1)
            wait_past(dve, oT_mm, n)
            nc.vector.tensor_tensor(on[:, :, :].rearrange("p t (j d) -> p (t j) d", j=2),
                                    o_ps.rearrange("p (u d) -> p u d", u=NU),
                                    rden[:, :, None].broadcast_to([P, NU, LAT]), ALU.mult).then_inc(o_norm, 1)

        def add_y(n, b):
            dve.wait_ge(y_mm, n + 1)
            wait_past(dve, y_add, n - NB + 1)
            ts = slice(b * TPB, (b + 1) * TPB)
            nc.vector.tensor_tensor(x[:, ts, :], m_ps.rearrange("p (t d) -> p t d", d=D), x[:, ts, :],
                                    ALU.add).then_inc(y_add, 1)

        rope_c(0)
        rope_s(0)
        rowmax(0, 0)
        rowmax(0, 1)
        copy_pT(0, 0)
        dve.wait_ge(o_ld, 16 * (NLATER + 1))

        def step(n, b):
            rowmax(n, 2)
            rope_c(n + 1)
            rowmax(n, 3)
            copy_pT(n, 2)
            rope_s(n + 1)
            rowmax(n, 4)
            rowmax(n, 5)
            copy_pT(n, 4)
            if not isinstance(n, int) or n > 0:
                add_y(n - 1, (b - 1) % NB)
            rowmax(n, 6)
            rowmax(n, 7)
            copy_pT(n, 6)
            rowmax(n + 1, 0)
            rowmax(n + 1, 1)
            copy_pT(n + 1, 0)
            normalise(n, b)

        each(dve, step)
        add_y(NI - 1, NB - 1)
        nc.vector.scalar_tensor_tensor(router[:, :], keysT[:, :], 2.0, rwT[:, :], ALU.mult, ALU.add).then_inc(rt1, 1)
        nc.vector.tensor_tensor(keys2[:, :], keysT[:, :], keysT[:, :], ALU.mult).then_inc(rt1, 1)
        norm.vector(dve)
        dve.wait_ge(set_mm, 3)
        nc.vector.tensor_tensor(rbias[:, :], rbrow[:, :], ps[0:1, 4, 0:NE], ALU.subtract).then_inc(rt1, 1)
        dve.wait_ge(lg_mm, 1)
        nc.vector.tensor_copy(keep["logits"][:, :, :], ps[:, 5, 0:NT * NE].rearrange("p (t e) -> p t e", e=NE)
                              ).then_inc(lg_ev, 1)

    @block.tensor
    def _(pe):
        pe.wait_ge(w_ld, 16 * NWEIGHTS)
        for a in range(2):
            ins = nc.tensor.matmul(ps[:, a, :], wd[:, :], wkT[:, a * 512:(a + 1) * 512], start=True, stop=True)
        ins.then_inc(set_mm, 1)
        for n in range(NT):
            ins = nc.tensor.matmul(ps[:, 4 + n // 8, (n % 8) * LAT:(n % 8 + 1) * LAT],
                                   xT[:, n // TPB, (n % TPB) * P:(n % TPB + 1) * P], wdT[:, :], start=True, stop=True)
        ins.then_inc(lat_mm, 1)
        pe.wait_ge(set_ev, 1)
        pe.wait_ge(wq_scaled, 1)

        def project(n, b):
            wait_past(pe, qkT_ev, 2 * n)
            h = n // NB % NP0
            for t in range(TPB):
                ins = nc.tensor.matmul(qk_ps[:, t, :], xT[:, b, t * P:(t + 1) * P],
                                       wqk[:, bass.ds(h, 1), :].rearrange("p a n -> p (a n)"),
                                       start=True, stop=True)
            ins.then_inc(qk_mm, 1)

        def turn_qk(n):
            pe.wait_ge(rope_add, n + 1)
            for w in range(2):
                for t in range(TPB):
                    ins = nc.tensor.transpose(ps[:, w, t * P:(t + 1) * P], qk_r[:, t, w * P:(w + 1) * P],
                                              ident[:, :])
                ins.then_inc(qkT_mm, 1)

        def scores(n, b, u):
            i, j = UNITS[u]
            if u == 0:
                pe.wait_ge(qkT_ev, 2 * n + 2)
            wait_past(pe, exp_done, NU * n + u - 1)
            r = slice(64 * j, 64 * j + 64)
            nc.tensor.matmul(ps[:, 2 + j, 0:(i + 1) * P], qkT[r, b % 2, 0, i * P:(i + 1) * P],
                             qkT[r, b % 2, 1, 0:(i + 1) * P], start=True, stop=False, skip_group_check=True)
            nc.tensor.matmul(ps[:, 2 + j, i * P:(i + 1) * P], identb[:, :], cmask[:, :],
                             start=False, stop=True, skip_group_check=True).then_inc(s_mm, 1)

        def turn_p(n, u):
            i, j = UNITS[u]
            pe.wait_ge(exp_done, NU * n + u + 1)
            wait_past(pe, pT_ev[j], 4 * n + u // 2)
            for t in range(i + 1):
                ins = nc.tensor.transpose(ps[:, 4 + j, t * P:(t + 1) * P], prob[:, u % 4, t * P:(t + 1) * P],
                                          ident[:, :])
            ins.then_inc(pT_mm, 1)

        def values(n, b, u):
            i, j = UNITS[u]
            pe.wait_ge(pT_ev[j], 4 * n + u // 2 + 1)
            if u == 0:
                wait_past(pe, o_norm, n)
            c = 64 * (2 * i + j)
            for t in range(i + 1):
                ins = nc.tensor.matmul(o_ps[:, c:c + 64], probT[:, j, t * P:(t + 1) * P], lat[:, b * TPB + t, :],
                                       start=(t == 0), stop=(t == i))
            if u == NU - 1:
                ins.then_inc(o_mm, 1)

        def turn_o(n):
            pe.wait_ge(o_norm, n + 1)
            wait_past(pe, y_add, n)
            for t in range(TPB):
                ins = nc.tensor.transpose(m_ps[:, t * P:(t + 1) * P], on[:, t, :], ident[:, :])
            ins.then_inc(oT_mm, 1)

        def output(n):
            h = n // NB
            pe.wait_ge(oT_ev, n + 1)
            for t in range(TPB):
                ins = nc.tensor.matmul(m_ps[:, t * P:(t + 1) * P], oT[:, t * P:(t + 1) * P],
                                       wvo[:, bass.ds(h, 1), :].rearrange("p a n -> p (a n)"),
                                       start=True, stop=True)
            ins.then_inc(y_mm, 1)

        project(0, 0)
        turn_qk(0)
        scores(0, 0, 0)
        scores(0, 0, 1)
        pe.wait_ge(o_ld, 16 * (NLATER + 1))
        for h in range(NP0):
            for j in range(2):
                r = slice(64 * j, 64 * j + 64)
                ins = nc.tensor.matmul(ps[r, 6 + h // 4, (h % 4) * P:(h % 4 + 1) * P], wv[r, h, :], woT[r, h, :],
                                       start=True, stop=True)
        ins.then_inc(set_mm, 1)
        pe.wait_ge(lat_ev, 1)
        turn_p(0, 0)
        pe.wait_ge(set_ev, 2)

        def step(n, b):
            past = not isinstance(n, int) or n > 0
            scores(n, b, 2)
            turn_p(n, 1)
            project(n + 1, (b + 1) % NB)
            values(n, b, 0)
            if past:
                turn_o(n - 1)

            scores(n, b, 3)
            turn_p(n, 2)
            values(n, b, 1)
            if past:
                output(n - 1)

            scores(n, b, 4)
            turn_p(n, 3)
            values(n, b, 2)

            scores(n, b, 5)
            turn_p(n, 4)
            values(n, b, 3)

            scores(n, b, 6)
            turn_p(n, 5)
            values(n, b, 4)
            turn_qk(n + 1)

            scores(n, b, 7)
            turn_p(n, 6)
            values(n, b, 5)

            scores(n + 1, b + 1, 0)
            turn_p(n, 7)
            values(n, b, 6)

            scores(n + 1, b + 1, 1)
            values(n, b, 7)
            turn_p(n + 1, 0)

        each(pe, step)
        turn_o(NI - 1)
        output(NI - 1)
        norm.tensor(pe)
        pe.wait_ge(rt1, 2)
        pe.wait_ge(ones_set, 1)
        nc.tensor.matmul(ps[0:1, 4, 0:NE], ones[:, 0:1], keys2[:, :], start=True, stop=True).then_inc(set_mm, 1)
        pe.wait_ge(rt1, 3)
        for n in range(NT):
            if n % TPB == 0:
                pe.wait_ge(norm.turn_ev, n // TPB + 1)
            c = slice(n * NE, (n + 1) * NE)
            nc.tensor.matmul(ps[:, 5, c], xT[:, n // TPB, (n % TPB) * P:(n % TPB + 1) * P], router[:, :],
                             start=True, stop=False)
            ins = nc.tensor.matmul(ps[:, 5, c], ones[0:1, :], rbias[:, :], start=False, stop=True)
        ins.then_inc(lg_mm, 1)


def experts0(nc, ctx, io, keep):

    def sb(name, shape, dt=F32):
        return ctx.enter_context(nc.sbuf_tensor("m_" + name, shape, dt))

    def sem(name):
        return nc.alloc_semaphore("m_" + name)

    ps = keep["ps"]

    pre = keep["pre"]
    w1, w2, b2, iota = pre.w1, pre.w2, pre.b2, pre.iota
    w1p = sb("w1p", [P, 2, 2, FF], F32R)
    w2p = sb("w2p", [P, 2, 2, FB, D], F32R)
    xp = sb("xp", [P, 2, NB, S], F32R)
    gates_d = nc.dram_tensor("m_gates_d", (NE, NB * S), F32).ap()
    gate_all = sb("gate_all", [P, 2, NB * S])
    gated = sb("gated", [P, 2, S])
    top = sb("top", [P, NT, 8])
    topi = sb("topi", [P, NT, 8], mybir.dt.uint32)
    topf = sb("topf", [P, NT, TOPK])
    tops = sb("tops", [P, NT, TOPK])
    tope = sb("tope", [P, NT, TOPK])
    topz = sb("topz", [P, NT])
    topr = sb("topr", [P, NT])
    topw = sb("topw", [P, NT, TOPK])
    hit = sb("hit", [P, NT, TOPK, NE])
    hitw = sb("hitw", [P, NT, TOPK, NE])
    gates = sb("gates", [P, NT, NE])
    gatesT = sb("gatesT", [NE, NB * S])
    hid = sb("hid", [P, 2, FB, S])
    hidp = sb("hidp", [P, 2, 2, FB, S], F32R)
    x, xT, logits, ident = keep["x"], keep["xT"], keep["logits"], keep["ident"]

    w1_ld = [sem(f"w1_ld{k}") for k in range(2)]
    w2_ld = [sem(f"w2_ld{k}") for k in range(2)]
    g_st = sem("g_st")
    g_ld = [sem(f"g_ld{k}") for k in range(2)]
    mul_done = sem("mul_done")
    x_mm = sem("x_mm")
    x_ev = sem("x_ev")
    top_done = sem("top_done")
    topi_done = sem("topi_done")
    gate_step = sem("gate_step")
    top_exp = sem("top_exp")
    gT_mm = sem("gT_mm")
    gT_ev = sem("gT_ev")
    b2_mm = sem("b2_mm")
    b2_add = sem("b2_add")
    w_split = sem("w_split")
    held = sem("held")
    x_high = sem("x_high")
    x_low = sem("x_low")
    high_done = sem("high_done")
    low_done = sem("low_done")
    up_mm = sem("up_mm")
    gelu_done = sem("gelu_done")
    down_mm = sem("down_mm")
    acc_done = sem("acc_done")
    STEPS = NE * NB
    norm = Norm(nc, ctx, keep, ps, [0, 1, 2, 3], x_ev, [1, 2, 3, 4], "mn_")

    block = ctx.enter_context(nc.Block())

    @block.sync
    def _(sp):
        def spread(e, k):
            sp.dma_start(gate_all[:, k, :], gates_d[bass.ds(e, 1), :].broadcast_to([P, NB * S])).then_inc(g_ld[k], 16)

        sp.wait_ge(gT_ev, NB)
        sp.dma_start(gates_d, gatesT[:, :]).then_inc(g_st, 16)
        sp.wait_ge(g_st, 16)
        for k in range(2):
            spread(k, k)
        with sp.Fori(1, NE // 2) as pair:
            for k in range(2):
                e = pair * 2 + k
                sp.wait_ge(gelu_done, FB * NB * (e - 1))
                sp.sem_inc(held, 1)
                sp.wait_ge(w_split, 4 * (e - 1))
                sp.sem_inc(held, 1)
                sp.dma_start(w1[:, k, :], io["w1T"][:, bass.ds(e, 1), :].rearrange("d a f -> d (a f)")
                             ).then_inc(w1_ld[k], 16)
                sp.dma_start(w2[:, k, :, :], io["w2T"][:, bass.ds(e * FB, FB), :]).then_inc(w2_ld[k], 16)
                sp.wait_ge(acc_done, NB * (e - 1) + NB)
                sp.sem_inc(held, 1)
                spread(e, k)

    @block.gpsimd
    def _(pool):
        def split(e, k):
            wait_past(pool, w1_ld[k], 16 * (e // 2))
            wait_past(pool, up_mm, FB * NB * (e - 1))
            pool.sem_inc(held, 1)
            nc.gpsimd.tensor_copy(w1p[:, k, 0, :], w1[:, k, 0:FF]).then_inc(w_split, 1)
            pool.wait_ge(w_split, 4 * e + 1)
            nc.gpsimd.tensor_tensor(w1p[:, k, 1, :], w1[:, k, 0:FF], w1p[:, k, 0, :], ALU.subtract
                                    ).then_inc(w_split, 1)
            wait_past(pool, w2_ld[k], 16 * (e // 2))
            wait_past(pool, down_mm, NB * (e - 1))
            pool.sem_inc(held, 1)
            nc.gpsimd.tensor_copy(w2p[:, k, 0, :, :], w2[:, k, :, :]).then_inc(w_split, 1)
            pool.wait_ge(w_split, 4 * e + 3)
            nc.gpsimd.tensor_tensor(w2p[:, k, 1, :, :], w2[:, k, :, :], w2p[:, k, 0, :, :], ALU.subtract
                                    ).then_inc(w_split, 1)

        split(0, 0)
        split(1, 1)
        with pool.Fori(1, NE // 2) as pair:
            for k in range(2):
                split(pair * 2 + k, k)
        pool.wait_ge(w_split, 4 * NE)
        pool.sem_inc(w_split, 2)
        norm.pool(pool)

    @block.scalar
    def _(act):
        for b in range(NB):
            nc.scalar.activation(xp[:, 0, b, :], xT[:, b, :], ACT.Copy).then_inc(x_high, 1)
        act.wait_ge(x_low, NB)

        def gelus(n, c, k):
            def high(f):
                act.wait_ge(gelu_done, n * FB + f + 1)
                nc.scalar.activation(hidp[:, c % 2, 0, f, :], hid[:, c % 2, f, :], ACT.Copy).then_inc(high_done, 1)

            for f in range(FB):
                act.wait_ge(up_mm, n * FB + f + 1)
                act.wait_ge(low_done, n * FB + f + 1)
                nc.scalar.activation(hid[:, c % 2, f, :], ps[:, f, :], ACT.Gelu, bias=w1[:, k, FF + f:FF + f + 1]
                                     ).then_inc(gelu_done, 1)
                if f:
                    high(f - 1)
            high(FB - 1)

        gelus(0, 0, 0)
        act.wait_ge(gate_step, 2)
        nc.scalar.activation(tope[:, :, :], tops[:, :, :], ACT.Exp).then_inc(top_exp, 1)
        for b in range(NB):
            act.wait_ge(gT_mm, b + 1)
            nc.scalar.activation(gatesT[:, b * S:(b + 1) * S], ps[0:NE, 4 + b, :], ACT.Copy).then_inc(gT_ev, 1)
        with act.Fori(0, NE // 2) as pair:
            for k in range(2):
                for c in range(NB):
                    n = pair * (2 * NB) + (k * NB + c)
                    gelus(n + 1, (c + 1) % NB, (k + (c + 1) // NB) % 2)
        for b in range(NB):
            act.wait_ge(x_mm, b + 1)
            nc.scalar.activation(x[:, b * TPB:(b + 1) * TPB, :], ps[:, 4 + b, :].rearrange("p (t d) -> p t d", d=D),
                                 ACT.Copy).then_inc(x_ev, 1)
        norm.scalar(act)

    @block.vector
    def _(dve):
        for b in range(NB):
            dve.wait_ge(x_high, b + 1)
            nc.vector.tensor_tensor(xp[:, 1, b, :], xT[:, b, :], xp[:, 0, b, :], ALU.subtract
                                          ).then_inc(x_low, 1)
        nc.vector.memset(gates[:, 0, 0:1], 0.0).then_inc(low_done, 2 * FB)

        def lows(n, c):
            for f in range(FB):
                dve.wait_ge(high_done, n * FB + f + 1)
                nc.vector.tensor_tensor(hidp[:, c % 2, 1, f, :], hid[:, c % 2, f, :], hidp[:, c % 2, 0, f, :],
                                        ALU.subtract).then_inc(low_done, 1)

        for t in range(NT):
            nc.vector.max(top[:, t, :], logits[:, t, :]).then_inc(top_done, 1)
        for t in range(NT):
            dve.wait_ge(top_done, t + 1)
            nc.vector.max_index(topi[:, t, :], top[:, t, :], logits[:, t, :]).then_inc(topi_done, 1)
        dve.wait_ge(topi_done, NT)
        nc.vector.tensor_copy(topf[:, :, :], topi[:, :, 0:TOPK]).then_inc(gate_step, 1)
        nc.vector.tensor_tensor(tops[:, :, :], top[:, :, 0:TOPK], top[:, :, 0:1].broadcast_to([P, NT, TOPK]),
                                ALU.subtract).then_inc(gate_step, 1)
        dve.wait_ge(gate_step, 1)
        nc.vector.tensor_tensor(hit[:, :, :, :], topf[:, :, :, None].broadcast_to([P, NT, TOPK, NE]),
                                iota[:, None, None, :].broadcast_to([P, NT, TOPK, NE]), ALU.is_equal
                                ).then_inc(gate_step, 1)
        dve.wait_ge(top_exp, 1)
        nc.vector.tensor_reduce(topz[:, :], tope[:, :, :], AX.X, ALU.add).then_inc(gate_step, 1)
        dve.wait_ge(gate_step, 4)
        nc.vector.reciprocal(topr[:, :], topz[:, :]).then_inc(gate_step, 1)
        dve.wait_ge(gate_step, 5)
        nc.vector.tensor_tensor(topw[:, :, :], tope[:, :, :], topr[:, :, None].broadcast_to([P, NT, TOPK]),
                                ALU.mult).then_inc(gate_step, 1)
        dve.wait_ge(gate_step, 6)
        nc.vector.tensor_tensor(hitw[:, :, :, :], hit[:, :, :, :], topw[:, :, :, None].broadcast_to([P, NT, TOPK, NE]),
                                ALU.mult).then_inc(gate_step, 1)
        dve.wait_ge(gate_step, 7)
        nc.vector.tensor_reduce(gates[:, :, :], hitw[:, :, :, :].rearrange("p t k e -> p t e k"), AX.X, ALU.add
                                ).then_inc(gate_step, 1)
        nc.vector.memset(gated[:, 1, 0:1], 0.0).then_inc(acc_done, NB)
        nc.vector.memset(gated[:, 0, 0:1], 0.0).then_inc(mul_done, 2)
        lows(0, 0)
        with dve.Fori(0, NE // 2) as pair:
            for k in range(2):
                for c in range(NB):
                    n = pair * (2 * NB) + (k * NB + c)
                    lows(n + 1, (c + 1) % NB)
                    if c == 0:
                        dve.wait_ge(g_ld[k], 16 * (pair + 1))
                    dve.wait_ge(down_mm, n + 1)
                    dve.wait_ge(acc_done, n + NB - 1)
                    nc.vector.tensor_tensor(gated[:, c % 2, :], ps[:, 4 + c % 2, :],
                                            gate_all[:, k, c * S:(c + 1) * S], ALU.mult).then_inc(mul_done, 1)
                    dve.wait_ge(mul_done, n + 3)
                    nc.vector.tensor_tensor(xT[:, c, :], xT[:, c, :], gated[:, c % 2, :], ALU.add
                                            ).then_inc(acc_done, 1)
        dve.wait_ge(acc_done, NB + STEPS)
        for b in range(NB):
            dve.wait_ge(b2_mm, b + 1)
            nc.vector.tensor_tensor(xT[:, b, :], ps[:, 4 + b, :], xT[:, b, :], ALU.add).then_inc(b2_add, 1)
        norm.vector(dve)

    @block.tensor
    def _(pe):
        passes = ((0, 0), (1, 0), (0, 1))

        def up(n, c, k):
            for f in range(FB):
                wait_past(pe, gelu_done, n * FB - FB + f + 1 if not isinstance(n, int) else 0)
                for i, (a, b) in enumerate(passes):
                    ins = nc.tensor.matmul(ps[:, f, :], w1p[:, k, a, f * P:(f + 1) * P], xp[:, b, c, :],
                                           start=(i == 0), stop=(i == 2))
                ins.then_inc(up_mm, 1)

        pe.wait_ge(x_low, NB)
        pe.wait_ge(w_split, 2)
        up(0, 0, 0)
        pe.wait_ge(gate_step, 8)
        for b in range(NB):
            for t in range(TPB):
                ins = nc.tensor.transpose(ps[0:NE, 4 + b, t * P:(t + 1) * P], gates[:, b * TPB + t, :], ident[:, :])
            ins.then_inc(gT_mm, 1)
        pe.wait_ge(gT_ev, NB)
        with pe.Fori(0, NE // 2) as pair:
            for k in range(2):
                e = pair * 2 + k
                for c in range(NB):
                    n = pair * (2 * NB) + (k * NB + c)
                    if c == NB - 1:
                        pe.wait_ge(w_split, 4 * (e + 1) + 2)
                        up(n + 1, 0, 1 - k)
                    else:
                        up(n + 1, c + 1, k)
                    if c == 0:
                        pe.wait_ge(w_split, 4 * (e + 1))
                    pe.wait_ge(low_done, (n + 1) * FB + 2 * FB)
                    pe.wait_ge(mul_done, n + 1)
                    for f in range(FB):
                        for i, (a, b) in enumerate(passes):
                            ins = nc.tensor.matmul(ps[:, 4 + c % 2, :], w2p[:, k, a, f, :], hidp[:, c % 2, b, f, :],
                                                   start=(f == 0 and i == 0), stop=(f == FB - 1 and i == 2))
                    ins.then_inc(down_mm, 1)
        pe.wait_ge(acc_done, NB + STEPS)
        for b in range(NB):
            nc.tensor.matmul(ps[:, 4 + b, :], b2[:, :], gatesT[:, b * S:(b + 1) * S], start=True, stop=True
                             ).then_inc(b2_mm, 1)
        for b in range(NB):
            pe.wait_ge(b2_add, b + 1)
            for t in range(TPB):
                ins = nc.tensor.transpose(ps[:, 4 + b, t * P:(t + 1) * P], xT[:, b, t * P:(t + 1) * P], ident[:, :])
            ins.then_inc(x_mm, 1)
        pe.wait_ge(gelu_done, FB * (STEPS + 1))
        norm.tensor(pe)


def attention1(nc, ctx, io, keep):

    def sb(name, shape, dt=F32):
        return ctx.enter_context(nc.sbuf_tensor("c_sb_" + name, shape, dt))

    def sem(name):
        return nc.alloc_semaphore("c_" + name)

    ps = keep["ps"]
    parts_d = nc.dram_tensor("c_parts_d", (NB, 2, 3 * HD1, NH1 * S), BF16).ap()
    shift_d = nc.dram_tensor("c_shift_d", (NB * QUADS, NSH, 4 * S), BF16).ap()

    shT_ps = ps[:, 7, :].bitcast(BF16)[0:NSH * 4, 0:S]

    pre = keep["pre"]
    q32 = pre.w2[:, :, :, :].rearrange("p w f d -> p w (f d)")
    r32 = pre.w1[:, :, 0:S]
    wq, wk, wv, rot, identb = pre.wq, pre.wk, pre.wv, pre.rot, pre.identb
    sq = sb("sq", [P, 2, NH1, S], BF16)
    sk = sb("sk", [P, 2, NH1, S], BF16)
    v_all = sb("v_all", [P, NT, P])
    v1 = sb("v1", [P, TPB, 4, 32])
    negmax = sb("negmax", [P, TPB, 4])
    shr = sb("shr", [P, TPB, 4])
    shp = sb("shp", [P, TPB, NSH, 4], BF16)
    shT = sb("shT", [NSH * 4, S], BF16)
    pT = sb("pT", [P, 2, 4, TPB, S])
    parts = pT[:, 1, :, :, :].rearrange("p g t s -> p (g t s)").bitcast(BF16)[:, 0:2 * 2 * 3 * S]\
        .rearrange("p (b w a s) -> p b w a s", b=2, w=2, a=3)
    oT = sb("oT", [P, S])
    rcp = sb("rcp", [P, TPB, 4])
    att = sb("att", [P, TPB, 4, HD1])
    x, xT, ident = keep["x"], keep["xT"], keep["ident"]

    sq_zero = sem("sq_zero")
    sk_one = sem("sk_one")
    v1_init = sem("v1_init")
    v_mm = sem("v_mm")
    v_ev = sem("v_ev")
    qk_mm = sem("qk_mm")
    part_a = sem("part_a")
    part_b = sem("part_b")
    parts_st = [sem(f"parts_st{k}") for k in range(4)]
    stack_ld = sem("stack_ld")
    max_free = sem("max_free")
    max_mm = sem("max_mm")
    shift_step = sem("shift_step")
    shift_mm = sem("shift_mm")
    shift_ev = sem("shift_ev")
    shift_st = sem("shift_st")
    shift_ld = sem("shift_ld")
    exp_free = sem("exp_free")
    st_mm = sem("st_mm")
    v1_done = sem("v1_done")
    pv_mm = sem("pv_mm")
    oT_ev = sem("oT_ev")
    oT_mm = sem("oT_mm")
    rcp_done = sem("rcp_done")
    att_done = sem("att_done")
    x_add = sem("x_add")
    held = sem("held")
    NQ = NB * QUADS
    SCALE = HD1 ** -0.5
    norm = Norm(nc, ctx, keep, ps, [0, 1, 2, 3], x_add, [QUADS * (b + 1) for b in range(NB)], "cn_")

    block = ctx.enter_context(nc.Block())

    def each_quad(eng, step):
        for m in range(2):
            step(m, m)
        with eng.Fori(1, NQ // 2 - 1) as pair:
            for k in range(2):
                step(pair * 2 + k, k)
        for k in range(2):
            step(NQ - 2 + k, k)

    def known(m, below):
        return isinstance(m, int) and m < below

    def stack(queue, b):
        for a in range(3):
            for c in range(3):
                r = (3 * a + c) * HD1
                queue.dma_start(sq[r:r + HD1, bass.ds(b % 2, 1), :, :].rearrange("r a h n -> r (a h n)"),
                             parts_d[bass.ds(b, 1), 0, a * HD1:(a + 1) * HD1, :].rearrange("b r n -> (b r) n")
                             ).then_inc(stack_ld, 16)
            r = 3 * a * HD1
            queue.dma_start(sk[r:r + 3 * HD1, bass.ds(b % 2, 1), :, :].rearrange("r a h n -> r (a h n)"),
                         parts_d[bass.ds(b, 1), 1, :, :].rearrange("b r n -> (b r) n")).then_inc(stack_ld, 16)

    @block.sync
    def _(sp):
        def store_parts(b):
            for w in range(2):
                sp.wait_ge(part_b, 3 * (2 * b + w + 1))
                sp.dma_start(parts_d[b, w].rearrange("(a d) (h n) -> (d h) a n", a=3, h=NH1), parts[:, b % 2, w, :, :]
                             ).then_inc(parts_st[2 * (b % 2) + w], 16)

        def shift(m):
            sp.wait_ge(shift_ev, m + 1)
            sp.sem_inc(held, 1)
            sp.dma_start(shift_d[bass.ds(m, 1)].rearrange("b a (h n) -> (b a h) n", h=4), shT[:, :]
                         ).then_inc(shift_st, 16)
            sp.wait_ge(shift_st, 16 * (m + 1))
            sp.sem_inc(held, 1)
            sp.dma_start(sq[KS:KS + NSH, bass.ds(m // QUADS % 2, 1), bass.ds(m % QUADS * 4, 4), :]
                         .rearrange("r a h n -> r (a h n)"),
                         shift_d[bass.ds(m, 1)].rearrange("b a n -> (b a) n")).then_inc(shift_ld, 16)

        store_parts(0)
        store_parts(1)
        sp.wait_ge(parts_st[0], 16)
        sp.wait_ge(parts_st[1], 16)
        sp.wait_ge(sq_zero, 1)
        sp.wait_ge(sk_one, 1)
        stack(sp, 0)
        for b in range(2, NB):
            store_parts(b)
        for k in range(4):
            sp.wait_ge(parts_st[k], 16 * NB // 2)
        sp.wait_ge(stack_ld, 192)
        stack(sp, 1)
        for m in range(QUADS + 1):
            shift(m)
        with sp.Fori(1, NB - 1) as b:
            sp.wait_ge(st_mm, NH1 * TPB * b)
            sp.sem_inc(held, 1)
            sp.wait_ge(stack_ld, 192 * (b + 1))
            sp.sem_inc(held, 1)
            stack(sp, b + 1)
            for q in range(QUADS):
                shift(b * QUADS + q + 1)
        for q in range(QUADS - 1):
            shift(NQ - QUADS + q + 1)

    @block.gpsimd
    def _(pool):
        nc.gpsimd.memset(sk[:, :, :, :], 1.0).then_inc(sk_one, 1)
        nc.gpsimd.memset(v1[:, :, :, :], 0.0).then_inc(v1_init, 1)
        pool.wait_ge(v1_init, 1)
        nc.gpsimd.memset(v1[:, :, :, HD1:HD1 + 1], 1.0).then_inc(v1_init, 1)
        pool.wait_ge(v1_init, 2)
        pool.wait_ge(v_ev, NB)

        def step(m, k):
            wait_past(pool, pv_mm, m)
            nc.gpsimd.tensor_copy(v1[:, :, :, 0:HD1],
                                  v_all[:, bass.ds(m // QUADS * TPB, TPB), bass.ds(m % QUADS * 4 * HD1, 4 * HD1)]
                                  .rearrange("p t (g d) -> p t g d", g=4)).then_inc(v1_done, 1)
            if not known(m, 2):
                add(m - 2)

        def add(m):
            pool.wait_ge(att_done, m + 1)
            xs = x[:, bass.ds(m // QUADS * TPB, TPB), bass.ds(m % QUADS * 4 * HD1, 4 * HD1)]
            nc.gpsimd.tensor_tensor(xs, xs, att[:, :, :, :].rearrange("p t g d -> p t (g d)"), ALU.add
                                    ).then_inc(x_add, 1)

        each_quad(pool, step)
        add(NQ - 2)
        add(NQ - 1)
        norm.pool(pool)

    @block.scalar
    def _(act):
        nc.scalar.activation(oT[:, 0:1], rot[:, 0:1], ACT.Copy).then_inc(exp_free, 2)
        for b in range(NB):
            act.wait_ge(v_mm, b + 1)
            nc.scalar.activation(v_all[:, b * TPB:(b + 1) * TPB, :].rearrange("p t d -> p (t d)"), ps[:, 4 + b, :],
                                 ACT.Copy).then_inc(v_ev, 1)
        for n in range(2 * NB):
            b, w = n // 2, n % 2
            act.wait_ge(qk_mm, n + 1)
            if n >= 2:
                act.wait_ge(part_b, 3 * (n - 1))
            if b >= 2:
                act.wait_ge(parts_st[2 * (b % 2) + w], 16 * (b // 2))
            nc.scalar.activation(q32[:, w, :], ps[:, n, :], ACT.Copy, scale=rot[:, b:b + 1]).then_inc(part_a, 1)
            act.wait_ge(part_a, 2 * n + 1)
            nc.scalar.activation(parts[:, b % 2, w, 0, :], q32[:, w, :], ACT.Copy).then_inc(part_a, 1)

        def exps(m, k, g):
            for t in range(TPB):
                act.wait_ge(st_mm, (m * 4 + g) * TPB + t + 1)
                nc.scalar.activation(pT[:, k, g, t, :], ps[:, 4 + t % 2, :], ACT.Exp, scale=SCALE).then_inc(exp_free, 1)

        def copy_shift(m):
            act.wait_ge(shift_mm, m + 1)
            wait_past(act, shift_st, 16 * m)
            nc.scalar.activation(shT[:, :], shT_ps, ACT.Copy).then_inc(shift_ev, 1)

        def copy_o(m):
            act.wait_ge(pv_mm, m + 1)
            wait_past(act, oT_mm, m)
            nc.scalar.activation(oT[:, :], ps[:, 6, :], ACT.Copy).then_inc(oT_ev, 1)

        for k in range(4):
            act.wait_ge(parts_st[k], 16 * NB // 2)
        copy_shift(0)

        def step(m, k):
            wait_past(act, pv_mm, m - 1)
            exps(m, k, 0)
            if not isinstance(m, int) or m < NQ - 1:
                copy_shift(m + 1)
            exps(m, k, 1)
            exps(m, k, 2)
            exps(m, k, 3)
            if not known(m, 1):
                copy_o(m - 1)

        each_quad(act, step)
        copy_o(NQ - 1)
        norm.scalar(act)

    @block.vector
    def _(dve):
        nc.vector.memset(sq[:, :, :, :], 0.0).then_inc(sq_zero, 1)
        for n in range(2 * NB):
            b, w = n // 2, n % 2
            dve.wait_ge(part_a, 2 * n + 2)
            nc.vector.tensor_tensor(r32[:, w, :], q32[:, w, :], parts[:, b % 2, w, 0, :], ALU.subtract).then_inc(part_b, 1)
            dve.wait_ge(part_b, 3 * n + 1)
            nc.vector.tensor_copy(parts[:, b % 2, w, 1, :], r32[:, w, :]).then_inc(part_b, 1)
            dve.wait_ge(part_b, 3 * n + 2)
            nc.vector.tensor_tensor(parts[:, b % 2, w, 2, :], r32[:, w, :], parts[:, b % 2, w, 1, :], ALU.subtract
                                    ).then_inc(part_b, 1)
        nc.vector.memset(negmax[:, 0, 0:1], 0.0).then_inc(max_free, 2)

        def maxima(m, g):
            for i in range(2):
                dve.wait_ge(max_mm, 2 * (4 * m + g) + i + 1)
                nc.vector.tensor_reduce(negmax[:, 2 * i:2 * i + 2, g], ps[:, 2 * i:2 * i + 2, :], AX.X, ALU.max,
                                        negate=True).then_inc(max_free, 1)

        def shift(m):
            dve.wait_ge(max_free, 2 + 8 * (m + 1))
            wait_past(dve, shift_mm, m)
            nc.vector.tensor_copy(shp[:, :, 0, :], negmax[:, :, :]).then_inc(shift_step, 1)
            dve.wait_ge(shift_step, 4 * m + 1)
            nc.vector.tensor_tensor(shr[:, :, :], negmax[:, :, :], shp[:, :, 0, :], ALU.subtract
                                    ).then_inc(shift_step, 1)
            dve.wait_ge(shift_step, 4 * m + 2)
            nc.vector.tensor_copy(shp[:, :, 1, :], shr[:, :, :]).then_inc(shift_step, 1)
            dve.wait_ge(shift_step, 4 * m + 3)
            nc.vector.tensor_tensor(shp[:, :, 2, :], shr[:, :, :], shp[:, :, 1, :], ALU.subtract
                                    ).then_inc(shift_step, 1)

        def normalise(m):
            dve.wait_ge(oT_mm, m + 1)
            wait_past(dve, x_add, m)
            o4 = ps[:, 7, :].rearrange("p (t g c) -> p t g c", t=TPB, g=4)
            nc.vector.reciprocal(rcp[:, :, :], o4[:, :, :, HD1]).then_inc(rcp_done, 1)
            dve.wait_ge(rcp_done, m + 1)
            nc.vector.tensor_tensor(att[:, :, :, :], o4[:, :, :, 0:HD1],
                                    rcp[:, :, :, None].broadcast_to([P, TPB, 4, HD1]), ALU.mult
                                    ).then_inc(att_done, 1)

        for m in range(2):
            for g in range(4):
                maxima(m, g)
            shift(m)

        def step(m, k):
            for g in range(4):
                if not isinstance(m, int) or m < NQ - 2:
                    maxima(m + 2, g)
                if g == 2 and not known(m, 2):
                    normalise(m - 2)
            if not isinstance(m, int) or m < NQ - 2:
                shift(m + 2)

        each_quad(dve, step)
        normalise(NQ - 2)
        normalise(NQ - 1)
        norm.vector(dve)

    @block.tensor
    def _(pe):
        for b in range(NB):
            for t in range(TPB):
                ins = nc.tensor.matmul(ps[:, 4 + b, t * P:(t + 1) * P], xT[:, b, t * P:(t + 1) * P],
                                       wv[:, :], start=True, stop=True)
            ins.then_inc(v_mm, 1)
        for n in range(2 * NB):
            b, w = n // 2, n % 2
            if n >= NB:
                pe.wait_ge(v_ev, n - NB + 1)
            nc.tensor.matmul(ps[:, n, :], (wq, wk)[w][:, :], xT[:, b, :], start=True, stop=True
                             ).then_inc(qk_mm, 1)

        def stacked(tile, m, g, rows, cols):
            return tile[0:rows, bass.ds(m // QUADS % 2, 1), bass.ds(m % QUADS * 4 + g, 1), cols]\
                .rearrange("r a h n -> r (a h n)")

        def max_scores(m, g, half):
            pe.wait_ge(max_free, 2 * (4 * m + g) + half + 1)
            for i in range(2 * half, 2 * half + 2):
                ins = nc.tensor.matmul(ps[:, i, :], stacked(sq, m, g, KS, slice(i * P, (i + 1) * P)),
                                       stacked(sk, m, g, KS, slice(0, S)), start=True, stop=True)
            ins.then_inc(max_mm, 1)

        def exp_scores(m, g, half):
            for t in range(2 * half, 2 * half + 2):
                pe.wait_ge(exp_free, (4 * m + g) * TPB + t + 1)
                nc.tensor.matmul(ps[:, 4 + t % 2, :], stacked(sk, m, g, P, slice(t * P, (t + 1) * P)),
                                 stacked(sq, m, g, P, slice(0, S)), start=True, stop=True).then_inc(st_mm, 1)

        def turn_shift(m):
            pe.wait_ge(shift_step, 4 * (m + 1))
            wait_past(pe, att_done, m - 3)
            wait_past(pe, shift_ev, m)
            pe.sem_inc(held, 1)
            for i in range(TPB):
                ins = nc.tensor.transpose(shT_ps[:, i * P:(i + 1) * P],
                                          shp[:, i, :, :].rearrange("p a h -> p (a h)"), identb[:, :])
            ins.then_inc(shift_mm, 1)

        def sums(m, k, t):
            if t == 0:
                pe.wait_ge(v1_done, m + 1)
                wait_past(pe, oT_ev, m)
                pe.wait_ge(exp_free, 2 + 4 * TPB * (m + 1))
            for g in range(4):
                ins = nc.tensor.matmul(ps[32 * g:32 * g + 32, 6, :], v1[:, t, g, :], pT[:, k, g, t, :],
                                       start=(t == 0), stop=(t == TPB - 1), skip_group_check=True)
            if t == TPB - 1:
                ins.then_inc(pv_mm, 1)

        def turn_o(m):
            pe.wait_ge(oT_ev, m + 1)
            wait_past(pe, att_done, m)
            pe.wait_ge(shift_ev, m + 4 if not isinstance(m, int) or m < NQ - 4 else NQ)
            for i in range(TPB):
                ins = nc.tensor.transpose(ps[:, 7, i * P:(i + 1) * P], oT[:, i * P:(i + 1) * P], ident[:, :])
            ins.then_inc(oT_mm, 1)

        pe.wait_ge(part_a, 2 * NB)
        pe.wait_ge(stack_ld, 192)
        for m in range(2):
            for g in range(4):
                for half in range(2):
                    max_scores(m, g, half)
            if m == 0:
                pe.wait_ge(part_a, 4 * NB)
                turn_shift(0)

        def step(m, k):
            early = not isinstance(m, int) or m < NQ - 2
            if early:
                pe.wait_ge(stack_ld, 192 * ((m + 2) // QUADS + 1))
            pe.wait_ge(shift_ld, 16 * (m + 1))
            for g in range(4):
                for half in range(2):
                    if early:
                        max_scores(m + 2, g, half)
                    exp_scores(m, g, half)
                if g == 0 and (not isinstance(m, int) or m < NQ - 1):
                    turn_shift(m + 1)
                if g == 1 and not known(m, 2):
                    turn_o(m - 2)
                if not known(m, 1):
                    sums(m - 1, 1 - k, g)

        each_quad(pe, step)
        turn_o(NQ - 2)
        for t in range(TPB):
            sums(NQ - 1, 1, t)
        turn_o(NQ - 1)
        norm.tensor(pe)


def local_attention(nc, ctx, io, keep, layer):

    def head(k, i):
        return 4 * (k // 2) + 2 * i + k % 2

    def keys(t):
        return slice(0 if t else WIN, KEYS)

    def sb(name, shape, dt=F32):
        return ctx.enter_context(nc.sbuf_tensor(f"l{layer}_sb_" + name, shape, dt))

    def sem(name):
        return nc.alloc_semaphore(f"l{layer}_" + name)

    ps = keep["ps"]
    o_ps = ps[:, 6, :]
    m_ps = ps[:, 7, :]
    PAIRS = NH2 // 2

    tab_c = sb("tab_c", [P, TPB, 2, HD2])
    tab_s = sb("tab_s", [P, TPB, 2, HD2])
    pre = keep["pre"]
    wqkv, wo, qks = pre.wqkv[layer], pre.wo[layer], pre.qks[layer]
    base_c, base_s, wmask, identb = pre.base_c, pre.base_s, pre.wmask, pre.identb
    hT = sb("hT", [P, P])
    qk_raw = sb("qk_raw", [P, 2, INNER])
    sqr = sb("sqr", [P, 2 * INNER])
    ssq = sb("ssq", [P, 2 * NH2])
    ssqc = sb("ssqc", [P, 2 * NH2])
    rn = sb("rn", [P, TPB, 2 * NH2])
    neg_half = sb("neg_half", [P, 2 * NH2])
    qk_c = sb("qk_c", [P, 2, INNER])
    qk_s = sb("qk_s", [P, 2, INNER])
    qk_r = sb("qk_r", [P, 2, INNER])
    k_n = sb("k_n", [P, INNER])
    qT = sb("qT", [P, PAIRS, P])
    kT = sb("kT", [P, 2, PAIRS, KEYS])
    v = sb("v", [P, TPB, INNER])
    negraw = sb("negraw", [P, NH2])
    negmax = sb("negmax", [P, NH2])
    den = sb("den", [P, 2, NH2])
    rden = sb("rden", [P, NH2])
    prob = sb("prob", [P, 2, 2, 2 * P])
    probT = sb("probT", [P, 2, 2, 2 * P])
    on = sb("on", [P, INNER])
    oT = sb("oT", [P, INNER])
    x, ident = keep["x"], keep["ident"]

    inited = sem("inited")
    tab_done = sem("tab_done")
    hT_done = sem("hT_done")
    qk_mm = sem("qk_mm")
    v_mm = sem("v_mm")
    v_ev = sem("v_ev")
    raw_done = sem("raw_done")
    sqr_done = sem("sqr_done")
    ssq_sum = sem("ssq_sum")
    ssq_done = sem("ssq_done")
    rn_step = sem("rn_step")
    rope_mul = sem("rope_mul")
    c_mul = sem("c_mul")
    rope_add = sem("rope_add")
    qk_norm = sem("qk_norm")
    qkT_mm = sem("qkT_mm")
    qkT_ev = sem("qkT_ev")
    s_mm = sem("s_mm")
    raw_max = sem("raw_max")
    max_done = sem("max_done")
    exp_done = sem("exp_done")
    pT_mm = sem("pT_mm")
    pT_ev = [sem(f"pT_ev{k}") for k in range(2)]
    o_mm = sem("o_mm")
    recip = sem("recip")
    o_norm = sem("o_norm")
    oT_mm = sem("oT_mm")
    oT_ev = sem("oT_ev")
    y_mm = sem("y_mm")
    y_add = sem("y_add")

    block = ctx.enter_context(nc.Block())

    def tab(tile, t, a, b):
        return tile[:, t, :, a:b][:, :, None, :].broadcast_to([P, 2, NH2, b - a])

    def each_tile(eng, step):
        for t in range(TPB):
            step(t, t)
        with eng.Fori(1, NB) as b:
            for t in range(TPB):
                step(TPB * b + t, t)

    @block.gpsimd
    def _(pool):
        nc.gpsimd.memset(neg_half[:, :], -0.5).then_inc(inited, 1)
        nc.gpsimd.memset(prob[:, :, :, :], 0.0).then_inc(inited, 1)
        nc.gpsimd.memset(keep["xT_pad"], 0.0).then_inc(inited, 1)
        pool.wait_ge(inited, 3)

        h = HD2 // 2
        raw = qk_raw[:, :, :].rearrange("p w (g d) -> p w g d", d=HD2)

        def rope_s(n, t):
            pool.wait_ge(raw_done, n + 1)
            wait_past(pool, rope_add, n)
            for a in (0, h):
                ins = nc.gpsimd.tensor_tensor(
                    qk_s[:, :, :].rearrange("p w (g d) -> p w g d", d=HD2)[:, :, :, a:a + h],
                    raw[:, :, :, h - a:2 * h - a], tab(tab_s, t, a, a + h), ALU.mult)
            ins.then_inc(rope_mul, 1)

        def norms(n, t):
            pool.wait_ge(ssq_done, n + 1)
            nc.gpsimd.tensor_tensor(rn[:, t, NH2:2 * NH2], ssqc[:, NH2:2 * NH2], neg_half[:, 0:NH2], ALU.pow
                                    ).then_inc(rn_step, 1)
            pool.wait_ge(rope_add, n + 1)
            pool.wait_ge(rn_step, 2 * n + 1)
            wait_past(pool, qkT_mm, 2 * n)
            nc.gpsimd.tensor_tensor(k_n[:, :].rearrange("p (h d) -> p h d", d=HD2),
                                    qk_r[:, 1, :].rearrange("p (h d) -> p h d", d=HD2),
                                    rn[:, t, NH2:2 * NH2, None].broadcast_to([P, NH2, HD2]), ALU.mult
                                    ).then_inc(qk_norm, 1)
            nc.gpsimd.tensor_tensor(rn[:, t, 0:NH2], ssqc[:, 0:NH2], neg_half[:, 0:NH2], ALU.pow
                                    ).then_inc(rn_step, 1)
            pool.wait_ge(rn_step, 2 * n + 2)

        pool.wait_ge(tab_done, 3)
        rope_s(0, 0)
        norms(0, 0)

        def step(n, t):
            rope_s(n + 1, (t + 1) % TPB)
            norms(n + 1, (t + 1) % TPB)

        each_tile(pool, step)

    @block.scalar
    def _(act):
        act.wait_ge(inited, 3)

        def copy_qk(n):
            wait_past(act, rope_mul, n)
            wait_past(act, c_mul, n)
            nc.scalar.activation(qk_raw[:, :, :], ps[:, 0:2, :], ACT.Copy).then_inc(raw_done, 1)

        def squares(n):
            act.wait_ge(qk_mm, n + 1)
            wait_past(act, ssq_sum, n)
            nc.scalar.activation(sqr[:, :], ps[:, 0:2, :].rearrange("p a n -> p (a n)"), ACT.Square
                                 ).then_inc(sqr_done, 1)

        def copy_v(n, t):
            act.wait_ge(v_mm, n + 1)
            nc.scalar.activation(v[:, t, :], m_ps, ACT.Copy).then_inc(v_ev, 1)

        def copy_qkT(n, t):
            act.wait_ge(qkT_mm, 2 * n + 1)
            nc.scalar.activation(qT[:, :, :], ps[:, 0, :].rearrange("p (a n) -> p a n", n=P), ACT.Copy
                                 ).then_inc(qkT_ev, 1)
            act.wait_ge(qkT_mm, 2 * n + 2)
            k4 = ps[:, 1, :].rearrange("p (a n) -> p a n", n=P)
            nc.scalar.activation(kT[:, t % 2, :, WIN:KEYS], k4, ACT.Copy).then_inc(qkT_ev, 1)
            nc.scalar.activation(kT[:, (t + 1) % 2, :, 0:WIN], k4[:, :, P - WIN:P], ACT.Copy).then_inc(qkT_ev, 1)

        def exps(n, t, k):
            c = keys(t)
            j = PAIRS * n + k
            act.wait_ge(max_done, j + 1)
            if k == 0:
                wait_past(act, recip, n - 1)
            for i in range(2):
                u = head(k, i)
                ins = nc.scalar.activation(prob[:, k % 2, i, WIN + c.start:2 * P],
                                           ps[:, 2 + k % 2, i * KEYS + c.start:(i + 1) * KEYS], ACT.Exp,
                                           bias=negmax[:, u:u + 1], scale=rn[:, t, u:u + 1], accum_out=den[:, t % 2, u:u + 1])
            ins.then_inc(exp_done, 1)

        def copy_pT(n, t, k):
            act.wait_ge(pT_mm, PAIRS * n + k + 1)
            c = slice(0 if t else P, 2 * P)
            nc.scalar.activation(probT[:, 1, :, c], ps[:, 5, :].rearrange("p (i c) -> p i c", i=2)[:, :, c],
                                 ACT.Copy).then_inc(pT_ev[1], 1)

        def copy_oT(n):
            act.wait_ge(oT_mm, n + 1)
            wait_past(act, y_mm, n)
            nc.scalar.activation(oT[:, :], m_ps, ACT.Copy).then_inc(oT_ev, 1)

        squares(0)
        copy_qk(0)
        copy_v(0, 0)
        copy_qkT(0, 0)
        squares(1)
        copy_qk(1)
        copy_v(1, 1)
        exps(0, 0, 0)
        exps(0, 0, 1)

        def step(n, t):
            copy_pT(n, t, 1)
            exps(n, t, 2)
            if not isinstance(n, int) or n > 0:
                copy_oT(n - 1)
            exps(n, t, 3)
            copy_qkT(n + 1, (t + 1) % TPB)
            copy_pT(n, t, 3)
            exps(n + 1, (t + 1) % TPB, 0)
            squares(n + 2)
            exps(n + 1, (t + 1) % TPB, 1)
            copy_qk(n + 2)
            copy_v(n + 2, (t + 2) % TPB)

        each_tile(act, step)
        copy_oT(NT - 1)

    @block.vector
    def _(dve):
        def shifted(n, t):
            b = n // TPB % NB
            wait_past(dve, v_mm, n)
            full = keep["xT_full"]
            nc.vector.tensor_copy(hT[0:64, :], full[0:64, bass.ds(b, 1), bass.ds(t * P + 1, P)]
                                  .rearrange("p a n -> p (a n)")).then_inc(hT_done, 1)
            nc.vector.tensor_copy(hT[64:P, :], full[64:P, bass.ds(b, 1), bass.ds(t * P, P)]
                                  .rearrange("p a n -> p (a n)")).then_inc(hT_done, 1)

        dve.wait_ge(inited, 3)
        shifted(0, 0)
        h = HD2 // 2
        nc.vector.tensor_tensor(tab_c[:, :, :, :], base_c[:, :, :, :],
                                qks[:, None, :, :].broadcast_to([P, TPB, 2, HD2]), ALU.mult).then_inc(tab_done, 1)
        for a in (0, h):
            nc.vector.tensor_tensor(tab_s[:, :, :, a:a + h], base_s[:, :, :, a:a + h],
                                    qks[:, None, :, h - a:2 * h - a].broadcast_to([P, TPB, 2, h]), ALU.mult
                                    ).then_inc(tab_done, 1)
        dve.wait_ge(tab_done, 3)

        raw = qk_raw[:, :, :].rearrange("p w (g d) -> p w g d", d=HD2)

        def rope_c(n, t):
            dve.wait_ge(raw_done, n + 1)
            nc.vector.tensor_tensor(qk_c[:, :, :].rearrange("p w (g d) -> p w g d", d=HD2), raw,
                                    tab(tab_c, t, 0, HD2), ALU.mult).then_inc(c_mul, 1)

        def rope_sum(n):
            dve.wait_ge(rope_mul, n + 1)
            dve.wait_ge(c_mul, n + 1)
            wait_past(dve, qkT_mm, 2 * n)
            nc.vector.tensor_tensor(qk_r[:, :, :], qk_c[:, :, :], qk_s[:, :, :], ALU.add).then_inc(rope_add, 1)

        def squares(n):
            dve.wait_ge(sqr_done, n + 1)
            nc.vector.tensor_reduce(ssq[:, :], sqr[:, :].rearrange("p (g d) -> p g d", d=HD2), AX.X, ALU.add
                                    ).then_inc(ssq_sum, 1)
            dve.wait_ge(ssq_sum, n + 1)
            wait_past(dve, rn_step, 2 * n)
            nc.vector.tensor_scalar(ssqc[:, :], ssq[:, :], 1e-24, None, ALU.max).then_inc(ssq_done, 1)

        def rowmax(n, t, k):
            dve.wait_ge(s_mm, PAIRS * n + k + 1)
            us = slice(head(k, 0), head(k, 1) + 1, 2)
            nc.vector.tensor_reduce(negraw[:, us],
                                    ps[:, 2 + k % 2, 0:2 * KEYS].rearrange("p (i c) -> p i c", i=2)[:, :, keys(t)],
                                    AX.X, ALU.max, negate=True).then_inc(raw_max, 1)
            dve.wait_ge(raw_max, PAIRS * n + k + 1)
            dve.wait_ge(rn_step, 2 * n + 2)
            nc.vector.tensor_tensor(negmax[:, us], negraw[:, us], rn[:, t, us], ALU.mult).then_inc(max_done, 1)

        def copy_pT(n, t, k):
            dve.wait_ge(pT_mm, PAIRS * n + k + 1)
            c = slice(0 if t else P, 2 * P)
            nc.vector.tensor_copy(probT[:, 0, :, c], ps[:, 4, :].rearrange("p (i c) -> p i c", i=2)[:, :, c]
                                  ).then_inc(pT_ev[0], 1)

        def normalise(n, t):
            dve.wait_ge(exp_done, PAIRS * (n + 1))
            nc.vector.reciprocal(rden[:, :], den[:, t % 2, :]).then_inc(recip, 1)
            dve.wait_ge(recip, n + 1)
            dve.wait_ge(o_mm, n + 1)
            wait_past(dve, oT_mm, n)
            nc.vector.tensor_tensor(on[:, :].rearrange("p (u d) -> p u d", d=HD2),
                                    o_ps.rearrange("p (u d) -> p u d", d=HD2),
                                    rden[:, :, None].broadcast_to([P, NH2, HD2]), ALU.mult).then_inc(o_norm, 1)

        def add_y(n):
            dve.wait_ge(y_mm, n + 1)
            xt = x[:, bass.ds(n, 1), :].rearrange("p a d -> p (a d)")
            nc.vector.tensor_tensor(xt, m_ps[:, 0:D], xt, ALU.add).then_inc(y_add, 1)

        shifted(1, 1)
        squares(0)
        rope_c(0, 0)
        rope_sum(0)
        squares(1)
        shifted(2, 2)
        rowmax(0, 0, 0)
        rowmax(0, 0, 1)
        copy_pT(0, 0, 0)

        def step(n, t):
            rowmax(n, t, 2)
            rope_c(n + 1, (t + 1) % TPB)
            rowmax(n, t, 3)
            rope_sum(n + 1)
            copy_pT(n, t, 2)
            if not isinstance(n, int) or n > 0:
                shifted(n + 2, (t + 2) % TPB)
            if not isinstance(n, int) or n > 0:
                add_y(n - 1)
            rowmax(n + 1, (t + 1) % TPB, 0)
            rowmax(n + 1, (t + 1) % TPB, 1)
            squares(n + 2)
            normalise(n, t)
            copy_pT(n + 1, (t + 1) % TPB, 0)

        each_tile(dve, step)
        add_y(NT - 1)

    @block.tensor
    def _(pe):
        pe.wait_ge(inited, 3)

        def project_qk(n):
            pe.wait_ge(hT_done, 2 * (n + 1))
            wait_past(pe, qkT_ev, 3 * n)
            for w in range(2):
                ins = nc.tensor.matmul(ps[:, w, :], hT[:, :], wqkv[:, w, :], start=True, stop=True)
            ins.then_inc(qk_mm, 1)

        def project_v(n):
            wait_past(pe, y_add, n - 2)
            wait_past(pe, v_ev, n)
            nc.tensor.matmul(m_ps, hT[:, :], wqkv[:, 2, :], start=True, stop=True).then_inc(v_mm, 1)

        def turn_qk(n, w):
            pe.wait_ge(qk_norm if w else rope_add, n + 1)
            src = k_n if w else qk_r[:, 0, :]
            for a in range(4):
                ins = nc.tensor.transpose(ps[:, w, a * P:(a + 1) * P], src[:, a * P:(a + 1) * P], ident[:, :])
            ins.then_inc(qkT_mm, 1)

        def scores(n, t, k):
            if k == 0:
                pe.wait_ge(qkT_ev, 3 * n + 3)
            wait_past(pe, exp_done, PAIRS * n + k - 1)
            c = keys(t)
            nc.tensor.matmul(ps[:, 2 + k % 2, 0:2 * KEYS].rearrange("p (i c) -> p i c", i=2)[:, :, c], identb[:, :],
                             wmask[:, 1 if t else 0, c][:, None, :].broadcast_to([P, 2, KEYS - c.start]),
                             start=True, stop=False, skip_group_check=True)
            for i in range(2):
                r = slice(64 * (k % 2), 64 * (k % 2) + 64)
                ins = nc.tensor.matmul(ps[:, 2 + k % 2, i * KEYS + c.start:(i + 1) * KEYS],
                                       qT[r, head(k, i) // 2, :], kT[r, t % 2, head(k, i) // 2, c],
                                       start=False, stop=(i == 1), skip_group_check=True)
            ins.then_inc(s_mm, 1)

        def turn_p(n, t, k):
            pe.wait_ge(exp_done, PAIRS * n + k + 1)
            wait_past(pe, pT_ev[k % 2], 2 * n + k // 2)
            for i in range(2):
                for a in range(0 if t else 1, 2):
                    ins = nc.tensor.transpose(ps[:, 4 + k % 2, (2 * i + a) * P:(2 * i + a + 1) * P],
                                              prob[:, k % 2, i, a * P:(a + 1) * P], ident[:, :])
            ins.then_inc(pT_mm, 1)

        def values(n, t, k):
            pe.wait_ge(pT_ev[k % 2], 2 * n + k // 2 + 1)
            if k == 0:
                wait_past(pe, o_norm, n)
                pe.wait_ge(v_ev, n + 1)
            for i in range(2):
                c = slice(HD2 * head(k, i), HD2 * (head(k, i) + 1))
                ins = nc.tensor.matmul(o_ps[:, c], probT[:, k % 2, i, P:2 * P], v[:, t, c], start=True,
                                       stop=(t == 0))
                if t:
                    ins = nc.tensor.matmul(o_ps[:, c], probT[64:P, k % 2, i, 0:P], v[64:P, t - 1, c],
                                           start=False, stop=True)
            if k == PAIRS - 1:
                ins.then_inc(o_mm, 1)

        def turn_o(n):
            pe.wait_ge(o_norm, n + 1)
            pe.wait_ge(v_ev, n + 3 if not isinstance(n, int) or n < NT - 1 else NT + 2)
            for a in range(4):
                ins = nc.tensor.transpose(m_ps[:, a * P:(a + 1) * P], on[:, a * P:(a + 1) * P], ident[:, :])
            ins.then_inc(oT_mm, 1)

        def output(n):
            pe.wait_ge(oT_ev, n + 1)
            for a in range(4):
                ins = nc.tensor.matmul(m_ps[:, 0:D], oT[:, a * P:(a + 1) * P], wo[:, a, :],
                                       start=(a == 0), stop=(a == 3))
            ins.then_inc(y_mm, 1)

        project_qk(0)
        project_v(0)
        turn_qk(0, 0)
        turn_qk(0, 1)
        project_qk(1)
        project_v(1)
        scores(0, 0, 0)
        scores(0, 0, 1)
        turn_p(0, 0, 0)

        def step(n, t):
            past = not isinstance(n, int) or n > 0
            scores(n, t, 2)
            turn_p(n, t, 1)
            scores(n, t, 3)
            values(n, t, 0)
            if past:
                turn_o(n - 1)

            turn_p(n, t, 2)
            values(n, t, 1)
            if past:
                output(n - 1)
            turn_qk(n + 1, 0)

            turn_p(n, t, 3)
            turn_qk(n + 1, 1)
            values(n, t, 2)
            scores(n + 1, (t + 1) % TPB, 0)

            project_qk(n + 2)
            scores(n + 1, (t + 1) % TPB, 1)
            turn_p(n + 1, (t + 1) % TPB, 0)
            values(n, t, 3)
            project_v(n + 2)

        each_tile(pe, step)
        turn_o(NT - 1)
        output(NT - 1)


def gated_mlp(nc, ctx, io, keep, layer):

    def sb(name, shape, dt=F32):
        return ctx.enter_context(nc.sbuf_tensor(f"g{layer}_sb_" + name, shape, dt))

    def sem(name):
        return nc.alloc_semaphore(f"g{layer}_" + name)

    ps = keep["ps"]

    pre = keep["pre"]
    w1, w2, b1, lgb = pre.m_w1[layer], pre.m_w2[layer], pre.m_b1[layer], pre.m_lgb[layer]
    hT = sb("hT", [P, S])
    stats = sb("stats", [P, NT, 6])
    mv = sb("mv", [P, NT, 2])
    var = sb("var", [P, NT])
    rstd = sb("rstd", [P, NT])
    eps = sb("eps", [P, TPB])
    neg_half = sb("neg_half", [P, TPB])
    hn = sb("hn", [P, TPB, D])
    hnT = sb("hnT", [P, 2, S])
    gl = sb("gl", [P, 2, S])
    hid = sb("hid", [P, 2, HB, S])
    x, xT, ident = keep["x"], keep["xT"], keep["ident"]

    inited = sem("inited")
    x1_mm = sem("x1_mm")
    x1_ev = sem("x1_ev")
    h_mm = sem("h_mm")
    stats_done = sem("stats_done")
    mv_done = sem("mv_done")
    var_done = sem("var_done")
    rstd_done = sem("rstd_done")
    hn_done = sem("hn_done")
    hn_mm = sem("hn_mm")
    hn_ev = sem("hn_ev")
    g_mm = sem("g_mm")
    a_mm = sem("a_mm")
    gelu_done = sem("gelu_done")
    hid_done = sem("hid_done")
    y_mm = sem("y_mm")
    y_add = sem("y_add")
    x2_mm = sem("x2_mm")
    x2_ev = sem("x2_ev")

    block = ctx.enter_context(nc.Block())

    @block.gpsimd
    def _(pool):
        nc.gpsimd.memset(eps[:, :], EPS).then_inc(inited, 1)
        nc.gpsimd.memset(neg_half[:, :], -0.5).then_inc(inited, 1)
        nc.gpsimd.memset(hT[:, 0:1], 0.0).then_inc(inited, 1)
        nc.gpsimd.memset(hid[:, :, HB - 1, :], 1.0).then_inc(inited, 1)
        pool.wait_ge(inited, 4)
        for b in range(NB):
            t = slice(b * TPB, (b + 1) * TPB)
            pool.wait_ge(mv_done, b + 1)
            nc.gpsimd.tensor_tensor(var[:, t], mv[:, t, 1], eps[:, :], ALU.add).then_inc(var_done, 1)
            pool.wait_ge(var_done, b + 1)
            nc.gpsimd.tensor_tensor(rstd[:, t], var[:, t], neg_half[:, :], ALU.pow).then_inc(rstd_done, 1)

    @block.scalar
    def _(act):
        act.wait_ge(inited, 4)

        def shift(b):
            act.wait_ge(x1_mm, b + 1)
            nc.scalar.activation(hT[0:64, :], ps[0:64, 0, :], ACT.Copy).then_inc(x1_ev, 1)
            nc.scalar.activation(hT[64:P, 1:S], ps[64:P, 0, 0:S - 1], ACT.Copy).then_inc(x1_ev, 1)

        def copy_hn(b):
            act.wait_ge(hn_mm, b + 1)
            nc.scalar.activation(hnT[:, b % 2, :], ps[:, 2, :], ACT.Identity, scale=lgb[:, 0:1], bias=lgb[:, 1:2]
                                 ).then_inc(hn_ev, 1)

        shift(0)
        copy_hn(0)
        for b in range(NB):
            if b + 1 < NB:
                shift(b + 1)
            for k in range(HB):
                r = HROWS[k]
                n = b * HB + k
                act.wait_ge(g_mm, n + 1)
                if n >= 2:
                    act.wait_ge(hid_done, n - 1)
                nc.scalar.activation(gl[0:r, n % 2, :], ps[0:r, 3 + n % 2, :], ACT.Gelu, bias=b1[0:r, 1, k:k + 1]
                                     ).then_inc(gelu_done, 1)
            if b + 1 < NB:
                copy_hn(b + 1)
            act.wait_ge(x2_mm, b + 1)
            nc.scalar.activation(xT[:, b, :], ps[:, 7, :], ACT.Copy).then_inc(x2_ev, 1)

    @block.vector
    def _(dve):
        dve.wait_ge(inited, 4)

        def moments(b):
            dve.wait_ge(h_mm, b + 1)
            for t in range(TPB):
                nc.vector.bn_stats(stats[:, b * TPB + t, :], ps[:, 1, t * P:(t + 1) * P]).then_inc(stats_done, 1)
            dve.wait_ge(stats_done, TPB * (b + 1))
            for t in range(TPB):
                ins = nc.vector.bn_aggr(mv[:, b * TPB + t, :], stats[:, b * TPB + t, :])
            ins.then_inc(mv_done, 1)

        def normalise(b):
            dve.wait_ge(rstd_done, b + 1)
            if b:
                dve.wait_ge(hn_mm, b)
            for t in range(TPB):
                n = b * TPB + t
                ins = nc.vector.tensor_scalar(hn[:, t, :], ps[:, 1, t * P:(t + 1) * P], mv[:, n, 0:1],
                                              rstd[:, n:n + 1], ALU.subtract, ALU.mult)
            ins.then_inc(hn_done, 1)

        moments(0)
        normalise(0)
        for b in range(NB):
            for k in range(HB):
                r = HROWS[k]
                n = b * HB + k
                if b + 1 < NB and k == 1:
                    moments(b + 1)
                if b + 1 < NB and k == 2:
                    normalise(b + 1)
                dve.wait_ge(gelu_done, n + 1)
                dve.wait_ge(a_mm, n + 1)
                if k == 0 and b >= 2:
                    dve.wait_ge(y_mm, b - 1)
                nc.vector.scalar_tensor_tensor(hid[0:r, b % 2, k, :], ps[0:r, 5 + n % 2, :], b1[0:r, 0, k:k + 1],
                                               gl[0:r, n % 2, :], ALU.add, ALU.mult).then_inc(hid_done, 1)
            dve.wait_ge(y_mm, b + 1)
            ts = slice(b * TPB, (b + 1) * TPB)
            nc.vector.tensor_tensor(x[:, ts, :], ps[:, 7, :].rearrange("p (t d) -> p t d", d=D), x[:, ts, :],
                                    ALU.add).then_inc(y_add, 1)

    @block.tensor
    def _(pe):

        def turn(bank, src, done):
            for t in range(TPB):
                ins = nc.tensor.transpose(ps[:, bank, t * P:(t + 1) * P], src(t), ident[:, :])
            ins.then_inc(done, 1)

        def turn_x(b):
            if b:
                pe.wait_ge(x1_ev, 2 * b)
            turn(0, lambda t: x[:, b * TPB + t, :], x1_mm)

        def turn_h(b):
            pe.wait_ge(x1_ev, 2 * (b + 1))
            pe.wait_ge(inited, 3)
            if b:
                pe.wait_ge(hn_done, b)
            turn(1, lambda t: hT[:, t * P:(t + 1) * P], h_mm)

        def turn_hn(b):
            pe.wait_ge(hn_done, b + 1)
            if b:
                pe.wait_ge(hn_ev, b)
            turn(2, lambda t: hn[:, t, :], hn_mm)

        def up(b):
            for k in range(HB):
                if k == 1 and b + 1 < NB:
                    turn_h(b + 1)
                r = HROWS[k]
                n = b * HB + k
                if k == 0:
                    pe.wait_ge(hn_ev, b + 1)
                if n >= 2:
                    pe.wait_ge(gelu_done, n - 1)
                nc.tensor.matmul(ps[0:r, 3 + n % 2, :], w1[:, 1, k * P:k * P + r], hnT[:, b % 2, :],
                                 start=True, stop=True).then_inc(g_mm, 1)
                if n >= 2:
                    pe.wait_ge(hid_done, n - 1)
                nc.tensor.matmul(ps[0:r, 5 + n % 2, :], w1[:, 0, k * P:k * P + r], hnT[:, b % 2, :],
                                 start=True, stop=True).then_inc(a_mm, 1)

        def down(b):
            pe.wait_ge(hid_done, HB * (b + 1))
            if b:
                pe.wait_ge(x2_ev, b)
            for t in range(TPB):
                for k in range(HB):
                    r = HROWS[k] + (k == HB - 1)
                    ins = nc.tensor.matmul(ps[:, 7, t * P:(t + 1) * P], hid[0:r, b % 2, k, t * P:(t + 1) * P],
                                           w2[0:r, k, :], start=(k == 0), stop=(k == HB - 1))
            ins.then_inc(y_mm, 1)

        turn_x(0)
        turn_h(0)
        turn_hn(0)
        for b in range(NB):
            if b + 1 < NB:
                turn_x(b + 1)
            up(b)
            if b + 1 < NB:
                turn_hn(b + 1)
            down(b)
            pe.wait_ge(y_add, b + 1)
            turn(7, lambda t: x[:, b * TPB + t, :], x2_mm)


def save_x(nc, ctx, keep):
    saved = nc.alloc_semaphore("x3_saved")
    block = ctx.enter_context(nc.Block())

    @block.vector
    def _(dve):
        nc.vector.tensor_copy(keep["x3"][:, :, :], keep["x"][:, :, :]).then_inc(saved, 1)


def finish(nc, ctx, keep, out):
    ps = keep["ps"]
    summed = nc.alloc_semaphore("f_summed")
    stored = nc.alloc_semaphore("f_stored")
    norm = Norm(nc, ctx, keep, ps, [0, 1, 2, 3], summed, [1, 2, 3, 4], "fn_")
    block = ctx.enter_context(nc.Block())
    x, x3 = keep["x"], keep["x3"]

    @block.gpsimd
    def _(pool):
        norm.pool(pool)

    @block.vector
    def _(dve):
        for b in range(NB):
            ts = slice(b * TPB, (b + 1) * TPB)
            nc.vector.tensor_tensor(x[:, ts, :], x[:, ts, :], x3[:, ts, :], ALU.add).then_inc(summed, 1)
        norm.vector(dve)

    @block.sync
    def _(sp):
        for b in range(NB):
            ts = slice(b * TPB, (b + 1) * TPB)
            sp.wait_ge(norm.norm_done, b + 1)
            sp.dma_start(out[b].rearrange("(t p) d -> p t d", p=P), x[:, ts, :]).then_inc(stored, 16)
        sp.wait_ge(stored, 16 * NB)


def program(nc, io, out):
    with ExitStack() as ctx:
        def tile(name, shape):
            return ctx.enter_context(nc.sbuf_tensor("keep_" + name, shape, F32))

        def run(phase, *args):
            with nc.cleanup_on_exit(), ExitStack() as inner:
                phase(nc, inner, *args)

        ps = ctx.enter_context(nc.psum_tensor("ps", [P, 8, 512], F32))
        xT_full = tile("xT", [P, NB, S + 1])
        keep = dict(ps=ps, x=tile("x", [P, NT, D]), logits=tile("logits", [P, NT, NE]), ident=tile("ident", [P, P]),
                    xT_full=xT_full, xT=xT_full[:, :, 1:S + 1], xT_pad=xT_full[:, :, 0:1],
                    pre=Preloaded(nc, ctx, io))
        for phase in (attention0, experts0, attention1):
            run(phase, io, keep)
        keep["x3"] = tile("x3", [P, NT, D])
        run(save_x, keep)
        for layer in range(LAYERS):
            run(local_attention, io, keep, layer)
            run(gated_mlp, io, keep, layer)
        run(finish, keep, out)


def rotary(length, width):
    f32 = np.float32
    inv = f32(1.0) / f32(10000.0) ** (np.arange(0, width, 2, dtype=f32) / f32(width))
    angle = np.arange(length, dtype=f32)[:, None] * inv[None, :].astype(f32)
    angle = np.concatenate([angle, angle], 1)
    return np.cos(angle).astype(f32), np.sin(angle).astype(f32)


def shape_constants():
    f32 = np.float32
    bf16 = mybir.dt.np(BF16)
    c = {}
    c["ident"] = np.eye(P, dtype=f32)
    c["identb"] = np.eye(P).astype(bf16)
    c["iota"] = np.tile(np.arange(NE, dtype=f32), (P, 1))
    c["cmask"] = np.where(np.arange(P)[None, :] > np.arange(P)[:, None], -1e30, 0).astype(bf16)
    cos, sin = rotary(S, HD0)
    first = np.where(np.arange(HD0) < HD0 // 2, -1, 1).astype(f32)
    c["cos0"], c["sin0"] = cos, sin * first
    cos, sin = rotary(NB, 8)
    c["c_rot"] = np.repeat(np.concatenate([(cos + sin)[:, :4], (cos - sin)[:, 4:]], 1).T, 16, 0).astype(f32)
    cos, sin = rotary(S, HD2)
    half = np.arange(0, HD2, 2, dtype=f32)
    base = (half + f32(0.4 * HD2)) / f32(1.4 * HD2)
    power = (np.arange(S, dtype=f32) - S // 2) / f32(WIN // 2)
    scale = (base[None, :] ** power[:, None]).astype(f32)
    scale = np.concatenate([scale, scale], 1)
    c["cos1"] = np.stack([8 * cos * scale, cos / scale], 1).reshape(TPB, P, 2, HD2).transpose(1, 0, 2, 3)
    c["sin1"] = np.stack([8 * sin * scale * first, sin / scale * first], 1)\
        .reshape(TPB, P, 2, HD2).transpose(1, 0, 2, 3)
    key, query = np.arange(KEYS)[None, :], np.arange(P)[:, None]
    seen = (key >= query) & (key <= query + WIN)
    c["wmask"] = np.where(np.stack([seen & (key >= WIN), seen], 1), 0, -1e30).astype(bf16)
    return c


def layouts(i):
    a = {}
    x = i["L0_attn_x"]
    a["x"] = x.reshape(NT, P, D).transpose(1, 0, 2)
    a["xT"] = x.reshape(NB * S, D).T
    a["wd"] = i["L0_attn_w_kv_down"]
    a["wdT"] = i["L0_attn_w_kv_down"].T
    a["wkT"] = i["L0_attn_w_k_up"].T
    a["wqT"] = i["L0_attn_wq"].T
    a["wv"] = i["L0_attn_w_v_up"]
    a["woT"] = i["L0_attn_wo"].T
    a["keysT"] = i["L0_ffn_keys"].T
    a["rwT"] = i["L0_ffn_rw"].T
    a["rb"] = i["L0_ffn_rb"].reshape(1, NE)
    a["w1T"] = np.concatenate([i["L0_ffn_w1"].transpose(2, 0, 1),
                               i["L0_ffn_b1"].reshape(NE, FB, P).transpose(2, 0, 1)], 2)
    a["w2T"] = i["L0_ffn_w2"].reshape(NE, D, FB, P).transpose(3, 0, 2, 1).reshape(P, NE * FB, D)
    a["b2"] = i["L0_ffn_b2"]
    order = (np.arange(16)[None, :] * 8 + np.arange(8)[:, None]).reshape(-1)
    a["c_wqT"] = i["L1_attn_Wq"][order].T
    a["c_wkT"] = i["L1_attn_Wk"][order].T
    a["c_wvT"] = i["L1_attn_Wv"].T
    a["wqkv"] = i["L1_ffn_wqkv"].reshape(LAYERS, D, 3, INNER)
    a["l_wo"] = i["L1_ffn_wo"].reshape(LAYERS, INNER // P, P, D).transpose(0, 2, 1, 3)
    a["q_scale"], a["k_scale"] = i["L1_ffn_q_scale"], i["L1_ffn_k_scale"]
    a["l_w1"] = i["L1_ffn_w1"].reshape(LAYERS, D, 2, HID)
    b1 = np.zeros((LAYERS, 2, HB * P), np.float32)
    b1[:, :, :HID] = i["L1_ffn_b1"].reshape(LAYERS, 2, HID)
    a["l_b1"] = b1.reshape(LAYERS, 2, HB, P).transpose(0, 3, 1, 2)
    a["l_gb"] = np.stack([i["L1_ffn_ln_g"], i["L1_ffn_ln_b"]], -1)
    a["l_w2"] = np.concatenate([i["L1_ffn_w2"], i["L1_ffn_b2"][:, None, :]], 1)
    return a


def kernel(**inputs):
    import concourse.bacc as bacc
    from concourse.bass_utils import run_bass_kernel_spmd

    inputs = {name: np.asarray(a) for name, a in inputs.items()}
    arrays = {**shape_constants(), **layouts(inputs)}
    arrays = {name: np.ascontiguousarray(a) for name, a in arrays.items()}
    nc = bacc.Bacc("TRN2", target_bir_lowering=False, num_devices=1)
    io = {name: nc.dram_tensor(name, a.shape, mybir.dt.from_np(a.dtype), kind="ExternalInput").ap()
          for name, a in arrays.items()}
    out = nc.dram_tensor("out", (NB, S, D), F32, kind="ExternalOutput").ap()
    program(nc, io, out)
    result = run_bass_kernel_spmd(nc, [arrays], core_ids=[0])
    return result.results[0]["out"]
```
